# Optimizing a Trainium2 kernel written in Bass

```python
import numpy as np
import jax
import jax.numpy as jnp

def _softmax(x, axis=-1):
    return jax.nn.softmax(x, axis=axis)

def _gelu(x):
    return jax.nn.gelu(x, approximate=True)

def _silu(x):
    return jax.nn.silu(x)

def _sigmoid(x):
    return jax.nn.sigmoid(x)

def _layernorm(x, axis=-1, eps=1e-05):
    m = jnp.mean(x, axis=axis, keepdims=True)
    v = jnp.var(x, axis=axis, keepdims=True)
    return (x - m) / jnp.sqrt(v + eps)

def _scatter_add(tgt, idx, src, axis=0):
    return tgt.at[idx].add(src)

def _segment_sum(src, seg, n):
    return jax.ops.segment_sum(src, seg, n)
kernel_name = 'mk_cond_resid_d4_seqx_r2_a95349'

def setup_inputs(seed: int=0):
    np.random.seed(seed)
    _w = jnp.asarray

    def _rec_inputs():
        import jax
        import jax.numpy as jnp
        _rk = jax.random.key(seed)
        x = 7.22e-05 + 1 * jax.random.normal(jax.random.fold_in(_rk, 1), (2, 2048, 512), jnp.float32)
        _lenS = 2048 - jax.random.randint(jax.random.fold_in(_rk, 7), (2,), 0, max(1, 2048 // 4) + 1, jnp.int32)
        _lenS2 = 2048 - jax.random.randint(jax.random.fold_in(_rk, 8), (2,), 0, max(1, 2048 // 4) + 1, jnp.int32)
        condB_tauraws = -5.74692 + 0.777674 * jax.random.normal(jax.random.fold_in(_rk, 11), (2,), jnp.float32)
        cond_256 = -0.000235209 + 0.019331 * jax.random.normal(jax.random.fold_in(_rk, 12), (2, 128), jnp.float32)
        condB_bn2 = jnp.zeros((2,), jnp.float32)
        cond_1024 = -4.10585e-05 + 0.0199478 * jax.random.normal(jax.random.fold_in(_rk, 14), (2, 512), jnp.float32)
        itok_B_0_30 = jax.random.randint(jax.random.fold_in(_rk, 15), (2,), 0, 31, jnp.int32)
        itok_B_0_8 = jax.random.randint(jax.random.fold_in(_rk, 16), (2,), 0, 9, jnp.int32)
        itok_B_0_7 = jax.random.randint(jax.random.fold_in(_rk, 17), (2,), 0, 8, jnp.int32)
        return (x, condB_tauraws, cond_256, condB_bn2, cond_1024, itok_B_0_30, itok_B_0_8, itok_B_0_7)
    x, condB_tauraws, cond_256, condB_bn2, cond_1024, itok_B_0_30, itok_B_0_8, itok_B_0_7 = _rec_inputs()

    def _L0_cond_setup():
        import jax, jax.numpy as jnp
        import numpy as np
        import math
        B, T, E, D = (4, 1024, 512, 4)

        def _tau_init(t):
            a = 0.1 ** (1.0 / max(t - 1, 1))
            tt = -math.log(max(a, 1e-10))
            return math.log(math.exp(tt) - 1 + 1e-10)

        def causal_ema(b, tau_raw):
            alpha = jnp.exp(-jax.nn.softplus(tau_raw)).astype(b.dtype)

            def step(h, bt):
                h = alpha * h + bt
                return (h, h)
            h0 = jnp.zeros((b.shape[0], b.shape[2]), b.dtype)
            _, hs = jax.lax.scan(step, h0, jnp.swapaxes(b, 0, 1))
            return jnp.swapaxes(hs, 0, 1)
        key = jax.random.key(seed)
        ks = jax.random.split(key, 10)
        s = 0.02
        return {'x': jax.random.normal(ks[0], (B, T, E), jnp.float32), 'tau_ctx': jnp.float32(_tau_init(max(T // 2, 4))), 'tau_raws': jnp.array([_tau_init(max(T // 2 ** i, 2)) for i in range(D)], jnp.float32), 'Wg': jax.random.normal(ks[1], (E, 2 * E), jnp.float32) * s, 'bg': jnp.full((E,), -0.5, jnp.float32), 'Wn1': jax.random.normal(ks[2], (E // 4, E), jnp.float32) * s, 'bn1': jnp.zeros((E // 4,), jnp.float32), 'Wn2': jax.random.normal(ks[3], (D, E // 4), jnp.float32) * s, 'bn2': jnp.zeros((D,), jnp.float32), 'blend': jax.random.normal(ks[4], (D, E), jnp.float32) * s, 'Wsoma': jax.random.normal(ks[5], (E, E), jnp.float32) * s, 'bsoma': jnp.zeros((E,), jnp.float32), 'Wtemp': jax.random.normal(ks[6], (E, E), jnp.float32) * s, 'btemp': jnp.zeros((E,), jnp.float32), 'Wout': jax.random.normal(ks[7], (E, E), jnp.float32) * s, 'gamma': jnp.ones((E,), jnp.float32), 'beta': jnp.zeros((E,), jnp.float32)}
    _L0_cond_all = _L0_cond_setup()
    _L0_cond_in = {k: v for k, v in _L0_cond_all.items() if k in ('tau_ctx', 'Wg', 'bg', 'Wn1', 'bn1', 'Wsoma', 'bsoma', 'Wtemp', 'btemp', 'Wout', 'gamma', 'beta')}
    del _L0_cond_all

    def _L1_cond_setup():
        import jax, jax.numpy as jnp
        import numpy as np
        C, I, O = (32, 512, 512)
        B, T = (64, 256)
        key = jax.random.key(seed)
        kx, kc, kw, kb = jax.random.split(key, 4)
        x = jax.random.normal(kx, (B, T, I), dtype=jnp.float32)
        cat_ids = jax.random.randint(kc, (B,), 0, C)
        W = 0.02 * jax.random.normal(kw, (C, I, O), dtype=jnp.float32)
        b = jnp.zeros((C, O), dtype=jnp.float32)
        return {'x': x, 'cat_ids': cat_ids, 'W': W, 'b': b}
    _L1_cond_all = _L1_cond_setup()
    _L1_cond_in = {k: v for k, v in _L1_cond_all.items() if k in ('W', 'b')}
    del _L1_cond_all

    def _L2_cond_setup():
        import jax, jax.numpy as jnp
        import numpy as np
        LN_EPS = 1e-05
        key = jax.random.key(seed)
        ks = jax.random.split(key, 8)
        B, S, H, A, L = (32, 1024, 512, 128, 10)
        return {'hidden_states': jax.random.normal(ks[0], (B, S, H), dtype=jnp.float32), 'language_ids': jax.random.randint(ks[1], (B,), 0, L, dtype=jnp.int64), 'W1': jax.random.normal(ks[2], (L, H, A), dtype=jnp.float32) * (1.0 / np.sqrt(H)), 'b1': jnp.zeros((L, A), dtype=jnp.float32), 'W2': jax.random.normal(ks[3], (L, A, H), dtype=jnp.float32) * (1.0 / np.sqrt(A)), 'b2': jnp.zeros((L, H), dtype=jnp.float32), 'gamma': jnp.ones((L, H), dtype=jnp.float32), 'beta': jnp.zeros((L, H), dtype=jnp.float32)}
    _L2_cond_all = _L2_cond_setup()
    _L2_cond_in = {k: v for k, v in _L2_cond_all.items() if k in ('W1', 'b1', 'W2', 'b2', 'gamma', 'beta')}
    del _L2_cond_all

    def _L3_cond_setup():
        import jax, jax.numpy as jnp
        import numpy as np
        S, O, H = (8, 512, 512)
        B, N = (32, 256)
        key = jax.random.key(seed)
        k1, k2, k3, k4 = jax.random.split(key, 4)
        x = jax.random.normal(k1, (B, N, H), dtype=jnp.float32)
        subject_id = jax.random.randint(k2, (B,), 0, S)
        wbound = jnp.sqrt(2.0 / 6.0) * jnp.sqrt(3.0 / H)
        weight = jax.random.uniform(k3, (S, O, H), minval=-wbound, maxval=wbound, dtype=jnp.float32)
        bbound = 1.0 / jnp.sqrt(H)
        bias = jax.random.uniform(k4, (S, O), minval=-bbound, maxval=bbound, dtype=jnp.float32)
        return {'x': x, 'subject_id': subject_id, 'weight': weight, 'bias': bias}
    _L3_cond_all = _L3_cond_setup()
    _L3_cond_in = {k: v for k, v in _L3_cond_all.items() if k in ('weight', 'bias')}
    del _L3_cond_all
    return {'x': x, 'condB_tauraws': condB_tauraws, 'cond_256': cond_256, 'condB_bn2': condB_bn2, 'cond_1024': cond_1024, 'itok_B_0_30': itok_B_0_30, 'itok_B_0_8': itok_B_0_8, 'itok_B_0_7': itok_B_0_7, 'L0_cond_tau_ctx': _L0_cond_in['tau_ctx'], 'L0_cond_Wg': _L0_cond_in['Wg'], 'L0_cond_bg': _L0_cond_in['bg'], 'L0_cond_Wn1': _L0_cond_in['Wn1'], 'L0_cond_bn1': _L0_cond_in['bn1'], 'L0_cond_Wsoma': _L0_cond_in['Wsoma'], 'L0_cond_bsoma': _L0_cond_in['bsoma'], 'L0_cond_Wtemp': _L0_cond_in['Wtemp'], 'L0_cond_btemp': _L0_cond_in['btemp'], 'L0_cond_Wout': _L0_cond_in['Wout'], 'L0_cond_gamma': _L0_cond_in['gamma'], 'L0_cond_beta': _L0_cond_in['beta'], 'L1_cond_W': _L1_cond_in['W'], 'L1_cond_b': _L1_cond_in['b'], 'L2_cond_W1': _L2_cond_in['W1'], 'L2_cond_b1': _L2_cond_in['b1'], 'L2_cond_W2': _L2_cond_in['W2'], 'L2_cond_b2': _L2_cond_in['b2'], 'L2_cond_gamma': _L2_cond_in['gamma'], 'L2_cond_beta': _L2_cond_in['beta'], 'L3_cond_weight': _L3_cond_in['weight'], 'L3_cond_bias': _L3_cond_in['bias']}

def reference(x, condB_tauraws, cond_256, condB_bn2, cond_1024, itok_B_0_30, itok_B_0_8, itok_B_0_7, L0_cond_tau_ctx, L0_cond_Wg, L0_cond_bg, L0_cond_Wn1, L0_cond_bn1, L0_cond_Wsoma, L0_cond_bsoma, L0_cond_Wtemp, L0_cond_btemp, L0_cond_Wout, L0_cond_gamma, L0_cond_beta, L1_cond_W, L1_cond_b, L2_cond_W1, L2_cond_b1, L2_cond_W2, L2_cond_b2, L2_cond_gamma, L2_cond_beta, L3_cond_weight, L3_cond_bias):
    import jax
    import jax.numpy as jnp

    def _L0_cond_ref(x, tau_ctx, tau_raws, Wg, bg, Wn1, bn1, Wn2, bn2, blend, Wsoma, bsoma, Wtemp, btemp, Wout, gamma, beta):
        import jax, jax.numpy as jnp
        import numpy as np
        import math
        B, T, E, D = (4, 1024, 512, 4)

        def _tau_init(t):
            a = 0.1 ** (1.0 / max(t - 1, 1))
            tt = -math.log(max(a, 1e-10))
            return math.log(math.exp(tt) - 1 + 1e-10)

        def causal_ema(b, tau_raw):
            alpha = jnp.exp(-jax.nn.softplus(tau_raw)).astype(b.dtype)

            def step(h, bt):
                h = alpha * h + bt
                return (h, h)
            h0 = jnp.zeros((b.shape[0], b.shape[2]), b.dtype)
            _, hs = jax.lax.scan(step, h0, jnp.swapaxes(b, 0, 1))
            return jnp.swapaxes(hs, 0, 1)
        ctx = causal_ema(x, tau_ctx)
        gate_in = jnp.concatenate([x, ctx], axis=-1)
        wg = jax.nn.sigmoid(jnp.einsum('btc,ec->bte', gate_in, Wg) + bg)
        gated = x * wg
        h1 = jax.nn.gelu(jnp.einsum('btc,hc->bth', x, Wn1) + bn1, approximate=False)
        mod = 0.5 + jax.nn.sigmoid(jnp.einsum('bth,dh->btd', h1, Wn2) + bn2)
        traces = jax.vmap(lambda tau, m: causal_ema(gated * m[..., None], tau))(tau_raws, jnp.moveaxis(mod, -1, 0))
        blend_w = jax.nn.softmax(blend, axis=0)
        temporal = jnp.einsum('dbtc,dc->btc', traces, blend_w)
        gate = jax.nn.sigmoid(jnp.einsum('btc,ec->bte', temporal, Wtemp) + btemp)
        soma = jax.nn.gelu(jnp.einsum('btc,ec->bte', x, Wsoma) + bsoma, approximate=False)
        out = jnp.einsum('btc,ec->bte', soma * gate, Wout)
        mu = out.mean(-1, keepdims=True)
        var = out.var(-1, keepdims=True)
        return (out - mu) / jnp.sqrt(var + 1e-05) * gamma + beta

    def _L1_cond_ref(x, cat_ids, W, b):
        import jax, jax.numpy as jnp
        import numpy as np
        C, I, O = (32, 512, 512)
        B, T = (64, 256)
        selected_W = W[cat_ids]
        selected_b = b[cat_ids]
        if x.ndim == 2:
            return jnp.einsum('bi,bio->bo', x, selected_W) + selected_b
        return jnp.einsum('bti,bio->bto', x, selected_W) + selected_b[:, None, :]

    def _L2_cond_ref(hidden_states, language_ids, W1, b1, W2, b2, gamma, beta):
        import jax, jax.numpy as jnp
        import numpy as np
        LN_EPS = 1e-05
        w1 = W1[language_ids]
        w2 = W2[language_ids]
        h = jnp.einsum('bsh,bha->bsa', hidden_states, w1) + b1[language_ids][:, None, :]
        h = jax.nn.relu(h)
        adapted = jnp.einsum('bsa,bah->bsh', h, w2) + b2[language_ids][:, None, :]
        x = hidden_states + adapted
        mean = jnp.mean(x, axis=-1, keepdims=True)
        var = jnp.mean(jnp.square(x - mean), axis=-1, keepdims=True)
        normed = (x - mean) * jax.lax.rsqrt(var + LN_EPS)
        return normed * gamma[language_ids][:, None, :] + beta[language_ids][:, None, :]

    def _L3_cond_ref(x, subject_id, weight, bias):
        import jax, jax.numpy as jnp
        import numpy as np
        S, O, H = (8, 512, 512)
        B, N = (32, 256)
        W = weight[subject_id]
        b = bias[subject_id]
        y = jnp.einsum('bnh,boh->bno', x, W) + b[:, None, :]
        return y
    x = x + _L0_cond_ref(x, L0_cond_tau_ctx, condB_tauraws, L0_cond_Wg, L0_cond_bg, L0_cond_Wn1, L0_cond_bn1, cond_256, condB_bn2, cond_1024, L0_cond_Wsoma, L0_cond_bsoma, L0_cond_Wtemp, L0_cond_btemp, L0_cond_Wout, L0_cond_gamma, L0_cond_beta)
    x = x + _L1_cond_ref(x, itok_B_0_30, L1_cond_W, L1_cond_b)
    x = x + _L2_cond_ref(x, itok_B_0_8, L2_cond_W1, L2_cond_b1, L2_cond_W2, L2_cond_b2, L2_cond_gamma, L2_cond_beta)
    x = x + _L3_cond_ref(x, itok_B_0_7, L3_cond_weight, L3_cond_bias)
    return x

_drawn_inputs = setup_inputs


def setup_inputs(seed=0):
    import zlib

    import numpy as np

    out = dict(_drawn_inputs(seed))
    spreads = {'condB_bn2': (0.0, 2.0),
     'L0_cond_bg': (-0.5, 0.6),
     'L0_cond_bn1': (0.0, 0.8),
     'L0_cond_bsoma': (0.0, 0.1),
     'L0_cond_btemp': (0.0, 0.487),
     'L0_cond_gamma': (1.0, 0.2),
     'L0_cond_beta': (0.0, 0.1),
     'L1_cond_b': (0.0, 0.1),
     'L2_cond_b1': (0.0, 0.521),
     'L2_cond_b2': (0.0, 0.371),
     'L2_cond_gamma': (1.0, 0.2),
     'L2_cond_beta': (0.0, 0.1)}
    factors = {'condB_tauraws': 8.0,
     'cond_256': 8.0,
     'cond_1024': 25.058,
     'L0_cond_Wn1': 8.0,
     'L3_cond_bias': 6.316}
    for name, (base, spread) in spreads.items():
        noise = np.random.default_rng([zlib.crc32(name.encode()), seed]).standard_normal(out[name].shape)
        drawn = base * np.exp(spread * noise) if base else spread * noise
        out[name] = jnp.asarray(drawn.astype(out[name].dtype))
    for name, factor in factors.items():
        out[name] = (out[name] * factor).astype(out[name].dtype)
    return out
```

```python
from contextlib import ExitStack

import concourse.bass as bass
from concourse import mybir

P = 128
BLK = 512
ALU = mybir.AluOpType
ACT = mybir.ActivationFunctionType
F32 = mybir.dt.float32
F32R = mybir.dt.float32r
I32 = mybir.dt.int32
EPS = 1e-5


def after(engine, semaphore, count):
    if not isinstance(count, int) or count > 0:
        engine.wait_ge(semaphore, count)


def residual_chain_kernel(nc: bass.Bass, t: dict, out: bass.AP):
    B, SEQ, E = t["x"].shape
    NC = E // P
    NBLK = B * SEQ // BLK
    PER_SEQ = SEQ // BLK
    TILES = BLK // P
    D = t["condB_tauraws"].shape[0]
    H = t["L0_cond_Wn1"].shape[0]
    A = t["L2_cond_W1"].shape[2]
    assert NC == 4 and TILES == 4 and D == 2 and B == 2 and H == P and A == P and NBLK == 8

    x_tiles = t["x"].rearrange("b (n p) e -> (b n) p e", p=P)
    out_tiles = out.rearrange("b (n p) e -> (b n) p e", p=P)
    x1_tiles = nc.dram_tensor("x1_scratch", (NBLK * TILES, P, E), F32, kind="Internal").ap()

    with ExitStack() as ctx:
        def sb(name, shape, dt=F32):
            return ctx.enter_context(nc.sbuf_tensor(name, shape, dt))

        def sem(name):
            return ctx.enter_context(nc.semaphore(name))

        wg_h, wg_l = sb("wg_h", [P, 2 * NC, E], F32R), sb("wg_l", [P, 2 * NC, E], F32R)
        ws_h, ws_l = sb("ws_h", [P, NC, E], F32R), sb("ws_l", [P, NC, E], F32R)
        wt_h, wt_l = sb("wt_h", [P, NC, E], F32R), sb("wt_l", [P, NC, E], F32R)
        wo_h, wo_l = sb("wo_h", [P, NC, E], F32R), sb("wo_l", [P, NC, E], F32R)
        wn1_h, wn1_l = sb("wn1_h", [P, NC, H], F32R), sb("wn1_l", [P, NC, H], F32R)
        wn2_h, wn2_l = sb("wn2_h", [P, D, P], F32R), sb("wn2_l", [P, D, P], F32R)
        x_tok = sb("x_tok", [P, 2, E])
        x_h, x_l = sb("x_h", [P, NC, BLK], F32R), sb("x_l", [P, NC, BLK], F32R)
        x_t = sb("x_t", [P, NC, BLK])
        ctx_t = sb("ctx_t", [P, 2, BLK])
        c_h, c_l = sb("c_h", [P, NC, BLK], F32R), sb("c_l", [P, NC, BLK], F32R)
        h1 = sb("h1", [P, BLK])
        h_h, h_l = sb("h_h", [P, BLK], F32R), sb("h_l", [P, BLK], F32R)
        mod = sb("mod", [P, D, BLK])
        soma = sb("soma", [P, NC, BLK])
        gate = sb("gate", [P, 2, BLK])
        t_h, t_l = sb("t_h", [P, NC, BLK], F32R), sb("t_l", [P, NC, BLK], F32R)
        s_h, s_l = sb("s_h", [P, NC, BLK], F32R), sb("s_l", [P, NC, BLK], F32R)
        stage_a = sb("stage_a", [P, 4, E])
        stage_b = sb("stage_b", [P, 4, E])
        x_again, normed = stage_a[:, 0:2, :], stage_a[:, 2:4, :]
        tr1, tr0 = stage_b[:, 0:2, :], stage_b[:, 2:4, :]
        gamma_row = sb("gamma_row", [P, E])
        ident = sb("ident", [P, P])
        names = ["bg", "bsoma", "btemp", "beta0"]
        cols = {n: sb("col_" + n, [P, NC]) for n in names}
        col_bn1 = sb("col_bn1", [P, 1])
        col_bn2 = sb("col_bn2", [P, D])
        col_wn2 = sb("col_wn2", [P, D])
        blend = sb("blend", [P, D, NC])
        dblend = sb("dblend", [P, D, NC])
        w_blend = sb("w_blend", [P, D, NC])
        taus = sb("taus", [P, 1 + D])
        alpha = sb("alpha", [P, 1 + D])
        carry = sb("carry", [P, 1 + D, NC])
        keep = sb("keep", [P, NBLK + 1])
        stats = sb("stats", [P, TILES, 6])
        mv = sb("mv", [P, TILES, 2])
        rstd = sb("rstd", [P, TILES])
        nbias = sb("nbias", [P, TILES])
        newton = sb("newton", [P, 3, TILES])
        const = sb("const", [P, 4, TILES])
        l2names = ["b1", "lb1", "b2", "gamma2", "beta2", "b1b2", "beta_b2"]
        seq = {n: sb("seq_" + n, [P, B, NC]) for n in l2names}
        idx = sb("idx", [1, 8], I32)

        pt = [ctx.enter_context(nc.psum_tensor(f"pt{i}", [P, 512], F32)) for i in range(2)]
        pc = [ctx.enter_context(nc.psum_tensor(f"pc{i}", [P, 512], F32)) for i in range(2)]
        pm = [ctx.enter_context(nc.psum_tensor(f"pm{i}", [P, 512], F32)) for i in range(4)]

        x_in = [sem(f"x_in{s}") for s in range(2)]
        again_in = [sem(f"again_in{s}") for s in range(2)]
        x1_out = [sem(f"x1_out{s}") for s in range(2)]
        small_in = sem("small_in")
        weight_in = [sem(f"weight_in{n}") for n in range(6)]
        idx_in = sem("idx_in")
        l1_in, l3_in, lw_in = ([sem(f"{n}{b}") for b in range(B)] for n in ("l1_in", "l3_in", "lw_in"))
        setup_done = sem("setup_done")
        consts_v = sem("consts_v")
        consts_a = sem("consts_a")
        w_turned = sem("w_turned")
        w_hi = sem("w_hi")
        w_lo = sem("w_lo")
        tx_done, h1_mm, soma_mm, mod_mm, z_mm, wt_mm, wo_mm = (
            sem(n) for n in ("tx_done", "h1_mm", "soma_mm", "mod_mm", "z_mm", "wt_mm", "wo_mm"))
        xcopy, ctx_hi, h1_gelu, h1_hi, soma_g, mod_t, z_t, weighed, temp_hi, gate_t, s_hi = (
            sem(n) for n in ("xcopy", "ctx_hi", "h1_gelu", "h1_hi", "soma_g", "mod_t", "z_t",
                             "weighed", "temp_hi", "gate_t", "s_hi"))
        xlo, ctx_scan, ctx_carry, ctx_lo, h1_lo, s_prod, s_lo, gated, prods, traces, tr_carry = (
            sem(n) for n in ("xlo", "ctx_scan", "ctx_carry", "ctx_lo", "h1_lo", "s_prod", "s_lo",
                             "gated", "prods", "traces", "tr_carry"))
        blended, temp_lo, ln_stats, ln_mv, ln_centred, x1_ready = (
            sem(n) for n in ("blended", "temp_lo", "ln_stats", "ln_mv", "ln_centred", "x1_ready"))
        pool_step, ln_rstd = sem("pool_step"), sem("ln_rstd")
        y_in = [sem(f"y_in{s}") for s in range(2)]
        out_done = [sem(f"out_done{s}") for s in range(2)]
        (ty_done, l1_mm, tn_done, w1_mm, xx_mm, l3_mm) = (
            sem(n) for n in ("ty_done", "l1_mm", "tn_done", "w1_mm", "xx_mm", "l3_mm"))
        (y_hi, x2_hi, x2_all, relu_done, hid_hi, n2_done, x3_hi) = (
            sem(n) for n in ("y_hi", "x2_hi", "x2_all", "relu_done", "hid_hi", "n2_done", "x3_hi"))
        (y_lo, x2_lo, hid_lo, ln2_stats, ln2_mv, x3_sum, x3_lo, out_ready) = (
            sem(n) for n in ("y_lo", "x2_lo", "hid_lo", "ln2_stats", "ln2_mv", "x3_sum", "x3_lo",
                             "out_ready"))
        ln2_rstd = sem("ln2_rstd")
        setup_v, stats_seen = sem("setup_v"), sem("stats_seen")
        v_hi, v_lo, v_eye, v_turned, bias_mm, bias_done = (
            sem(n) for n in ("v_hi", "v_lo", "v_eye", "v_turned", "bias_mm", "bias_done"))

        def l1_w(b):
            return wg_h[:, b * NC:(b + 1) * NC, :], wg_l[:, b * NC:(b + 1) * NC, :]

        def w1_w(b):
            if b == 0:
                return wn1_h[:, :, :], wn1_l[:, :, :]
            return tuple(w[:, 0, :].rearrange("p (k a) -> p k a", k=NC) for w in (wo_h, wo_l))

        def w2_w(b):
            return wo_h[:, 1 + b, :], wo_l[:, 1 + b, :]

        def l3_w(b):
            return (ws_h[:, :, :], ws_l[:, :, :]) if b == 0 else (wt_h[:, :, :], wt_l[:, :, :])

        V_L2, V_L3, V_ALL = NC, NC + 2, 2 * NC + 2

        block = ctx.enter_context(nc.Block())

        def tile_of(tiles, i, j):
            return tiles[bass.ds(i * TILES + j, 1)].rearrange("a p e -> (a p) e")

        wn1_raw, whole_a, whole_b = gate[:, 0:1, :], stage_a, stage_b
        L0W = [
            ("wn1", t["L0_cond_Wn1"].rearrange("(n p) c -> p n c", p=P), wn1_raw),
            ("wsoma", t["L0_cond_Wsoma"].rearrange("(n p) c -> p n c", p=P), whole_a),
            ("wg_x", t["L0_cond_Wg"][:, 0:E].rearrange("(n p) c -> p n c", p=P), whole_b),
            ("wg_ctx", t["L0_cond_Wg"][:, E:2 * E].rearrange("(n p) c -> p n c", p=P), whole_a),
            ("wtemp", t["L0_cond_Wtemp"].rearrange("(n p) c -> p n c", p=P), whole_a),
            ("wout", t["L0_cond_Wout"].rearrange("(n p) c -> p n c", p=P), whole_a),
        ]
        W_COUNT = [1, 4, 4, 4, 4, 4]
        W_SCALE = [1.0, 1.0, 1.0, 1.0, 1.0, 0.5]
        W_BEFORE = [sum(W_COUNT[:n]) for n in range(6)]

        def w_dest(n, k):
            if n == 0:
                return (w[:, :, :].rearrange("p a b -> p (a b)") for w in (wn1_h, wn1_l))
            h, lo, at = [None, (ws_h, ws_l, 0), (wg_h, wg_l, 0), (wg_h, wg_l, NC), (wt_h, wt_l, 0),
                         (wo_h, wo_l, 0)][n]
            return h[:, at + k, :], lo[:, at + k, :]

        @block.sync
        def _(sp):
            def load_weight(n):
                _, src, raw = L0W[n]
                if n == 3:
                    sp.wait_ge(w_turned, W_BEFORE[2])
                if n in (4, 5):
                    sp.wait_ge(w_turned, W_BEFORE[n])
                sp.dma_start(raw[:, :, :], src).then_inc(weight_in[n], 16)

            def load_x(i, j):
                after(sp, tx_done, i * TILES + (j - 1))
                sp.dma_start(x_tok[:, j % 2, :], tile_of(x_tiles, i, j)).then_inc(x_in[j % 2], 16)

            def load_again(j, k):
                after(sp, x1_out[k % 2], (j * 2 + k // 2) * 16)
                sp.dma_start(x_again[:, k % 2, :], tile_of(x_tiles, j, k)).then_inc(again_in[k % 2], 16)

            def store_x1(j, k):
                sp.wait_ge(x1_ready, j * TILES + k + 1)
                sp.dma_start(tile_of(x1_tiles, j, k), x_again[:, k % 2, :]).then_inc(x1_out[k % 2], 16)

            load_x(0, 0)
            load_x(0, 1)
            load_weight(0)
            load_weight(1)
            load_x(0, 2)
            load_x(0, 3)
            load_weight(2)
            load_weight(3)

            def step(i, prev, nxt):
                if nxt:
                    load_x(i + 1, 0)
                    load_x(i + 1, 1)
                if prev:
                    j = i - 1
                    load_again(j, 0)
                    load_again(j, 1)
                if nxt:
                    load_x(i + 1, 2)
                    load_x(i + 1, 3)
                if prev:
                    store_x1(j, 0)
                    store_x1(j, 1)
                    load_again(j, 2)
                    load_again(j, 3)
                    store_x1(j, 2)
                    store_x1(j, 3)

            load_x(1, 0)
            load_x(1, 1)
            load_weight(4)
            load_x(1, 2)
            load_x(1, 3)
            load_weight(5)
            sp.wait_ge(w_turned, W_BEFORE[5] + W_COUNT[5])
            step(1, True, True)
            with sp.Fori(2, NBLK - 1) as i:
                step(i, True, True)
            step(NBLK - 1, True, False)

            sp.wait_ge(idx_in, 48)
            which = [sp.value_load(idx[0:1, n:n + 1], min_val=0, max_val=m)
                     for n, m in enumerate([31, 31, 9, 9, 7, 7])]

            def cat(b):
                return which[b]

            def lang(b):
                return which[2 + b]

            def subj(b):
                return which[4 + b]

            def cols_of(src, n):
                return src[bass.ds(n, 1), :].rearrange("a (k p) -> p (a k)", p=P)

            with nc.allow_non_contiguous_dma(reason="bias columns, a few hundred words"):
                for b in range(B):
                    sp.dma_start(seq["b1"][:, b, :], cols_of(t["L1_cond_b"], cat(b))).then_inc(lw_in[b], 16)
                    sp.dma_start(seq["lb1"][:, b, 0:1], cols_of(t["L2_cond_b1"], lang(b))).then_inc(lw_in[b], 16)
                    for n, src in (("b2", "L2_cond_b2"), ("gamma2", "L2_cond_gamma"), ("beta2", "L2_cond_beta")):
                        sp.dma_start(seq[n][:, b, :], cols_of(t[src], lang(b))).then_inc(lw_in[b], 16)

            def load_l1(b):
                if b == 0:
                    sp.wait_ge(temp_lo, NBLK * NC)
                else:
                    sp.wait_ge(v_turned, NC)
                sp.dma_start(stage_b[:, :, :], t["L1_cond_W"][bass.ds(cat(b), 1)].rearrange(
                    "a (k p) o -> p (a k) o", p=P)).then_inc(l1_in[b], 16)

            def load_l2(b):
                sp.wait_ge(v_hi, V_ALL * b + V_L2)
                sp.wait_ge(v_lo, V_ALL * b + V_L2)
                sp.wait_ge(bias_mm, b + 1)
                sp.dma_start(stage_b[:, 0, :].rearrange("p (k a) -> p k a", k=NC),
                             t["L2_cond_W1"][bass.ds(lang(b), 1)].rearrange(
                                 "a (k p) h -> p (a k) h", p=P)).then_inc(l1_in[b], 16)
                sp.dma_start(stage_b[:, 1, :], t["L2_cond_W2"][bass.ds(lang(b), 1)].rearrange(
                    "a p o -> (a p) o")).then_inc(l1_in[b], 16)

            def load_l3(b):
                sp.wait_ge(v_hi, V_ALL * b + V_L3)
                sp.wait_ge(v_lo, V_ALL * b + V_L3)
                sp.dma_start(stage_b[:, :, :], t["L3_cond_weight"][bass.ds(subj(b), 1)].rearrange(
                    "a (k p) c -> p (a k) c", p=P)).then_inc(l3_in[b], 16)

            def load_b3(b):
                sp.wait_ge(prods, NBLK * NC * D)
                sp.dma_start(mod[:, b, :], t["L3_cond_bias"][bass.ds(subj(b), 1), :].rearrange(
                    "a c -> (a c)").partition_broadcast(P)).then_inc(lw_in[b], 16)

            def load_y(i, j):
                after(sp, ty_done, i * TILES + (j - 1))
                sp.dma_start(x_tok[:, j % 2, :], tile_of(x1_tiles, i, j)).then_inc(y_in[j % 2], 16)

            def store_out(j, k):
                sp.wait_ge(out_ready, j * TILES + k + 1)
                sp.dma_start(tile_of(out_tiles, j, k), ctx_t[:, k % 2, :]).then_inc(out_done[k % 2], 16)

            load_b3(0)
            load_b3(1)
            load_l1(0)
            step(NBLK, True, False)
            load_l2(0)
            load_l3(0)
            for s in range(2):
                sp.wait_ge(x1_out[s], 16 * 2 * NBLK)
            for k in range(TILES):
                load_y(0, k)

            def step2(i, prev, nxt):
                if nxt:
                    load_y(i + 1, 0)
                    load_y(i + 1, 1)
                    load_y(i + 1, 2)
                if prev:
                    store_out(i - 1, 0)
                if nxt:
                    load_y(i + 1, 3)
                if prev:
                    store_out(i - 1, 1)
                    store_out(i - 1, 2)
                    store_out(i - 1, 3)

            step2(0, False, True)
            load_l1(1)
            step2(1, True, True)
            with sp.Fori(2, PER_SEQ) as i:
                step2(i, True, True)
            load_l2(1)
            load_l3(1)
            step2(PER_SEQ, True, True)
            with sp.Fori(PER_SEQ + 1, NBLK - 1) as i:
                step2(i, True, True)
            step2(NBLK - 1, True, False)
            step2(NBLK, True, False)
            for s in range(2):
                sp.wait_ge(out_done[s], 16 * 2 * NBLK)

        @block.gpsimd
        def _(pool):
            def row(src, n):
                return src.rearrange("(a k) -> a k", a=1)

            with nc.allow_non_contiguous_dma(reason="bias columns, a few hundred words"):
                for n, src in (("bg", "L0_cond_bg"), ("bsoma", "L0_cond_bsoma"),
                               ("btemp", "L0_cond_btemp"), ("beta0", "L0_cond_beta")):
                    pool.dma_start(cols[n][:, :], t[src].rearrange("(k p) -> p k", p=P)).then_inc(small_in, 16)
                pool.dma_start(col_bn1[:, :], t["L0_cond_bn1"].rearrange("(p k) -> p k", k=1)).then_inc(small_in, 16)
                pool.dma_start(col_wn2[:, :], t["cond_256"].rearrange("d p -> p d")).then_inc(small_in, 16)
                for d in range(D):
                    pool.dma_start(blend[:, d, :], t["cond_1024"][d, :].rearrange("(k p) -> p k", p=P)).then_inc(small_in, 16)
                pool.dma_start(col_bn2[:, :], t["condB_bn2"].partition_broadcast(P)).then_inc(small_in, 16)
                pool.dma_start(taus[:, 0:1], t["L0_cond_tau_ctx"].partition_broadcast(P)).then_inc(small_in, 16)
                pool.dma_start(taus[:, 1:1 + D], t["condB_tauraws"].partition_broadcast(P)).then_inc(small_in, 16)
                pool.dma_start(gamma_row[:, :], t["L0_cond_gamma"].partition_broadcast(P)).then_inc(small_in, 16)
            for n, src in enumerate(("itok_B_0_30", "itok_B_0_8", "itok_B_0_7")):
                pool.dma_start(idx[0:1, 2 * n:2 * n + 2], t[src].rearrange("(a k) -> a k", a=1)).then_inc(idx_in, 16)
            nc.gpsimd.memset(ident[:, :], 0.0).then_inc(pool_step, 1)
            pool.wait_ge(pool_step, 1)
            nc.gpsimd.affine_select(out=ident[:, :], in_=ident[:, :], compare_op=ALU.not_equal, fill=1.0,
                                    base=0, pattern=[[-1, P]], channel_multiplier=1).then_inc(setup_done, 1)
            eps, minus_half, minus_three, half = (const[:, q, :] for q in range(4))
            for c, value in ((eps, EPS), (minus_half, -0.5), (minus_three, -3.0), (half, 0.5)):
                nc.gpsimd.memset(c, value).then_inc(pool_step, 1)
            pool.wait_ge(pool_step, 5)

            def inv_sqrt(tiles, at):
                n = tiles.stop - tiles.start
                v, y, q = newton[:, 0, 0:n], newton[:, 1, 0:n], newton[:, 2, 0:n]
                nc.gpsimd.tensor_tensor(v, mv[:, tiles, 1], eps[:, 0:n], ALU.add).then_inc(pool_step, 1)
                pool.wait_ge(pool_step, at + 1)
                nc.gpsimd.tensor_tensor(y, v, minus_half[:, 0:n], ALU.pow).then_inc(pool_step, 1)
                pool.wait_ge(pool_step, at + 2)
                nc.gpsimd.tensor_tensor(q, y, y, ALU.mult).then_inc(pool_step, 1)
                pool.wait_ge(pool_step, at + 3)
                nc.gpsimd.tensor_tensor(q, q, v, ALU.mult).then_inc(pool_step, 1)
                pool.wait_ge(pool_step, at + 4)
                nc.gpsimd.tensor_tensor(q, q, minus_three[:, 0:n], ALU.add).then_inc(pool_step, 1)
                pool.wait_ge(pool_step, at + 5)
                nc.gpsimd.tensor_tensor(q, q, y, ALU.mult).then_inc(pool_step, 1)
                pool.wait_ge(pool_step, at + 6)
                return q

            def x_lo_part(i, k):
                tok = slice(k * P, (k + 1) * P)
                pool.wait_ge(xcopy, i * TILES + (k + 1))
                if k == 0:
                    pool.wait_ge(z_mm, i * NC)
                nc.gpsimd.tensor_tensor(x_l[:, :, tok], x_t[:, :, tok], x_h[:, :, tok].bitcast(F32),
                                        ALU.subtract).then_inc(xlo, 1)

            def norm_scale(j, k):
                pool.wait_ge(ln_mv, j * TILES + (k + 1))
                corr = inv_sqrt(slice(k, k + 1), j * (TILES * 6) + (5 + k * 6))
                nc.gpsimd.tensor_tensor(rstd[:, k:k + 1], corr, minus_half[:, 0:1], ALU.mult).then_inc(ln_rstd, 1)
                pool.wait_ge(ln_rstd, j * TILES + (k + 1))

            for k in range(TILES):
                x_lo_part(1, k)
            with pool.Fori(1, NBLK - 1) as i:
                norm_scale(i - 1, 0)
                x_lo_part(i + 1, 0)
                norm_scale(i - 1, 1)
                x_lo_part(i + 1, 1)
                norm_scale(i - 1, 2)
                norm_scale(i - 1, 3)
                x_lo_part(i + 1, 2)
                x_lo_part(i + 1, 3)
            for j in (NBLK - 2, NBLK - 1):
                for k in range(TILES):
                    norm_scale(j, k)
            second = 5 + NBLK * TILES * 6
            with pool.Fori(0, NBLK) as j:
                at = j * 8 + second
                pool.wait_ge(ln2_mv, j * TILES + TILES)
                corr = inv_sqrt(slice(0, TILES), at)
                nc.gpsimd.tensor_tensor(rstd[:, :], corr, minus_half, ALU.mult).then_inc(pool_step, 1)
                nc.gpsimd.tensor_tensor(nbias[:, :], corr, mv[:, :, 0], ALU.mult).then_inc(pool_step, 1)
                pool.wait_ge(pool_step, at + 8)
                nc.gpsimd.tensor_tensor(nbias[:, :], nbias[:, :], half, ALU.mult).then_inc(ln2_rstd, 1)
                pool.wait_ge(ln2_rstd, j + 1)

        @block.tensor
        def _(pe):
            def product(acc, pairs, start=True, stop=True):
                n = len(pairs)
                for q, (ah, al, bh, bl) in enumerate(pairs):
                    nc.tensor.matmul(acc, ah, bh, start=start and q == 0, stop=False)
                    nc.tensor.matmul(acc, ah, bl, start=False, stop=False)
                    last = nc.tensor.matmul(acc, al, bh, start=False, stop=stop and q == n - 1)
                return last

            def turn(acc, sources, stop=True):
                for q, src in enumerate(sources):
                    last = nc.tensor.matmul(acc[:, q * P:(q + 1) * P], src, ident[:, :], is_transpose=True,
                                            start=(q == 0), stop=stop and (q == 3), skip_group_check=True)
                return last

            def out_cols(m):
                return slice(m * P, (m + 1) * P)

            def prepare(n):
                pe.wait_ge(weight_in[n], 16)
                raw = L0W[n][2]
                for k in range(W_COUNT[n]):
                    c = W_BEFORE[n] + k
                    if c >= 4:
                        pe.wait_ge(w_hi, c - 3)
                        pe.wait_ge(w_lo, c - 3)
                    pieces = ([raw[:, 0, out_cols(q)] for q in range(4)] if n == 0 else
                              [raw[:, q, out_cols(k)] for q in range(4)])
                    turn(pm[c % 4], pieces).then_inc(w_turned, 1)

            def ready(n):
                pe.wait_ge(w_hi, W_BEFORE[n] + W_COUNT[n])
                pe.wait_ge(w_lo, W_BEFORE[n] + W_COUNT[n])

            def turn_x(i, k):
                pe.wait_ge(x_in[k % 2], (i * 2 + (k // 2 + 1)) * 16)
                if k == 0:
                    after(pe, h1_gelu, i)
                if k >= 2:
                    pe.wait_ge(xcopy, i * TILES + (k - 1))
                turn(pt[k % 2], [x_tok[:, k % 2, out_cols(c)] for c in range(NC)]).then_inc(tx_done, 1)

            def h1_product(i):
                pe.wait_ge(xcopy, i * TILES + TILES)
                pe.wait_ge(xlo, i * TILES + TILES)
                product(pt[0][:, :], [(wn1_h[:, c, :], wn1_l[:, c, :], x_h[:, c, :], x_l[:, c, :])
                                      for c in range(NC)]).then_inc(h1_mm, 1)

            def soma_product(i):
                for m in range(NC):
                    if m >= 2:
                        pe.wait_ge(soma_g, i * NC + (m - 1))
                    else:
                        after(pe, z_t, i * NC + (m - 1))
                    o = out_cols(m)
                    product(pc[m % 2][:, :], [(ws_h[:, c, o], ws_l[:, c, o], x_h[:, c, :], x_l[:, c, :])
                                              for c in range(NC)]).then_inc(soma_mm, 1)

            def mod_product(i):
                pe.wait_ge(h1_hi, i + 1)
                pe.wait_ge(h1_lo, i + 1)
                for d in range(D):
                    pe.wait_ge(soma_g, i * NC + (3 + d))
                    product(pc[d][:, :], [(wn2_h[:, d, :], wn2_l[:, d, :], h_h[:, :], h_l[:, :])]).then_inc(mod_mm, 1)

            def z_product(i):
                for m in range(NC):
                    if m < 2:
                        pe.wait_ge(mod_t, i * D + (m + 1))
                    else:
                        pe.wait_ge(z_t, i * NC + (m - 1))
                    o = out_cols(m)
                    product(pc[m % 2][:, :],
                            [(wg_h[:, c, o], wg_l[:, c, o], x_h[:, c, :], x_l[:, c, :]) for c in range(NC)],
                            stop=False)
                    if m == 0:
                        pe.wait_ge(ctx_hi, i * NC + NC)
                        pe.wait_ge(ctx_lo, i * NC + NC)
                    product(pc[m % 2][:, :],
                            [(wg_h[:, NC + c, o], wg_l[:, NC + c, o], c_h[:, c, :], c_l[:, c, :])
                             for c in range(NC)], start=False).then_inc(z_mm, 1)

            def temp_product(j):
                def part(c, m):
                    if c == 0:
                        after(pe, ln_centred, j * TILES + (m - 3))
                    o = out_cols(m)
                    nc.tensor.matmul(pm[m][:, :], wt_h[:, c, o], t_h[:, c, :], start=(c == 0), stop=False)
                    nc.tensor.matmul(pm[m][:, :], wt_h[:, c, o], t_l[:, c, :], start=False, stop=False)
                    last = nc.tensor.matmul(pm[m][:, :], wt_l[:, c, o], t_h[:, c, :], start=False,
                                            stop=(c == NC - 1))
                    if c == NC - 1:
                        last.then_inc(wt_mm, 1)

                for c in (0, 1):
                    pe.wait_ge(temp_hi, j * NC + (c + 1))
                    pe.wait_ge(temp_lo, j * NC + (c + 1))
                    for m in range(NC - 1):
                        part(c, m)
                for c in (0, 1):
                    part(c, NC - 1)
                for c in (2, 3):
                    pe.wait_ge(temp_hi, j * NC + (c + 1))
                    pe.wait_ge(temp_lo, j * NC + (c + 1))
                    for m in range(NC):
                        part(c, m)

            def out_product(j, k):
                if k == 0:
                    pe.wait_ge(gate_t, j * NC + NC)
                    pe.wait_ge(s_hi, j * NC + NC)
                    pe.wait_ge(s_lo, j * NC + NC)
                tok = out_cols(k)
                product(pm[k][:, :], [(s_h[:, c, tok], s_l[:, c, tok], wo_h[:, c, :], wo_l[:, c, :])
                                      for c in range(NC)]).then_inc(wo_mm, 1)

            def step(i, nxt):
                temp_product(i - 1)
                h1_product(i)
                soma_product(i)
                mod_product(i)
                z_product(i)
                for k in range(TILES):
                    out_product(i - 1, k)
                    if nxt:
                        turn_x(i + 1, k)

            pe.wait_ge(setup_done, 1)
            prepare(0)
            for k in range(TILES):
                turn_x(0, k)
            prepare(1)
            ready(0)
            h1_product(0)
            ready(1)
            soma_product(0)
            prepare(2)
            prepare(3)
            pe.wait_ge(consts_v, 1 + D)
            mod_product(0)
            ready(3)
            z_product(0)
            for k in range(TILES):
                turn_x(1, k)
            prepare(4)
            prepare(5)
            ready(5)
            step(1, True)
            with pe.Fori(2, NBLK - 1) as i:
                step(i, True)
            step(NBLK - 1, False)
            temp_product(NBLK - 1)
            for k in range(TILES):
                out_product(NBLK - 1, k)

            def beta_product(b):
                pe.wait_ge(v_eye, 2 * b + 1)
                if b == 0:
                    pe.wait_ge(ln_centred, NBLK * TILES)
                    pe.wait_ge(xlo, NBLK * TILES)
                else:
                    pe.wait_ge(y_hi, 2 * TILES)
                    pe.wait_ge(y_lo, 2 * TILES)
                for m in range(NC):
                    for c in range(NC):
                        last = nc.tensor.matmul(pt[1][:, 2 * m:2 * m + 1], stage_b[:, c, out_cols(m)],
                                                cols["beta0"][:, c:c + 1], start=(c == 0), stop=(c == NC - 1))
                last.then_inc(bias_mm, 1)

            def turn_l3(b):
                pe.wait_ge(v_eye, 2 * b + 2)
                pe.wait_ge(bias_done, b + 1)
                if b == 0:
                    pe.wait_ge(h1_gelu, NBLK)
                else:
                    pe.wait_ge(y_hi, (PER_SEQ + 1) * TILES)
                    pe.wait_ge(y_lo, (PER_SEQ + 1) * TILES)
                for k in range(NC):
                    if k >= 2:
                        pe.wait_ge(v_hi, V_ALL * b + V_L3 + (k - 1))
                        pe.wait_ge(v_lo, V_ALL * b + V_L3 + (k - 1))
                    turn(pt[k % 2], [stage_b[:, q, out_cols(k)] for q in range(4)]).then_inc(v_turned, 1)

            def turn_y(i, k, shared=False):
                if k < 2 and shared:
                    pe.wait_ge(x3_sum, i * NC + (k - 5))
                pe.wait_ge(y_in[k % 2], (i * 2 + (k // 2 + 1)) * 16)
                if k >= 2:
                    pe.wait_ge(y_hi, i * TILES + (k - 1))
                    pe.wait_ge(y_lo, i * TILES + (k - 1))
                turn(pt[k % 2], [x_tok[:, k % 2, out_cols(c)] for c in range(NC)]).then_inc(ty_done, 1)

            def l1_product(i, b, m):
                if m == 0:
                    pe.wait_ge(y_hi, i * TILES + TILES)
                    pe.wait_ge(y_lo, i * TILES + TILES)
                    after(pe, relu_done, i)
                if m >= 2:
                    pe.wait_ge(x2_hi, i * NC + (m - 1))
                    pe.wait_ge(x2_lo, i * NC + (m - 1))
                o = out_cols(m)
                wh, wl = l1_w(b)
                product(pc[m % 2][:, :], [(wh[:, c, o], wl[:, c, o], x_h[:, c, :], x_l[:, c, :])
                                          for c in range(NC)]).then_inc(l1_mm, 1)

            def w1_product(i, b):
                pe.wait_ge(x2_hi, i * NC + NC)
                pe.wait_ge(x2_lo, i * NC + NC)
                wh, wl = w1_w(b)
                product(pc[0][:, :], [(wh[:, c, :], wl[:, c, :], c_h[:, c, :], c_l[:, c, :])
                                      for c in range(NC)]).then_inc(w1_mm, 1)

            def xx_product(i, b, k):
                if k == 0:
                    pe.wait_ge(hid_hi, i + 1)
                    pe.wait_ge(hid_lo, i + 1)
                after(pe, out_ready, i * TILES + (k - 3))
                tok = out_cols(k)
                turn(pm[k], [x_t[:, c, tok] for c in range(NC)], stop=False)
                wh, wl = w2_w(b)
                nc.tensor.matmul(pm[k][:, :], h_h[:, tok], wh, start=False, stop=False, skip_group_check=True)
                nc.tensor.matmul(pm[k][:, :], h_l[:, tok], wh, start=False, stop=False, skip_group_check=True)
                nc.tensor.matmul(pm[k][:, :], h_h[:, tok], wl, start=False, stop=True,
                                 skip_group_check=True).then_inc(xx_mm, 1)

            def turn_n2(j, chunks):
                for c in chunks:
                    if c == 0:
                        pe.wait_ge(n2_done, j * TILES + TILES)
                    if c >= 2:
                        pe.wait_ge(x3_sum, j * NC + (c - 1))
                    turn(pt[c % 2], [stage_a[:, k, out_cols(c)] for k in range(TILES)]).then_inc(tn_done, 1)

            def l3_product(j, b, k):
                if k == 0:
                    pe.wait_ge(x3_hi, j * NC + NC)
                    pe.wait_ge(x3_lo, j * NC + NC)
                pe.wait_ge(n2_done, j * TILES + (k + 1))
                tok = out_cols(k)
                wh, wl = l3_w(b)
                product(pm[k][:, :], [(t_h[:, c, tok], t_l[:, c, tok], wh[:, c, :], wl[:, c, :])
                                      for c in range(NC)]).then_inc(l3_mm, 1)

            def step2(i, b, bp, prev, nxt):
                l1_product(i, b, 0)
                l1_product(i, b, 1)
                if prev:
                    turn_n2(i - 1, (0, 1))
                l1_product(i, b, 2)
                if prev:
                    turn_n2(i - 1, (2, 3))
                l1_product(i, b, 3)
                for k in range(TILES):
                    if nxt:
                        turn_y(i + 1, k, prev)
                    if prev:
                        l3_product(i - 1, bp, k)
                    if k == 0:
                        w1_product(i, b)
                for k in range(TILES):
                    xx_product(i, b, k)

            def split_done(count):
                pe.wait_ge(v_hi, count)
                pe.wait_ge(v_lo, count)

            beta_product(0)
            turn_l3(0)
            split_done(V_ALL)
            pe.wait_ge(z_t, NBLK * NC)
            for k in range(TILES):
                turn_y(0, k)
            step2(0, 0, None, False, True)
            beta_product(1)
            pe.wait_ge(bias_done, 2)
            step2(1, 0, 0, True, True)
            with pe.Fori(2, PER_SEQ) as i:
                step2(i, 0, 0, True, True)
            turn_l3(1)
            split_done(2 * V_ALL)
            step2(PER_SEQ, 1, 0, True, True)
            with pe.Fori(PER_SEQ + 1, NBLK - 1) as i:
                step2(i, 1, 1, True, True)
            step2(NBLK - 1, 1, 1, True, False)
            turn_n2(NBLK - 1, range(NC))
            for k in range(TILES):
                l3_product(NBLK - 1, 1, k)

        @block.scalar
        def _(act):
            def prepare(n):
                for k in range(W_COUNT[n]):
                    c = W_BEFORE[n] + k
                    hi, _ = w_dest(n, k)
                    act.wait_ge(w_turned, c + 1)
                    nc.scalar.activation(hi, pm[c % 4][:, :], ACT.Identity, scale=W_SCALE[n]).then_inc(w_hi, 1)

            def copy_x(i, k):
                tok = slice(k * P, (k + 1) * P)
                act.wait_ge(tx_done, i * TILES + (k + 1))
                if k == 0:
                    after(act, z_mm, i * NC)
                    after(act, gated, i * NC)
                src = pt[k % 2][:, :].rearrange("p (c q) -> p c q", c=NC)
                nc.scalar.activation(x_h[:, :, tok], src, ACT.Identity)
                nc.scalar.activation(x_t[:, :, tok], src, ACT.Identity).then_inc(xcopy, 1)

            def context_hi(i, c):
                if c == 0:
                    after(act, z_mm, i * NC)
                act.wait_ge(ctx_scan, i * NC + (c + 1))
                nc.scalar.activation(c_h[:, c, :], ctx_t[:, c % 2, :], ACT.Identity).then_inc(ctx_hi, 1)

            def hidden(i):
                act.wait_ge(h1_mm, i + 1)
                after(act, h1_lo, i)
                nc.scalar.activation(h1[:, :], pt[0][:, :], ACT.Gelu, bias=col_bn1[:, 0:1]).then_inc(h1_gelu, 1)
                act.wait_ge(h1_gelu, i + 1)
                after(act, mod_mm, i * D)
                nc.scalar.activation(h_h[:, :], h1[:, :], ACT.Identity).then_inc(h1_hi, 1)

            def gate_tanh(j, m):
                act.wait_ge(wt_mm, j * NC + (m + 1))
                after(act, s_lo, j * NC + (m - 1))
                nc.scalar.activation(gate[:, m % 2, :], pm[m][:, :], ACT.Tanh, bias=cols["btemp"][:, m:m + 1],
                                     scale=0.5).then_inc(gate_t, 1)

            def gated_soma_hi(j, m):
                after(act, wo_mm, j * TILES)
                act.wait_ge(s_prod, j * NC + (m + 1))
                nc.scalar.activation(s_h[:, m, :], gate[:, m % 2, :], ACT.Identity).then_inc(s_hi, 1)

            def gates(j):
                gate_tanh(j, 0)
                gate_tanh(j, 1)
                gated_soma_hi(j, 0)
                gate_tanh(j, 2)
                gated_soma_hi(j, 1)
                gate_tanh(j, 3)
                gated_soma_hi(j, 2)
                gated_soma_hi(j, 3)

            def soma_gelu(i, m):
                act.wait_ge(soma_mm, i * NC + (m + 1))
                after(act, s_prod, i * NC + (m - 3))
                nc.scalar.activation(soma[:, m, :], pc[m % 2][:, :], ACT.Gelu,
                                     bias=cols["bsoma"][:, m:m + 1]).then_inc(soma_g, 1)

            def mod_tanh(i):
                for d in range(D):
                    act.wait_ge(mod_mm, i * D + (d + 1))
                    after(act, prods, i * (D * NC))
                    nc.scalar.activation(mod[:, d, :], pc[d][:, :], ACT.Tanh, bias=col_bn2[:, d:d + 1],
                                         scale=0.5).then_inc(mod_t, 1)

            def z_tanh(i, m):
                act.wait_ge(z_mm, i * NC + (m + 1))
                after(act, temp_lo, i * NC + (m - 1))
                nc.scalar.activation(tr1[:, m % 2, :], pc[m % 2][:, :], ACT.Tanh, bias=cols["bg"][:, m:m + 1],
                                     scale=0.5).then_inc(z_t, 1)

            def weigh(i, m):
                act.wait_ge(traces, (i * NC + (m + 1)) * D)
                act.wait_ge(tr_carry, (i * NC + (m + 1)) * D)
                nc.scalar.activation(tr0[:, m % 2, :], tr0[:, m % 2, :], ACT.Identity,
                                     scale=w_blend[:, 0, m:m + 1]).then_inc(weighed, 1)

            def temporal_hi(i, m):
                after(act, wt_mm, i * NC)
                act.wait_ge(blended, i * NC + (m + 1))
                nc.scalar.activation(t_h[:, m, :], tr0[:, m % 2, :], ACT.Identity).then_inc(temp_hi, 1)

            def trace_part(i):
                z_tanh(i, 0)
                for m in range(NC - 1):
                    z_tanh(i, m + 1)
                    weigh(i, m)
                    temporal_hi(i, m)

            def trace_end(i, nxt):
                if nxt:
                    copy_x(i + 1, 0)
                weigh(i, 3)
                if nxt:
                    copy_x(i + 1, 1)
                temporal_hi(i, 3)
                if nxt:
                    copy_x(i + 1, 2)
                    copy_x(i + 1, 3)

            def step(i, nxt):
                gates(i - 1)
                hidden(i)
                soma_gelu(i, 0)
                context_hi(i, 0)
                soma_gelu(i, 1)
                context_hi(i, 1)
                context_hi(i, 2)
                soma_gelu(i, 2)
                context_hi(i, 3)
                soma_gelu(i, 3)
                mod_tanh(i)
                trace_part(i)
                trace_end(i, nxt)

            prepare(0)
            for k in range(TILES):
                copy_x(0, k)
            act.wait_ge(consts_v, 1)
            nc.scalar.activation(alpha[:, :], taus[:, :], ACT.Tanh, scale=-0.5).then_inc(consts_a, 1)
            nc.scalar.activation(w_blend[:, :, :], dblend[:, :, :], ACT.Tanh, scale=0.5).then_inc(consts_a, 1)
            prepare(1)
            hidden(0)
            for m in range(NC):
                soma_gelu(0, m)
            prepare(2)
            prepare(3)
            for c in range(NC):
                context_hi(0, c)
            mod_tanh(0)
            trace_part(0)
            trace_end(0, True)
            prepare(4)
            prepare(5)
            step(1, True)
            with act.Fori(2, NBLK - 1) as i:
                step(i, True)
            step(NBLK - 1, False)

            def l1_hi(b):
                act.wait_ge(z_mm, NBLK * NC)
                act.wait_ge(v_eye, 2 * b + 1)
                for k in range(NC):
                    nc.scalar.activation(l1_w(b)[0][:, k, :], stage_b[:, k, :], ACT.Identity).then_inc(v_hi, 1)

            def l2_l3_hi(b):
                act.wait_ge(wo_mm, NBLK * TILES)
                act.wait_ge(l1_in[b], 48)
                nc.scalar.activation(w1_w(b)[0], stage_b[:, 0, :].rearrange("p (k a) -> p k a", k=NC),
                                     ACT.Identity).then_inc(v_hi, 1)
                nc.scalar.activation(w2_w(b)[0], stage_b[:, 1, :], ACT.Identity).then_inc(v_hi, 1)
                for k in range(NC):
                    act.wait_ge(v_turned, b * NC + k + 1)
                    nc.scalar.activation(l3_w(b)[0][:, k, :], pt[k % 2][:, :], ACT.Identity).then_inc(v_hi, 1)

            def copy_y(i, k):
                tok = slice(k * P, (k + 1) * P)
                act.wait_ge(ty_done, i * TILES + (k + 1))
                if k == 0:
                    after(act, l1_mm, i * NC)
                nc.scalar.activation(x_h[:, :, tok], pt[k % 2][:, :].rearrange("p (c q) -> p c q", c=NC),
                                     ACT.Identity).then_inc(y_hi, 1)

            def x2_parts(i, b, m):
                act.wait_ge(l1_mm, i * NC + (m + 1))
                after(act, w1_mm, i)
                nc.scalar.activation(c_h[:, m, :], pc[m % 2][:, :], ACT.Identity, bias=seq["b1"][:, b, m:m + 1])
                after(act, xx_mm, i * TILES)
                nc.scalar.activation(x_t[:, m, :], pc[m % 2][:, :], ACT.Identity,
                                     bias=seq["b1b2"][:, b, m:m + 1]).then_inc(x2_hi, 1)

            def x2_beta(i, b, m):
                after(act, x3_sum, i * NC + (m - 3))
                act.wait_ge(x2_hi, i * NC + (m + 1))
                nc.scalar.activation(soma[:, m, :], x_t[:, m, :], ACT.Identity,
                                     bias=seq["beta_b2"][:, b, m:m + 1]).then_inc(x2_all, 1)

            def x3_hi_part(j, m):
                after(act, l3_mm, j * TILES)
                act.wait_ge(x3_sum, j * NC + (m + 1))
                nc.scalar.activation(t_h[:, m, :], gate[:, m % 2, :], ACT.Identity).then_inc(x3_hi, 1)

            def relu_part(i, b):
                act.wait_ge(w1_mm, i + 1)
                after(act, hid_lo, i)
                nc.scalar.activation(h1[:, :], pc[0][:, :], ACT.Relu, bias=seq["lb1"][:, b, 0:1]).then_inc(relu_done, 1)
                act.wait_ge(relu_done, i + 1)
                after(act, xx_mm, i * TILES)
                nc.scalar.activation(h_h[:, :], h1[:, :], ACT.Identity).then_inc(hid_hi, 1)

            def normalise(i, k):
                act.wait_ge(ln2_rstd, i + 1)
                after(act, tn_done, i * NC)
                nc.scalar.activation(stage_a[:, k, :], pm[k][:, :], ACT.Identity, bias=nbias[:, k:k + 1],
                                     scale=rstd[:, k:k + 1]).then_inc(n2_done, 1)

            def step2(i, b, prev, nxt):
                x2_parts(i, b, 0)
                x2_parts(i, b, 1)
                x2_beta(i, b, 0)
                x2_beta(i, b, 1)
                if prev:
                    x3_hi_part(i - 1, 0)
                    x3_hi_part(i - 1, 1)
                x2_parts(i, b, 2)
                if prev:
                    x3_hi_part(i - 1, 2)
                    x3_hi_part(i - 1, 3)
                x2_parts(i, b, 3)
                for k in range(TILES):
                    if nxt:
                        copy_y(i + 1, k)
                    if k == 0:
                        relu_part(i, b)
                    if k == 1:
                        x2_beta(i, b, 2)
                        x2_beta(i, b, 3)
                for k in range(TILES):
                    normalise(i, k)

            l1_hi(0)
            gates(NBLK - 1)
            l2_l3_hi(0)
            for k in range(TILES):
                copy_y(0, k)
            act.wait_ge(bias_done, 1)
            act.wait_ge(s_prod, NBLK * NC)
            act.wait_ge(x1_out[0], 16 * 2 * NBLK)
            act.wait_ge(x1_out[1], 16 * 2 * NBLK)
            step2(0, 0, False, True)
            l1_hi(1)
            step2(1, 0, True, True)
            with act.Fori(2, PER_SEQ) as i:
                step2(i, 0, True, True)
            l2_l3_hi(1)
            act.wait_ge(bias_done, 2)
            step2(PER_SEQ, 1, True, True)
            with act.Fori(PER_SEQ + 1, NBLK - 1) as i:
                step2(i, 1, True, True)
            step2(NBLK - 1, 1, True, False)
            for m in range(NC):
                x3_hi_part(NBLK - 1, m)

        @block.vector
        def _(dve):
            def f32(ap):
                return ap.bitcast(F32)

            def prepare(n):
                for k in range(W_COUNT[n]):
                    c = W_BEFORE[n] + k
                    hi, lo = w_dest(n, k)
                    dve.wait_ge(w_hi, c + 1)
                    nc.vector.scalar_tensor_tensor(lo, pm[c % 4][:, :], W_SCALE[n], f32(hi), ALU.mult,
                                                   ALU.subtract).then_inc(w_lo, 1)

            def x_lo_first(k):
                tok = slice(k * P, (k + 1) * P)
                dve.wait_ge(xcopy, k + 1)
                nc.vector.tensor_tensor(x_l[:, :, tok], x_t[:, :, tok], f32(x_h[:, :, tok]),
                                        ALU.subtract).then_inc(xlo, 1)

            def scan_context(i, c):
                after(dve, ctx_hi, i * NC + (c - 1))
                after(dve, ctx_lo, i * NC + (c - 1))
                after(dve, ctx_carry, i * NC + (c - 3))
                nc.vector.tensor_tensor_scan(ctx_t[:, c % 2, :], alpha[:, 0:1].to_broadcast([P, BLK]), x_t[:, c, :],
                                             carry[:, 0, c:c + 1], ALU.mult, ALU.add).then_inc(ctx_scan, 1)

            def carry_context(i, c):
                dve.wait_ge(ctx_scan, i * NC + (c + 1))
                nc.vector.tensor_scalar(carry[:, 0, c:c + 1], ctx_t[:, c % 2, BLK - 1:BLK],
                                        keep[:, bass.ds(i + 1, 1)], None, ALU.mult).then_inc(ctx_carry, 1)

            def split_context(i, c):
                dve.wait_ge(ctx_hi, i * NC + (c + 1))
                nc.vector.tensor_tensor(c_l[:, c, :], ctx_t[:, c % 2, :], f32(c_h[:, c, :]),
                                        ALU.subtract).then_inc(ctx_lo, 1)

            def context(i):
                dve.wait_ge(xcopy, i * TILES + TILES)
                after(dve, z_mm, i * NC)
                scan_context(i, 0)
                scan_context(i, 1)
                carry_context(i, 0)
                split_context(i, 0)
                scan_context(i, 2)
                carry_context(i, 1)
                split_context(i, 1)
                scan_context(i, 3)
                carry_context(i, 2)
                split_context(i, 2)
                carry_context(i, 3)
                split_context(i, 3)

            def hidden_lo(i):
                dve.wait_ge(h1_hi, i + 1)
                after(dve, mod_mm, i * D)
                nc.vector.tensor_tensor(h_l[:, :], h1[:, :], f32(h_h[:, :]), ALU.subtract).then_inc(h1_lo, 1)

            def gate_soma(j, m):
                dve.wait_ge(gate_t, j * NC + (m + 1))
                dve.wait_ge(soma_g, j * NC + (m + 1))
                nc.vector.scalar_tensor_tensor(gate[:, m % 2, :], gate[:, m % 2, :], 1.0, soma[:, m, :],
                                               ALU.add, ALU.mult).then_inc(s_prod, 1)

            def gated_soma_lo(j, m):
                after(dve, wo_mm, j * TILES)
                dve.wait_ge(s_hi, j * NC + (m + 1))
                nc.vector.tensor_tensor(s_l[:, m, :], gate[:, m % 2, :], f32(s_h[:, m, :]),
                                        ALU.subtract).then_inc(s_lo, 1)

            def gates(j):
                gate_soma(j, 0)
                gate_soma(j, 1)
                gated_soma_lo(j, 0)
                gate_soma(j, 2)
                gated_soma_lo(j, 1)
                gate_soma(j, 3)
                gated_soma_lo(j, 2)
                gated_soma_lo(j, 3)

            def gate_x(i, m):
                dve.wait_ge(z_t, i * NC + (m + 1))
                nc.vector.scalar_tensor_tensor(tr1[:, m % 2, :], tr1[:, m % 2, :], 1.0, x_t[:, m, :],
                                               ALU.add, ALU.mult).then_inc(gated, 1)

            def modulate(i, m):
                dve.wait_ge(gated, i * NC + (m + 1))
                dve.wait_ge(mod_t, i * D + D)
                nc.vector.scalar_tensor_tensor(tr0[:, m % 2, :], mod[:, 0, :], 2.0, tr1[:, m % 2, :],
                                               ALU.add, ALU.mult).then_inc(prods, 1)
                nc.vector.scalar_tensor_tensor(tr1[:, m % 2, :], mod[:, 1, :], 2.0, tr1[:, m % 2, :],
                                               ALU.add, ALU.mult).then_inc(prods, 1)

            def scan_traces(i, m):
                after(dve, tr_carry, (i * NC + (m - 3)) * D)
                for d, tr in enumerate((tr0, tr1)):
                    dve.wait_ge(prods, i * (D * NC) + (m * D + d + 1))
                    nc.vector.tensor_tensor_scan(tr[:, m % 2, :], alpha[:, 1 + d:2 + d].to_broadcast([P, BLK]),
                                                 tr[:, m % 2, :], carry[:, 1 + d, m:m + 1], ALU.mult,
                                                 ALU.add).then_inc(traces, 1)
                for d, tr in enumerate((tr0, tr1)):
                    dve.wait_ge(traces, i * (D * NC) + (m * D + d + 1))
                    nc.vector.tensor_scalar(carry[:, 1 + d, m:m + 1], tr[:, m % 2, BLK - 1:BLK],
                                            keep[:, bass.ds(i + 1, 1)], None, ALU.mult).then_inc(tr_carry, 1)

            def blend_traces(i, m):
                dve.wait_ge(weighed, i * NC + (m + 1))
                nc.vector.scalar_tensor_tensor(tr0[:, m % 2, :], tr1[:, m % 2, :], w_blend[:, 1, m:m + 1],
                                               tr0[:, m % 2, :], ALU.mult, ALU.add).then_inc(blended, 1)

            def temporal_lo(i, m):
                after(dve, wt_mm, i * NC)
                dve.wait_ge(temp_hi, i * NC + (m + 1))
                nc.vector.tensor_tensor(t_l[:, m, :], tr0[:, m % 2, :], f32(t_h[:, m, :]),
                                        ALU.subtract).then_inc(temp_lo, 1)

            def trace_part(i):
                gate_x(i, 0)
                modulate(i, 0)
                scan_traces(i, 0)
                gate_x(i, 1)
                blend_traces(i, 0)
                modulate(i, 1)
                temporal_lo(i, 0)
                scan_traces(i, 1)
                gate_x(i, 2)
                blend_traces(i, 1)
                modulate(i, 2)
                temporal_lo(i, 1)
                scan_traces(i, 2)
                gate_x(i, 3)
                blend_traces(i, 2)
                modulate(i, 3)
                temporal_lo(i, 2)
                scan_traces(i, 3)

            def norm_stats(j, k):
                dve.wait_ge(wo_mm, j * TILES + (k + 1))
                after(dve, ln_mv, j * TILES + (k - 3))
                nc.vector.bn_stats(stats[:, k, :], pm[k][:, :]).then_inc(ln_stats, 1)
                dve.wait_ge(ln_stats, j * TILES + (k + 1))
                dve.sem_inc(stats_seen, 1)
                nc.vector.bn_aggr(mv[:, k, :], stats[:, k, :]).then_inc(ln_mv, 1)
                dve.wait_ge(ln_mv, j * TILES + (k + 1))
                after(dve, x1_ready, j * TILES + (k - 1))
                nc.vector.scalar_tensor_tensor(normed[:, k % 2, :], pm[k][:, :], mv[:, k, 0:1], gamma_row[:, :],
                                               ALU.subtract, ALU.mult).then_inc(ln_centred, 1)

            def norm_sum(j, k):
                dve.wait_ge(ln_centred, j * TILES + (k + 1))
                dve.wait_ge(ln_rstd, j * TILES + (k + 1))
                dve.wait_ge(again_in[k % 2], (j * 2 + (k // 2 + 1)) * 16)
                nc.vector.scalar_tensor_tensor(x_again[:, k % 2, :], normed[:, k % 2, :], rstd[:, k:k + 1],
                                               x_again[:, k % 2, :], ALU.mult, ALU.add).then_inc(x1_ready, 1)

            def tail(i):
                j = i - 1
                norm_stats(j, 0)
                blend_traces(i, 3)
                norm_stats(j, 1)
                temporal_lo(i, 3)
                norm_sum(j, 0)
                norm_stats(j, 2)
                norm_sum(j, 1)
                norm_stats(j, 3)
                norm_sum(j, 2)
                norm_sum(j, 3)

            def step(i):
                gates(i - 1)
                context(i)
                hidden_lo(i)
                trace_part(i)
                tail(i)

            nc.vector.memset(keep[:, :], 1.0).then_inc(setup_v, 1)
            nc.vector.memset(carry[:, :, :], 0.0).then_inc(setup_v, 1)
            dve.wait_ge(setup_v, 2)
            for b in range(B + 1):
                nc.vector.memset(keep[:, b * PER_SEQ:b * PER_SEQ + 1], 0.0).then_inc(setup_v, 1)
            dve.wait_ge(small_in, 16 * 12)
            for d in range(D):
                nc.vector.tensor_tensor(dblend[:, d, :], blend[:, d, :], blend[:, 1 - d, :],
                                        ALU.subtract).then_inc(setup_v, 1)
            nc.vector.tensor_scalar(cols["bg"][:, :], cols["bg"][:, :], 0.5, None, ALU.mult).then_inc(setup_v, 1)
            nc.vector.tensor_scalar(cols["btemp"][:, :], cols["btemp"][:, :], 0.5, None, ALU.mult).then_inc(setup_v, 1)
            nc.vector.tensor_scalar(col_bn2[:, :], col_bn2[:, :], 0.5, None, ALU.mult).then_inc(consts_v, 1)
            prepare(0)
            for k in range(TILES):
                x_lo_first(k)
            dve.wait_ge(consts_a, 2)
            nc.vector.tensor_scalar(alpha[:, :], alpha[:, :], 0.5, 0.5, ALU.mult, ALU.add).then_inc(setup_v, 1)
            nc.vector.tensor_scalar(w_blend[:, :, :], w_blend[:, :, :], 0.125, 0.125, ALU.mult,
                                    ALU.add).then_inc(setup_v, 1)
            dve.wait_ge(setup_v, 7 + B + D)
            dve.wait_ge(setup_done, 1)
            for d in range(D):
                nc.vector.tensor_scalar(wn2_h[:, d, :], ident[:, :], 0.0, col_wn2[:, d:d + 1], ALU.mult,
                                        ALU.add).then_inc(setup_v, 1)
            dve.wait_ge(setup_v, 7 + B + 2 * D)
            for d in range(D):
                nc.vector.tensor_scalar(wn2_l[:, d, :], f32(wn2_h[:, d, :]), -1.0, col_wn2[:, d:d + 1], ALU.mult,
                                        ALU.add).then_inc(consts_v, 1)
            prepare(1)
            hidden_lo(0)
            prepare(2)
            prepare(3)
            context(0)
            trace_part(0)
            blend_traces(0, 3)
            temporal_lo(0, 3)
            prepare(4)
            prepare(5)
            step(1)
            with dve.Fori(2, NBLK) as i:
                step(i)

            def add_eye(semaphore, count, b):
                dve.wait_ge(semaphore, count)
                for q in range(NC):
                    o = slice(q * P, (q + 1) * P)
                    last = nc.vector.tensor_tensor(stage_b[:, q, o], stage_b[:, q, o], ident[:, :], ALU.add)
                last.then_inc(v_eye, 1)

            def l1_lo(b):
                for k in range(NC):
                    dve.wait_ge(v_hi, V_ALL * b + k + 1)
                    wh, wl = l1_w(b)
                    nc.vector.tensor_tensor(wl[:, k, :], stage_b[:, k, :], f32(wh[:, k, :]),
                                            ALU.subtract).then_inc(v_lo, 1)

            def biases(b):
                dve.wait_ge(bias_mm, b + 1)
                dve.wait_ge(lw_in[b], 16 * 6)
                share = pt[1][:, 0:2 * NC].rearrange("p (c q) -> p c q", q=2)[:, :, 0]
                nc.vector.tensor_tensor(seq["b1"][:, b, :], share, seq["b1"][:, b, :], ALU.add).then_inc(setup_v, 1)
                dve.wait_ge(setup_v, 7 + B + 2 * D + b + 1)
                nc.vector.tensor_tensor(seq["b1b2"][:, b, :], seq["b1"][:, b, :], seq["b2"][:, b, :], ALU.add)
                nc.vector.tensor_tensor(seq["beta_b2"][:, b, :], seq["beta2"][:, b, :], seq["b2"][:, b, :],
                                        ALU.subtract).then_inc(bias_done, 1)

            def l2_l3_lo(b):
                at = V_ALL * b + V_L2
                dve.wait_ge(v_hi, at + 1)
                wh, wl = w1_w(b)
                nc.vector.tensor_tensor(wl, stage_b[:, 0, :].rearrange("p (k a) -> p k a", k=NC), f32(wh),
                                        ALU.subtract).then_inc(v_lo, 1)
                dve.wait_ge(v_hi, at + 2)
                wh, wl = w2_w(b)
                nc.vector.tensor_tensor(wl, stage_b[:, 1, :], f32(wh), ALU.subtract).then_inc(v_lo, 1)
                add_eye(l3_in[b], 16, b)
                for k in range(NC):
                    dve.wait_ge(v_hi, at + 3 + k)
                    wh, wl = l3_w(b)
                    nc.vector.tensor_tensor(wl[:, k, :], pt[k % 2][:, :], f32(wh[:, k, :]),
                                            ALU.subtract).then_inc(v_lo, 1)

            def y_lo_part(i, k):
                tok = slice(k * P, (k + 1) * P)
                dve.wait_ge(y_hi, i * TILES + (k + 1))
                nc.vector.tensor_tensor(x_l[:, :, tok], pt[k % 2][:, :].rearrange("p (c q) -> p c q", c=NC),
                                        f32(x_h[:, :, tok]), ALU.subtract).then_inc(y_lo, 1)

            def x2_lo_part(i, b, m):
                after(dve, w1_mm, i)
                dve.wait_ge(x2_hi, i * NC + (m + 1))
                nc.vector.scalar_tensor_tensor(c_l[:, m, :], pc[m % 2][:, :], seq["b1"][:, b, m:m + 1],
                                               f32(c_h[:, m, :]), ALU.add, ALU.subtract).then_inc(x2_lo, 1)

            def x3_sum_part(j, b, m):
                dve.wait_ge(tn_done, j * NC + (m + 1))
                dve.wait_ge(x2_all, j * NC + (m + 1))
                if m >= 2:
                    dve.wait_ge(x3_hi, j * NC + (m - 1))
                    dve.wait_ge(x3_lo, j * NC + (m - 1))
                nc.vector.scalar_tensor_tensor(gate[:, m % 2, :], pt[m % 2][:, :], seq["gamma2"][:, b, m:m + 1],
                                               soma[:, m, :], ALU.mult, ALU.add).then_inc(x3_sum, 1)

            def x3_lo_part(j, m):
                after(dve, l3_mm, j * TILES)
                dve.wait_ge(x3_hi, j * NC + (m + 1))
                nc.vector.tensor_tensor(t_l[:, m, :], gate[:, m % 2, :], f32(t_h[:, m, :]),
                                        ALU.subtract).then_inc(x3_lo, 1)

            def hid_lo_part(i):
                dve.wait_ge(hid_hi, i + 1)
                nc.vector.tensor_tensor(h_l[:, :], h1[:, :], f32(h_h[:, :]), ALU.subtract).then_inc(hid_lo, 1)

            def output(j, b, k):
                dve.wait_ge(l3_mm, j * TILES + (k + 1))
                after(dve, out_done[k % 2], (j * 2 + k // 2) * 16)
                nc.vector.tensor_tensor(ctx_t[:, k % 2, :], pm[k][:, :], mod[:, b, :], ALU.add).then_inc(out_ready, 1)

            def norm2_stats(i, k):
                dve.wait_ge(xx_mm, i * TILES + (k + 1))
                nc.vector.bn_stats(stats[:, k, :], pm[k][:, :]).then_inc(ln2_stats, 1)
                dve.wait_ge(ln2_stats, i * TILES + (k + 1))
                dve.sem_inc(stats_seen, 1)
                nc.vector.bn_aggr(mv[:, k, :], stats[:, k, :]).then_inc(ln2_mv, 1)

            def step2(i, b, bp, prev, nxt):
                x2_lo_part(i, b, 0)
                x2_lo_part(i, b, 1)
                if prev:
                    x3_sum_part(i - 1, bp, 0)
                    x3_sum_part(i - 1, bp, 1)
                    x3_lo_part(i - 1, 0)
                    x3_lo_part(i - 1, 1)
                x2_lo_part(i, b, 2)
                if prev:
                    x3_sum_part(i - 1, bp, 2)
                    x3_sum_part(i - 1, bp, 3)
                    x3_lo_part(i - 1, 2)
                    x3_lo_part(i - 1, 3)
                x2_lo_part(i, b, 3)
                for k in range(TILES):
                    if nxt:
                        y_lo_part(i + 1, k)
                    if prev:
                        output(i - 1, bp, k)
                    if k == 0:
                        hid_lo_part(i)
                for k in range(TILES):
                    norm2_stats(i, k)

            add_eye(l1_in[0], 16, 0)
            l1_lo(0)
            gates(NBLK - 1)
            for k in range(TILES):
                norm_stats(NBLK - 1, k)
                if k:
                    norm_sum(NBLK - 1, k - 1)
            norm_sum(NBLK - 1, TILES - 1)
            biases(0)
            l2_l3_lo(0)
            for k in range(TILES):
                y_lo_part(0, k)
            step2(0, 0, None, False, True)
            add_eye(l1_in[1], 16, 1)
            l1_lo(1)
            biases(1)
            step2(1, 0, 0, True, True)
            with dve.Fori(2, PER_SEQ) as i:
                step2(i, 0, 0, True, True)
            l2_l3_lo(1)
            step2(PER_SEQ, 1, 0, True, True)
            with dve.Fori(PER_SEQ + 1, NBLK - 1) as i:
                step2(i, 1, 1, True, True)
            step2(NBLK - 1, 1, 1, True, False)
            x3_sum_part(NBLK - 1, 1, 0)
            x3_sum_part(NBLK - 1, 1, 1)
            x3_lo_part(NBLK - 1, 0)
            x3_sum_part(NBLK - 1, 1, 2)
            x3_lo_part(NBLK - 1, 1)
            x3_sum_part(NBLK - 1, 1, 3)
            x3_lo_part(NBLK - 1, 2)
            x3_lo_part(NBLK - 1, 3)
            for k in range(TILES):
                output(NBLK - 1, 1, k)


_INS = ['x', 'condB_tauraws', 'cond_256', 'condB_bn2', 'cond_1024', 'itok_B_0_30', 'itok_B_0_8', 'itok_B_0_7',
        'L0_cond_tau_ctx', 'L0_cond_Wg', 'L0_cond_bg', 'L0_cond_Wn1', 'L0_cond_bn1', 'L0_cond_Wsoma',
        'L0_cond_bsoma', 'L0_cond_Wtemp', 'L0_cond_btemp', 'L0_cond_Wout', 'L0_cond_gamma', 'L0_cond_beta',
        'L1_cond_W', 'L1_cond_b', 'L2_cond_W1', 'L2_cond_b1', 'L2_cond_W2', 'L2_cond_b2', 'L2_cond_gamma',
        'L2_cond_beta', 'L3_cond_weight', 'L3_cond_bias']


def kernel(**inputs):
    import numpy as _np
    import concourse.bacc as _bacc
    from concourse import mybir as _mybir
    from concourse.bass_utils import run_bass_kernel_spmd as _run

    nc = _bacc.Bacc("TRN2", target_bir_lowering=False, num_devices=1)
    arrays, args = {}, {}
    for name in _INS:
        a = _np.ascontiguousarray(inputs[name])
        if a.ndim == 0:
            a = a.reshape(1)
        arrays[f"in_{name}_dram"] = a
        args[name] = nc.dram_tensor(f"in_{name}_dram", a.shape, _mybir.dt.from_np(a.dtype), kind="ExternalInput").ap()
    x = arrays["in_x_dram"]
    out = nc.dram_tensor("out_0_dram", x.shape, _mybir.dt.from_np(x.dtype), kind="ExternalOutput").ap()
    residual_chain_kernel(nc, args, out)
    r = _run(nc, [arrays], core_ids=[0])
    return r.results[0]["out_0_dram"]
```

```python
from contextlib import ExitStack

import concourse.bass as bass
from concourse import mybir

P = 128
BLK = 512
ALU = mybir.AluOpType
ACT = mybir.ActivationFunctionType
F32 = mybir.dt.float32
F32R = mybir.dt.float32r
I32 = mybir.dt.int32
EPS = 1e-5


def after(engine, semaphore, count):
    if not isinstance(count, int) or count > 0:
        engine.wait_ge(semaphore, count)


def residual_chain_kernel(nc: bass.Bass, t: dict, out: bass.AP):
    B, SEQ, E = t["x"].shape
    NC = E // P
    NBLK = B * SEQ // BLK
    PER_SEQ = SEQ // BLK
    TILES = BLK // P
    D = t["condB_tauraws"].shape[0]
    H = t["L0_cond_Wn1"].shape[0]
    A = t["L2_cond_W1"].shape[2]
    assert NC == 4 and TILES == 4 and D == 2 and B == 2 and H == P and A == P and NBLK == 8

    x_tiles = t["x"].rearrange("b (n p) e -> (b n) p e", p=P)
    out_tiles = out.rearrange("b (n p) e -> (b n) p e", p=P)
    x1_tiles = nc.dram_tensor("x1_scratch", (NBLK * TILES, P, E), F32, kind="Internal").ap()

    with ExitStack() as ctx:
        def sb(name, shape, dt=F32):
            return ctx.enter_context(nc.sbuf_tensor(name, shape, dt))

        def sem(name):
            return ctx.enter_context(nc.semaphore(name))

        wg_h, wg_l = sb("wg_h", [P, 2 * NC, E], F32R), sb("wg_l", [P, 2 * NC, E], F32R)
        ws_h, ws_l = sb("ws_h", [P, NC, E], F32R), sb("ws_l", [P, NC, E], F32R)
        wt_h, wt_l = sb("wt_h", [P, NC, E], F32R), sb("wt_l", [P, NC, E], F32R)
        wo_h, wo_l = sb("wo_h", [P, NC, E], F32R), sb("wo_l", [P, NC, E], F32R)
        wn1_h, wn1_l = sb("wn1_h", [P, NC, H], F32R), sb("wn1_l", [P, NC, H], F32R)
        wn2_h, wn2_l = sb("wn2_h", [P, D, P], F32R), sb("wn2_l", [P, D, P], F32R)
        x_tok = sb("x_tok", [P, 2, E])
        x_h, x_l = sb("x_h", [P, NC, BLK], F32R), sb("x_l", [P, NC, BLK], F32R)
        x_t = sb("x_t", [P, NC, BLK])
        ctx_t = sb("ctx_t", [P, 2, BLK])
        c_h, c_l = sb("c_h", [P, NC, BLK], F32R), sb("c_l", [P, NC, BLK], F32R)
        h1 = sb("h1", [P, BLK])
        h_h, h_l = sb("h_h", [P, BLK], F32R), sb("h_l", [P, BLK], F32R)
        mod = sb("mod", [P, D, BLK])
        soma = sb("soma", [P, NC, BLK])
        gate = sb("gate", [P, 2, BLK])
        t_h, t_l = sb("t_h", [P, NC, BLK], F32R), sb("t_l", [P, NC, BLK], F32R)
        s_h, s_l = sb("s_h", [P, NC, BLK], F32R), sb("s_l", [P, NC, BLK], F32R)
        stage_a = sb("stage_a", [P, 4, E])
        stage_b = sb("stage_b", [P, 4, E])
        x_again, normed = stage_a[:, 0:2, :], stage_a[:, 2:4, :]
        tr1, tr0 = stage_b[:, 0:2, :], stage_b[:, 2:4, :]
        gamma_row = sb("gamma_row", [P, E])
        ident = sb("ident", [P, P])
        names = ["bg", "bsoma", "btemp", "beta0"]
        cols = {n: sb("col_" + n, [P, NC]) for n in names}
        col_bn1 = sb("col_bn1", [P, 1])
        col_bn2 = sb("col_bn2", [P, D])
        col_wn2 = sb("col_wn2", [P, D])
        blend = sb("blend", [P, D, NC])
        dblend = sb("dblend", [P, D, NC])
        w_blend = sb("w_blend", [P, D, NC])
        taus = sb("taus", [P, 1 + D])
        alpha = sb("alpha", [P, 1 + D])
        carry = sb("carry", [P, 1 + D, NC])
        keep = sb("keep", [P, NBLK + 1])
        stats = sb("stats", [P, TILES, 6])
        mv = sb("mv", [P, TILES, 2])
        rstd = sb("rstd", [P, TILES])
        nbias = sb("nbias", [P, TILES])
        newton = sb("newton", [P, 3, TILES])
        const = sb("const", [P, 4, TILES])
        l2names = ["b1", "lb1", "b2", "gamma2", "beta2", "b1b2", "beta_b2"]
        seq = {n: sb("seq_" + n, [P, B, NC]) for n in l2names}
        idx = sb("idx", [1, 8], I32)

        pt = [ctx.enter_context(nc.psum_tensor(f"pt{i}", [P, 512], F32)) for i in range(2)]
        pc = [ctx.enter_context(nc.psum_tensor(f"pc{i}", [P, 512], F32)) for i in range(2)]
        pm = [ctx.enter_context(nc.psum_tensor(f"pm{i}", [P, 512], F32)) for i in range(4)]

        x_in = [sem(f"x_in{s}") for s in range(2)]
        first_in = [sem(f"first_in{s}") for s in range(2)]
        again_in = [sem(f"again_in{s}") for s in range(2)]
        x1_out = [sem(f"x1_out{s}") for s in range(2)]
        small_in, wide_in = sem("small_in"), sem("wide_in")
        weight_in = [sem(f"weight_in{n}") for n in range(6)]
        idx_in = sem("idx_in")
        l1_in, l2_in, l3_in, lw_in = ([sem(f"{n}{b}") for b in range(B)] for n in ("l1_in", "l2_in", "l3_in", "lw_in"))
        setup_done = sem("setup_done")
        consts_v = sem("consts_v")
        consts_a = sem("consts_a")
        w_turned = sem("w_turned")
        w_hi = sem("w_hi")
        w_lo = sem("w_lo")
        tx_done, h1_mm, soma_mm, mod_mm, z_mm, wt_mm, wo_mm = (
            sem(n) for n in ("tx_done", "h1_mm", "soma_mm", "mod_mm", "z_mm", "wt_mm", "wo_mm"))
        xcopy, ctx_hi, h1_gelu, h1_hi, soma_g, mod_t, z_t, weighed, temp_hi, gate_t, s_hi = (
            sem(n) for n in ("xcopy", "ctx_hi", "h1_gelu", "h1_hi", "soma_g", "mod_t", "z_t",
                             "weighed", "temp_hi", "gate_t", "s_hi"))
        xlo, ctx_scan, ctx_carry, ctx_lo, h1_lo, s_prod, s_lo, gated, prods, traces, tr_carry = (
            sem(n) for n in ("xlo", "ctx_scan", "ctx_carry", "ctx_lo", "h1_lo", "s_prod", "s_lo",
                             "gated", "prods", "traces", "tr_carry"))
        blended, temp_lo, ln_stats, ln_mv, ln_centred, x1_ready = (
            sem(n) for n in ("blended", "temp_lo", "ln_stats", "ln_mv", "ln_centred", "x1_ready"))
        pool_step, ln_rstd = sem("pool_step"), sem("ln_rstd")
        y_in = [sem(f"y_in{s}") for s in range(2)]
        out_done = [sem(f"out_done{s}") for s in range(2)]
        (ty_done, l1_mm, tn_done, w1_mm, xx_mm, l3_mm) = (
            sem(n) for n in ("ty_done", "l1_mm", "tn_done", "w1_mm", "xx_mm", "l3_mm"))
        (y_hi, x2_hi, x2_all, relu_done, hid_hi, n2_act, n2_dve, x3_hi) = (
            sem(n) for n in ("y_hi", "x2_hi", "x2_all", "relu_done", "hid_hi", "n2_act", "n2_dve", "x3_hi"))
        (y_lo, x2_lo, hid_lo, ln2_stats, ln2_mv, x3_sum, x3_lo, out_ready) = (
            sem(n) for n in ("y_lo", "x2_lo", "hid_lo", "ln2_stats", "ln2_mv", "x3_sum", "x3_lo",
                             "out_ready"))
        ln2_rstd = sem("ln2_rstd")
        setup_v, stats_seen = sem("setup_v"), sem("stats_seen")
        l1_hi, l1_lo, l2_hi, l2_lo, l3_hi, l3_lo = (
            sem(n) for n in ("l1_hi", "l1_lo", "l2_hi", "l2_lo", "l3_hi", "l3_lo"))
        l1_eye, l3_eye, l3_turned, bias_mm, bias_done = (
            sem(n) for n in ("l1_eye", "l3_eye", "l3_turned", "bias_mm", "bias_done"))

        def l1_w(b):
            return wg_h[:, b * NC:(b + 1) * NC, :], wg_l[:, b * NC:(b + 1) * NC, :]

        def w1_w(b):
            if b == 0:
                return wn1_h[:, :, :], wn1_l[:, :, :]
            return tuple(w[:, 1, :].rearrange("p (k a) -> p k a", k=NC) for w in (ws_h, ws_l))

        def w2_w(b):
            return ws_h[:, 2 * b, :], ws_l[:, 2 * b, :]

        def l3_w(b):
            return (wt_h[:, :, :], wt_l[:, :, :]) if b == 0 else (wo_h[:, :, :], wo_l[:, :, :])

        l1_raw = [[ctx_t[:, :, :], mod[:, :, :]], [stage_b[:, 0:2, :], stage_b[:, 2:4, :]]]
        l2_raw = [soma[:, 0:2, :], stage_b[:, 0:2, :]]
        l3_raw = stage_b[:, :, :]

        def l1_chunk(b, k):
            return l1_raw[b][k // 2][:, k % 2, :]

        block = ctx.enter_context(nc.Block())

        def tile_of(tiles, i, j):
            return tiles[bass.ds(i * TILES + j, 1)].rearrange("a p e -> (a p) e")

        wn1_raw, whole_a, whole_b = gate[:, 0:1, :], stage_a, stage_b
        L0W = [
            ("wn1", t["L0_cond_Wn1"].rearrange("(n p) c -> p n c", p=P), wn1_raw),
            ("wsoma", t["L0_cond_Wsoma"].rearrange("(n p) c -> p n c", p=P), whole_a),
            ("wg_x", t["L0_cond_Wg"][:, 0:E].rearrange("(n p) c -> p n c", p=P), whole_b),
            ("wg_ctx", t["L0_cond_Wg"][:, E:2 * E].rearrange("(n p) c -> p n c", p=P), whole_a),
            ("wtemp", t["L0_cond_Wtemp"].rearrange("(n p) c -> p n c", p=P), whole_a),
            ("wout", t["L0_cond_Wout"].rearrange("(n p) c -> p n c", p=P), whole_a),
        ]
        W_COUNT = [1, 4, 4, 4, 4, 4]
        W_SCALE = [1.0, 1.0, 1.0, 1.0, 1.0, 0.5]
        W_BEFORE = [sum(W_COUNT[:n]) for n in range(6)]

        W4_AFTER = [[0, 1], [2], [3], []]

        def w_dest(n, k):
            if n == 0:
                return (w[:, :, :].rearrange("p a b -> p (a b)") for w in (wn1_h, wn1_l))
            h, lo, at = [None, (ws_h, ws_l, 0), (wg_h, wg_l, 0), (wg_h, wg_l, NC), (wt_h, wt_l, 0),
                         (wo_h, wo_l, 0)][n]
            return h[:, at + k, :], lo[:, at + k, :]

        def x_first(j):
            return x_tok[:, j, :] if j < 2 else soma[:, j - 2, :]

        @block.sync
        def _(sp):
            def load_weight(n):
                _, src, raw = L0W[n]
                if n == 3:
                    sp.wait_ge(w_turned, W_BEFORE[2])
                if n in (4, 5):
                    sp.wait_ge(w_turned, W_BEFORE[n])
                sp.dma_start(raw[:, :, :], src).then_inc(weight_in[n], 16)

            def load_x(i, j):
                if isinstance(i, int) and i == 0:
                    loaded = x_in[j] if j < 2 else first_in[j - 2]
                    sp.dma_start(x_first(j), tile_of(x_tiles, 0, j)).then_inc(loaded, 16)
                    return
                after(sp, tx_done, i * TILES + (j - 1))
                if isinstance(i, int) and i == NBLK:
                    sp.wait_ge(x1_out[j % 2], (j // 2 + 1) * 16)
                    src = tile_of(x1_tiles, 0, j)
                else:
                    src = tile_of(x_tiles, i, j)
                sp.dma_start(x_tok[:, j % 2, :], src).then_inc(x_in[j % 2], 16)

            def load_again(j, k):
                after(sp, x1_out[k % 2], (j * 2 + k // 2) * 16)
                sp.dma_start(x_again[:, k % 2, :], tile_of(x_tiles, j, k)).then_inc(again_in[k % 2], 16)

            def store_x1(j, k):
                sp.wait_ge(x1_ready, j * TILES + k + 1)
                sp.dma_start(tile_of(x1_tiles, j, k), x_again[:, k % 2, :]).then_inc(x1_out[k % 2], 16)

            for j in range(TILES):
                load_x(0, j)
            load_weight(0)
            load_weight(1)
            with nc.allow_non_contiguous_dma(reason="bias columns, a few hundred words"):
                sp.dma_start(col_bn1[:, :], t["L0_cond_bn1"].rearrange("(p k) -> p k", k=1)).then_inc(small_in, 16)
                for n, src in (("bsoma", "L0_cond_bsoma"), ("bg", "L0_cond_bg"),
                               ("btemp", "L0_cond_btemp"), ("beta0", "L0_cond_beta")):
                    sp.dma_start(cols[n][:, :], t[src].rearrange("(k p) -> p k", p=P)).then_inc(small_in, 16)
                for d in range(D):
                    sp.dma_start(blend[:, d, :], t["cond_1024"][d, :].rearrange("(k p) -> p k", p=P)).then_inc(small_in, 16)
            load_weight(2)
            load_weight(3)

            def step(i, weights=None):
                j = i - 1
                load_x(i + 1, 0)
                load_x(i + 1, 1)
                load_again(j, 0)
                load_again(j, 1)
                if weights:
                    weights()
                load_x(i + 1, 2)
                load_x(i + 1, 3)
                store_x1(j, 0)
                store_x1(j, 1)
                load_again(j, 2)
                load_again(j, 3)
                store_x1(j, 2)
                store_x1(j, 3)

            load_x(1, 0)
            load_x(1, 1)
            load_weight(4)
            load_x(1, 2)
            load_x(1, 3)
            load_weight(5)
            sp.wait_ge(w_turned, W_BEFORE[5] + W_COUNT[5])
            step(1)
            with sp.Fori(2, NBLK - 1) as i:
                step(i)

            sp.wait_ge(idx_in, 48)
            which = [sp.value_load(idx[0:1, n:n + 1], min_val=0, max_val=m)
                     for n, m in enumerate([31, 31, 9, 9, 7, 7])]

            def cat(b):
                return which[b]

            def lang(b):
                return which[2 + b]

            def subj(b):
                return which[4 + b]

            def cols_of(src, n):
                return src[bass.ds(n, 1), :].rearrange("a (k p) -> p (a k)", p=P)

            with nc.allow_non_contiguous_dma(reason="bias columns, a few hundred words"):
                for b in range(B):
                    sp.dma_start(seq["b1"][:, b, :], cols_of(t["L1_cond_b"], cat(b))).then_inc(lw_in[b], 16)
                    sp.dma_start(seq["lb1"][:, b, 0:1], cols_of(t["L2_cond_b1"], lang(b))).then_inc(lw_in[b], 16)
                    for n, src in (("b2", "L2_cond_b2"), ("gamma2", "L2_cond_gamma"), ("beta2", "L2_cond_beta")):
                        sp.dma_start(seq[n][:, b, :], cols_of(t[src], lang(b))).then_inc(lw_in[b], 16)

            def load_l1(b, half):
                src = t["L1_cond_W"][bass.ds(cat(b), 1)].rearrange("a (k p) o -> p (a k) o", p=P)
                sp.dma_start(l1_raw[b][half], src[:, 2 * half:2 * half + 2, :]).then_inc(l1_in[b], 16)

            def load_l2(b):
                sp.dma_start(l2_raw[b][:, 0, :].rearrange("p (k a) -> p k a", k=NC),
                             t["L2_cond_W1"][bass.ds(lang(b), 1)].rearrange(
                                 "a (k p) h -> p (a k) h", p=P)).then_inc(l2_in[b], 16)
                sp.dma_start(l2_raw[b][:, 1, :], t["L2_cond_W2"][bass.ds(lang(b), 1)].rearrange(
                    "a p o -> (a p) o")).then_inc(l2_in[b], 16)

            def load_l3(b):
                sp.dma_start(l3_raw, t["L3_cond_weight"][bass.ds(subj(b), 1)].rearrange(
                    "a (k p) c -> p (a k) c", p=P)).then_inc(l3_in[b], 16)

            def load_b3(b):
                sp.wait_ge(prods, NBLK * NC * D)
                sp.dma_start(mod[:, b, :], t["L3_cond_bias"][bass.ds(subj(b), 1), :].rearrange(
                    "a c -> (a c)").partition_broadcast(P)).then_inc(lw_in[b], 16)

            def load_y(i, j):
                if isinstance(i, int) and i == 1 and j < 2:
                    sp.wait_ge(tx_done, NBLK * TILES + TILES)
                else:
                    sp.wait_ge(ty_done, i * TILES + (j - 5))
                sp.dma_start(x_tok[:, j % 2, :], tile_of(x1_tiles, i, j)).then_inc(y_in[j % 2], 16)

            def store_out(j, k):
                sp.wait_ge(out_ready, j * TILES + k + 1)
                sp.dma_start(tile_of(out_tiles, j, k), ctx_t[:, k % 2, :]).then_inc(out_done[k % 2], 16)

            def first_weights():
                for done in (ctx_hi, ctx_lo, ctx_carry):
                    sp.wait_ge(done, NBLK * NC)
                load_l1(0, 0)
                sp.wait_ge(prods, NBLK * NC * D)
                load_l1(0, 1)

            step(NBLK - 1, first_weights)
            sp.wait_ge(temp_lo, NBLK * NC)
            sp.wait_ge(temp_hi, NBLK * NC)
            load_l3(0)
            sp.wait_ge(s_prod, NBLK * NC)
            load_l2(0)
            for s in range(2):
                sp.wait_ge(x1_out[s], 16 * 2 * 2)
            load_y(1, 0)
            load_y(1, 1)
            for half in range(2):
                for k in (2 * half, 2 * half + 1):
                    load_again(NBLK - 1, k)
                for k in (2 * half, 2 * half + 1):
                    store_x1(NBLK - 1, k)
            for s in range(2):
                sp.wait_ge(x1_out[s], 16 * 2 * NBLK)
            load_y(1, 2)
            load_y(1, 3)
            sp.wait_ge(l3_turned, NC)
            load_l1(1, 0)
            load_l1(1, 1)
            for done, count in ((l1_hi, NC), (l1_lo, NC), (bias_mm, 1)):
                sp.wait_ge(done, count)
            load_b3(0)
            load_b3(1)

            def second_l3():
                for done, count in ((l1_hi, 2 * NC), (l1_lo, 2 * NC), (bias_mm, 2)):
                    sp.wait_ge(done, count)
                load_l3(1)

            def second_l2():
                sp.wait_ge(l3_turned, 2 * NC)
                load_l2(1)

            def step2(i, prev, nxt):
                if nxt:
                    load_y(i + 1, 0)
                    load_y(i + 1, 1)
                    load_y(i + 1, 2)
                if prev:
                    store_out(i - 1, 0)
                if nxt:
                    load_y(i + 1, 3)
                if prev:
                    store_out(i - 1, 1)
                    store_out(i - 1, 2)
                    store_out(i - 1, 3)

            second_l3()
            step2(1, True, True)
            second_l2()
            with sp.Fori(2, NBLK - 1) as i:
                step2(i, True, True)
            step2(NBLK - 1, True, False)
            step2(NBLK, True, False)
            for s in range(2):
                sp.wait_ge(out_done[s], 16 * 2 * NBLK)

        @block.gpsimd
        def _(pool):
            nc.gpsimd.memset(ident[:, :], 0.0).then_inc(pool_step, 1)
            pool.wait_ge(pool_step, 1)
            nc.gpsimd.affine_select(out=ident[:, :], in_=ident[:, :], compare_op=ALU.not_equal, fill=1.0,
                                    base=0, pattern=[[-1, P]], channel_multiplier=1).then_inc(setup_done, 1)
            with nc.allow_non_contiguous_dma(reason="bias columns, a few hundred words"):
                pool.dma_start(col_wn2[:, :], t["cond_256"].rearrange("d p -> p d")).then_inc(wide_in, 16)
                pool.dma_start(col_bn2[:, :], t["condB_bn2"].partition_broadcast(P)).then_inc(wide_in, 16)
                pool.dma_start(taus[:, 0:1], t["L0_cond_tau_ctx"].partition_broadcast(P)).then_inc(wide_in, 16)
                pool.dma_start(taus[:, 1:1 + D], t["condB_tauraws"].partition_broadcast(P)).then_inc(wide_in, 16)
                pool.dma_start(gamma_row[:, :], t["L0_cond_gamma"].partition_broadcast(P)).then_inc(wide_in, 16)
            for n, src in enumerate(("itok_B_0_30", "itok_B_0_8", "itok_B_0_7")):
                pool.dma_start(idx[0:1, 2 * n:2 * n + 2], t[src].rearrange("(a k) -> a k", a=1)).then_inc(idx_in, 16)
            eps, minus_half, minus_three, half = (const[:, q, :] for q in range(4))
            for c, value in ((eps, EPS), (minus_half, -0.5), (minus_three, -3.0), (half, 0.5)):
                nc.gpsimd.memset(c, value).then_inc(pool_step, 1)
            pool.wait_ge(pool_step, 5)

            def inv_sqrt(tiles, at):
                n = tiles.stop - tiles.start
                v, y, q = newton[:, 0, 0:n], newton[:, 1, 0:n], newton[:, 2, 0:n]
                nc.gpsimd.tensor_tensor(v, mv[:, tiles, 1], eps[:, 0:n], ALU.add).then_inc(pool_step, 1)
                pool.wait_ge(pool_step, at + 1)
                nc.gpsimd.tensor_tensor(y, v, minus_half[:, 0:n], ALU.pow).then_inc(pool_step, 1)
                pool.wait_ge(pool_step, at + 2)
                nc.gpsimd.tensor_tensor(q, y, y, ALU.mult).then_inc(pool_step, 1)
                pool.wait_ge(pool_step, at + 3)
                nc.gpsimd.tensor_tensor(q, q, v, ALU.mult).then_inc(pool_step, 1)
                pool.wait_ge(pool_step, at + 4)
                nc.gpsimd.tensor_tensor(q, q, minus_three[:, 0:n], ALU.add).then_inc(pool_step, 1)
                pool.wait_ge(pool_step, at + 5)
                nc.gpsimd.tensor_tensor(q, q, y, ALU.mult).then_inc(pool_step, 1)
                pool.wait_ge(pool_step, at + 6)
                return q

            def x_lo_part(i, k):
                tok = slice(k * P, (k + 1) * P)
                pool.wait_ge(xcopy, i * TILES + (k + 1))
                if k == 0:
                    pool.wait_ge(z_mm, i * NC)
                nc.gpsimd.tensor_tensor(x_l[:, :, tok], x_t[:, :, tok], x_h[:, :, tok].bitcast(F32),
                                        ALU.subtract).then_inc(xlo, 1)

            def norm_scale(j, k):
                pool.wait_ge(ln_mv, j * TILES + (k + 1))
                corr = inv_sqrt(slice(k, k + 1), j * (TILES * 6) + (5 + k * 6))
                nc.gpsimd.tensor_tensor(rstd[:, k:k + 1], corr, minus_half[:, 0:1], ALU.mult).then_inc(ln_rstd, 1)
                pool.wait_ge(ln_rstd, j * TILES + (k + 1))

            for k in range(TILES):
                x_lo_part(1, k)
            with pool.Fori(1, NBLK - 1) as i:
                norm_scale(i - 1, 0)
                x_lo_part(i + 1, 0)
                norm_scale(i - 1, 1)
                x_lo_part(i + 1, 1)
                norm_scale(i - 1, 2)
                norm_scale(i - 1, 3)
                x_lo_part(i + 1, 2)
                x_lo_part(i + 1, 3)

            def add_eye(chunks, eye):
                for q, chunk in enumerate(chunks):
                    o = slice(q * P, (q + 1) * P)
                    nc.gpsimd.tensor_tensor(chunk[:, o], chunk[:, o], ident[:, :], ALU.add).then_inc(eye, 1)

            def l1_residual(b):
                pool.wait_ge(l1_in[b], 32)
                add_eye([l1_chunk(b, q) for q in range(NC)], l1_eye)

            def l3_residual(b):
                pool.wait_ge(l3_in[b], 16)
                add_eye([l3_raw[:, q, :] for q in range(NC)], l3_eye)

            def linear_lo(b):
                wh, wl = l1_w(b)
                pool.wait_ge(l1_eye, (b + 1) * NC)
                for k in range(NC):
                    pool.wait_ge(l1_hi, b * NC + k + 1)
                    nc.gpsimd.tensor_tensor(wl[:, k, :], l1_chunk(b, k), wh[:, k, :].bitcast(F32),
                                            ALU.subtract).then_inc(l1_lo, 1)

            def adapter_lo(b):
                pool.wait_ge(l2_hi, b * 2 + 1)
                wh, wl = w1_w(b)
                nc.gpsimd.tensor_tensor(wl, l2_raw[b][:, 0, :].rearrange("p (k a) -> p k a", k=NC),
                                        wh.bitcast(F32), ALU.subtract).then_inc(l2_lo, 1)
                pool.wait_ge(l2_hi, b * 2 + 2)
                wh, wl = w2_w(b)
                nc.gpsimd.tensor_tensor(wl, l2_raw[b][:, 1, :], wh.bitcast(F32), ALU.subtract).then_inc(l2_lo, 1)

            second = 5 + NBLK * TILES * 6

            def norm2_scale(j):
                at = j * 8 + second
                pool.wait_ge(ln2_mv, j * TILES + TILES)
                corr = inv_sqrt(slice(0, TILES), at)
                nc.gpsimd.tensor_tensor(rstd[:, :], corr, minus_half, ALU.mult).then_inc(pool_step, 1)
                nc.gpsimd.tensor_tensor(nbias[:, :], corr, mv[:, :, 0], ALU.mult).then_inc(pool_step, 1)
                pool.wait_ge(pool_step, at + 8)
                nc.gpsimd.tensor_tensor(nbias[:, :], nbias[:, :], half, ALU.mult).then_inc(ln2_rstd, 1)
                pool.wait_ge(ln2_rstd, j + 1)

            l1_residual(0)
            norm_scale(NBLK - 2, 0)
            norm_scale(NBLK - 2, 1)
            linear_lo(0)
            norm_scale(NBLK - 2, 2)
            norm_scale(NBLK - 2, 3)
            x_lo_part(NBLK, 0)
            x_lo_part(NBLK, 1)
            l3_residual(0)
            adapter_lo(0)
            for k in range(TILES):
                norm_scale(NBLK - 1, k)
            l1_residual(1)
            norm2_scale(0)
            linear_lo(1)
            l3_residual(1)
            with pool.Fori(1, PER_SEQ) as j:
                norm2_scale(j)
            adapter_lo(1)
            with pool.Fori(PER_SEQ, NBLK) as j:
                norm2_scale(j)

        @block.tensor
        def _(pe):
            def product(acc, pairs, start=True, stop=True):
                n = len(pairs)
                for q, (ah, al, bh, bl) in enumerate(pairs):
                    nc.tensor.matmul(acc, ah, bh, start=start and q == 0, stop=False)
                    nc.tensor.matmul(acc, ah, bl, start=False, stop=False)
                    last = nc.tensor.matmul(acc, al, bh, start=False, stop=stop and q == n - 1)
                return last

            def turn(acc, sources, stop=True):
                for q, src in enumerate(sources):
                    last = nc.tensor.matmul(acc[:, q * P:(q + 1) * P], src, ident[:, :], is_transpose=True,
                                            start=(q == 0), stop=stop and (q == 3), skip_group_check=True)
                return last

            def out_cols(m):
                return slice(m * P, (m + 1) * P)

            def prepare(n, chunks):
                pe.wait_ge(weight_in[n], 16)
                raw = L0W[n][2]
                for k in chunks:
                    c = W_BEFORE[n] + k
                    if c >= 4:
                        pe.wait_ge(w_hi, c - 3)
                        pe.wait_ge(w_lo, c - 3)
                    pieces = ([raw[:, 0, out_cols(q)] for q in range(4)] if n == 0 else
                              [raw[:, q, out_cols(k)] for q in range(4)])
                    turn(pm[c % 4], pieces).then_inc(w_turned, 1)

            def ready(n):
                pe.wait_ge(w_hi, W_BEFORE[n] + W_COUNT[n])
                pe.wait_ge(w_lo, W_BEFORE[n] + W_COUNT[n])

            def turn_x(i, k):
                if isinstance(i, int) and i == 0:
                    pe.wait_ge(x_in[k] if k < 2 else first_in[k - 2], 16)
                else:
                    pe.wait_ge(x_in[k % 2], (i * 2 + k // 2) * 16)
                if k < 2:
                    after(pe, mod_t, i * D + (k + 1 - D))
                if k >= 2:
                    pe.wait_ge(xcopy, i * TILES + (k - 1))
                src = x_first(k) if isinstance(i, int) and i == 0 else x_tok[:, k % 2, :]
                turn(pt[k % 2], [src[:, out_cols(c)] for c in range(NC)]).then_inc(tx_done, 1)

            def h1_product(i):
                pe.wait_ge(xcopy, i * TILES + TILES)
                pe.wait_ge(xlo, i * TILES + TILES)
                product(pt[0][:, :], [(wn1_h[:, c, :], wn1_l[:, c, :], x_h[:, c, :], x_l[:, c, :])
                                      for c in range(NC)]).then_inc(h1_mm, 1)

            def soma_product(i, after_chunk=None):
                for m in range(NC):
                    if m >= 2:
                        pe.wait_ge(soma_g, i * NC + (m - 1))
                    else:
                        after(pe, z_t, i * NC + (m - 1))
                    o = out_cols(m)
                    product(pc[m % 2][:, :], [(ws_h[:, c, o], ws_l[:, c, o], x_h[:, c, :], x_l[:, c, :])
                                              for c in range(NC)]).then_inc(soma_mm, 1)
                    if after_chunk:
                        after_chunk(m)

            def mod_product(i):
                pe.wait_ge(h1_hi, i + 1)
                pe.wait_ge(h1_lo, i + 1)
                for d in range(D):
                    product(pt[d][:, :], [(wn2_h[:, d, :], wn2_l[:, d, :], h_h[:, :], h_l[:, :])]).then_inc(mod_mm, 1)

            def z_product(i, first=False):
                for m in range(NC):
                    if m < 2:
                        pe.wait_ge(soma_g, i * NC + (3 + m))
                    else:
                        pe.wait_ge(z_t, i * NC + (m - 1))
                    o = out_cols(m)
                    product(pc[m % 2][:, :],
                            [(wg_h[:, c, o], wg_l[:, c, o], x_h[:, c, :], x_l[:, c, :]) for c in range(NC)],
                            stop=False)
                    if first and m == 0:
                        ready(3)
                    if m == 0:
                        pe.wait_ge(ctx_hi, i * NC + NC)
                        pe.wait_ge(ctx_lo, i * NC + NC)
                    product(pc[m % 2][:, :],
                            [(wg_h[:, NC + c, o], wg_l[:, NC + c, o], c_h[:, c, :], c_l[:, c, :])
                             for c in range(NC)], start=False).then_inc(z_mm, 1)
                    if first:
                        prepare(4, W4_AFTER[m])

            def temp_product(j, halves=(0, 1)):
                def part(c, m):
                    if c == 0:
                        after(pe, ln_centred, j * TILES + (m - 3))
                    o = out_cols(m)
                    nc.tensor.matmul(pm[m][:, :], wt_h[:, c, o], t_h[:, c, :], start=(c == 0), stop=False)
                    nc.tensor.matmul(pm[m][:, :], wt_h[:, c, o], t_l[:, c, :], start=False, stop=False)
                    last = nc.tensor.matmul(pm[m][:, :], wt_l[:, c, o], t_h[:, c, :], start=False,
                                            stop=(c == NC - 1))
                    if c == NC - 1:
                        last.then_inc(wt_mm, 1)

                for c in (0, 1) if 0 in halves else ():
                    pe.wait_ge(temp_hi, j * NC + (c + 1))
                    pe.wait_ge(temp_lo, j * NC + (c + 1))
                    for m in range(NC - 1):
                        part(c, m)
                for c in (0, 1) if 0 in halves else ():
                    part(c, NC - 1)
                for c in (2, 3) if 1 in halves else ():
                    pe.wait_ge(temp_hi, j * NC + (c + 1))
                    pe.wait_ge(temp_lo, j * NC + (c + 1))
                    for m in range(NC):
                        part(c, m)

            def out_product(j, k):
                if k == 0:
                    pe.wait_ge(gate_t, j * NC + NC)
                    pe.wait_ge(s_hi, j * NC + NC)
                    pe.wait_ge(s_lo, j * NC + NC)
                tok = out_cols(k)
                product(pm[k][:, :], [(s_h[:, c, tok], s_l[:, c, tok], wo_h[:, c, :], wo_l[:, c, :])
                                      for c in range(NC)]).then_inc(wo_mm, 1)

            def step(i):
                temp_product(i - 1)
                h1_product(i)
                soma_product(i)
                mod_product(i)
                z_product(i)
                for k in range(TILES):
                    out_product(i - 1, k)
                    turn_x(i + 1, k)

            pe.wait_ge(setup_done, 1)
            for k in range(TILES):
                turn_x(0, k)
            prepare(0, [0])
            prepare(1, range(NC))
            ready(0)
            h1_product(0)
            ready(1)
            soma_product(0, lambda m: prepare(2 + m // 2, [m % 2 * 2, m % 2 * 2 + 1]))
            pe.wait_ge(consts_v, 1 + D)
            mod_product(0)
            ready(2)
            z_product(0, first=True)
            turn_x(1, 0)
            turn_x(1, 1)
            ready(4)
            temp_product(0, [0])
            turn_x(1, 2)
            turn_x(1, 3)
            temp_product(0, [1])
            h1_product(1)
            soma_product(1)
            pe.wait_ge(gate_t, NC)
            prepare(5, range(NC))
            mod_product(1)
            z_product(1)
            ready(5)
            for k in range(TILES):
                out_product(0, k)
                turn_x(2, k)
            with pe.Fori(2, NBLK) as i:
                step(i)

            def beta_product(b):
                pe.wait_ge(l1_eye, (b + 1) * NC)
                if b == 0:
                    pe.wait_ge(z_t, NBLK * NC)
                else:
                    pe.wait_ge(x2_hi, NC)
                    pe.wait_ge(x2_lo, NC)
                for m in range(NC):
                    for c in range(NC):
                        last = nc.tensor.matmul(pc[1][:, 2 * m:2 * m + 1], l1_chunk(b, c)[:, out_cols(m)],
                                                cols["beta0"][:, c:c + 1], start=(c == 0), stop=(c == NC - 1))
                last.then_inc(bias_mm, 1)

            def turn_l3(b, k, bank):
                pe.wait_ge(l3_eye, (b + 1) * NC)
                if k >= 2:
                    pe.wait_ge(l3_hi, b * NC + k - 1)
                    pe.wait_ge(l3_lo, b * NC + k - 1)
                turn(bank, [l3_raw[:, q, out_cols(k)] for q in range(4)]).then_inc(l3_turned, 1)

            def turn_y(i, k, shared=False):
                if k < 2 and shared:
                    pe.wait_ge(x3_sum, i * NC + (k - 5))
                pe.wait_ge(y_in[k % 2], (i * 2 + (k // 2 - 1)) * 16)
                if k >= 2:
                    pe.wait_ge(y_hi, i * TILES + (k - 5))
                    pe.wait_ge(y_lo, i * TILES + (k - 5))
                turn(pt[k % 2], [x_tok[:, k % 2, out_cols(c)] for c in range(NC)]).then_inc(ty_done, 1)

            def l1_product(i, b, m):
                if m == 0 and isinstance(i, int) and i == 0:
                    pe.wait_ge(xcopy, (NBLK + 1) * TILES)
                    pe.wait_ge(xlo, (NBLK + 1) * TILES)
                elif m == 0:
                    pe.wait_ge(y_hi, i * TILES)
                    pe.wait_ge(y_lo, i * TILES)
                    after(pe, relu_done, i)
                if m >= 2:
                    pe.wait_ge(x2_hi, i * NC + (m - 1))
                    pe.wait_ge(x2_lo, i * NC + (m - 1))
                o = out_cols(m)
                wh, wl = l1_w(b)
                product(pc[m % 2][:, :], [(wh[:, c, o], wl[:, c, o], x_h[:, c, :], x_l[:, c, :])
                                          for c in range(NC)]).then_inc(l1_mm, 1)

            def w1_product(i, b):
                if isinstance(i, int):
                    pe.wait_ge(l2_hi, b * 2 + 2)
                    pe.wait_ge(l2_lo, b * 2 + 2)
                pe.wait_ge(x2_hi, i * NC + NC)
                pe.wait_ge(x2_lo, i * NC + NC)
                wh, wl = w1_w(b)
                product(pc[0][:, :], [(wh[:, c, :], wl[:, c, :], c_h[:, c, :], c_l[:, c, :])
                                      for c in range(NC)]).then_inc(w1_mm, 1)

            def xx_product(i, b, k):
                if k == 0:
                    pe.wait_ge(hid_hi, i + 1)
                    pe.wait_ge(hid_lo, i + 1)
                if k < 3:
                    after(pe, out_ready, i * TILES + (k - 3))
                tok = out_cols(k)
                turn(pm[k], [x_t[:, c, tok] for c in range(NC)], stop=False)
                wh, wl = w2_w(b)
                nc.tensor.matmul(pm[k][:, :], h_h[:, tok], wh, start=False, stop=False, skip_group_check=True)
                nc.tensor.matmul(pm[k][:, :], h_l[:, tok], wh, start=False, stop=False, skip_group_check=True)
                nc.tensor.matmul(pm[k][:, :], h_h[:, tok], wl, start=False, stop=True,
                                 skip_group_check=True).then_inc(xx_mm, 1)

            def turn_n2(j, chunks):
                for c in chunks:
                    if c == 0:
                        pe.wait_ge(n2_act, j * 2 + 2)
                        pe.wait_ge(n2_dve, j * 2 + 2)
                        after(pe, out_ready, j * TILES)
                    if c >= 2:
                        pe.wait_ge(x3_sum, j * NC + (c - 1))
                    turn(pt[c % 2], [stage_a[:, k, out_cols(c)] for k in range(TILES)]).then_inc(tn_done, 1)

            def l3_product(j, b, k):
                if k == 0:
                    pe.wait_ge(x3_hi, j * NC + NC)
                    pe.wait_ge(x3_lo, j * NC + NC)
                if k == 3 and isinstance(j, int) and j >= NBLK - 2:
                    pe.wait_ge(x3_sum, (j + 1) * NC - 1)
                elif k == 3:
                    pe.wait_ge(y_hi, j * TILES + 7)
                    pe.wait_ge(y_lo, j * TILES + 7)
                tok = out_cols(k)
                wh, wl = l3_w(b)
                bank = pm[k] if k < 3 else pt[0]
                product(bank[:, :], [(t_h[:, c, tok], t_l[:, c, tok], wh[:, c, :], wl[:, c, :])
                                     for c in range(NC)]).then_inc(l3_mm, 1)

            def step2(i, b, bp, nxt, weights=False):
                l1_product(i, b, 0)
                turn_n2(i - 1, (0, 1))
                l1_product(i, b, 1)
                turn_n2(i - 1, (2, 3))
                l1_product(i, b, 2)
                l1_product(i, b, 3)
                if nxt:
                    turn_y(i + 1, 0, True)
                    turn_y(i + 1, 1, True)
                l3_product(i - 1, bp, 0)
                w1_product(i, b)
                if nxt:
                    turn_y(i + 1, 2)
                l3_product(i - 1, bp, 1)
                if nxt:
                    turn_y(i + 1, 3)
                l3_product(i - 1, bp, 2)
                for k in range(TILES):
                    xx_product(i, b, k)
                if weights:
                    pe.wait_ge(y_hi, i * TILES + TILES)
                    pe.wait_ge(y_lo, i * TILES + TILES)
                    turn_l3(1, 0, pt[1])
                    turn_l3(1, 1, pc[1])
                if nxt:
                    l3_product(i - 1, bp, 3)
                if weights:
                    turn_l3(1, 2, pt[1])
                    turn_l3(1, 3, pc[1])

            beta_product(0)
            temp_product(NBLK - 1)
            pe.wait_ge(l1_hi, NC)
            pe.wait_ge(l1_lo, NC)
            l1_product(0, 0, 0)
            pe.wait_ge(bias_done, 1)
            l1_product(0, 0, 1)
            for k in range(TILES):
                out_product(NBLK - 1, k)
            l1_product(0, 0, 2)
            l1_product(0, 0, 3)
            turn_l3(0, 0, pt[0])
            turn_l3(0, 1, pt[1])
            w1_product(0, 0)
            turn_l3(0, 2, pt[0])
            turn_l3(0, 3, pt[1])
            pe.wait_ge(l3_hi, NC)
            pe.wait_ge(l3_lo, NC)
            for k in range(TILES):
                turn_y(1, k)
            pe.wait_ge(ln_centred, NBLK * TILES)
            for k in range(TILES):
                xx_product(0, 0, k)
            beta_product(1)
            pe.wait_ge(bias_done, 2)
            step2(1, 0, 0, True, weights=True)
            pe.wait_ge(l3_hi, 2 * NC)
            pe.wait_ge(l3_lo, 2 * NC)
            with pe.Fori(2, PER_SEQ) as i:
                step2(i, 0, 0, True)
            pe.wait_ge(l1_hi, 2 * NC)
            pe.wait_ge(l1_lo, 2 * NC)
            step2(PER_SEQ, 1, 0, True)
            with pe.Fori(PER_SEQ + 1, NBLK - 1) as i:
                step2(i, 1, 1, True)
            step2(NBLK - 1, 1, 1, False)
            l3_product(NBLK - 2, 1, 3)
            turn_n2(NBLK - 1, range(NC))
            for k in range(TILES):
                l3_product(NBLK - 1, 1, k)

        @block.scalar
        def _(act):
            def prepare(n, chunks):
                for k in chunks:
                    c = W_BEFORE[n] + k
                    hi, _ = w_dest(n, k)
                    act.wait_ge(w_turned, c + 1)
                    nc.scalar.activation(hi, pm[c % 4][:, :], ACT.Identity, scale=W_SCALE[n]).then_inc(w_hi, 1)

            def copy_x(i, k):
                tok = slice(k * P, (k + 1) * P)
                act.wait_ge(tx_done, i * TILES + (k + 1))
                if k == 0:
                    after(act, z_mm, i * NC)
                    after(act, gated, i * NC)
                src = pt[k % 2][:, :].rearrange("p (c q) -> p c q", c=NC)
                nc.scalar.activation(x_h[:, :, tok], src, ACT.Identity)
                nc.scalar.activation(x_t[:, :, tok], src, ACT.Identity).then_inc(xcopy, 1)

            def context_hi(i, c):
                if c == 0:
                    after(act, z_mm, i * NC)
                act.wait_ge(ctx_scan, i * NC + (c + 1))
                nc.scalar.activation(c_h[:, c, :], ctx_t[:, c % 2, :], ACT.Identity).then_inc(ctx_hi, 1)

            def hidden(i):
                act.wait_ge(h1_mm, i + 1)
                after(act, h1_lo, i)
                nc.scalar.activation(h1[:, :], pt[0][:, :], ACT.Gelu, bias=col_bn1[:, 0:1]).then_inc(h1_gelu, 1)
                act.wait_ge(h1_gelu, i + 1)
                after(act, mod_mm, i * D)
                nc.scalar.activation(h_h[:, :], h1[:, :], ACT.Identity).then_inc(h1_hi, 1)

            def gate_tanh(j, m):
                act.wait_ge(wt_mm, j * NC + (m + 1))
                after(act, s_lo, j * NC + (m - 1))
                nc.scalar.activation(gate[:, m % 2, :], pm[m][:, :], ACT.Tanh, bias=cols["btemp"][:, m:m + 1],
                                     scale=0.5).then_inc(gate_t, 1)

            def gated_soma_hi(j, m):
                after(act, wo_mm, j * TILES)
                act.wait_ge(s_prod, j * NC + (m + 1))
                nc.scalar.activation(s_h[:, m, :], gate[:, m % 2, :], ACT.Identity).then_inc(s_hi, 1)

            def gates(j):
                gate_tanh(j, 0)
                gate_tanh(j, 1)
                gated_soma_hi(j, 0)
                gate_tanh(j, 2)
                gated_soma_hi(j, 1)
                gate_tanh(j, 3)
                gated_soma_hi(j, 2)
                gated_soma_hi(j, 3)

            def soma_gelu(i, m):
                act.wait_ge(soma_mm, i * NC + (m + 1))
                after(act, s_prod, i * NC + (m - 3))
                nc.scalar.activation(soma[:, m, :], pc[m % 2][:, :], ACT.Gelu,
                                     bias=cols["bsoma"][:, m:m + 1]).then_inc(soma_g, 1)

            def mod_tanh(i):
                for d in range(D):
                    act.wait_ge(mod_mm, i * D + (d + 1))
                    after(act, prods, i * (D * NC))
                    nc.scalar.activation(mod[:, d, :], pt[d][:, :], ACT.Tanh, bias=col_bn2[:, d:d + 1],
                                         scale=0.5).then_inc(mod_t, 1)

            def z_tanh(i, m):
                act.wait_ge(z_mm, i * NC + (m + 1))
                after(act, temp_lo, i * NC + (m - 1))
                nc.scalar.activation(tr1[:, m % 2, :], pc[m % 2][:, :], ACT.Tanh, bias=cols["bg"][:, m:m + 1],
                                     scale=0.5).then_inc(z_t, 1)

            def weigh(i, m):
                act.wait_ge(traces, (i * NC + (m + 1)) * D)
                act.wait_ge(tr_carry, (i * NC + (m + 1)) * D)
                nc.scalar.activation(tr0[:, m % 2, :], tr0[:, m % 2, :], ACT.Identity,
                                     scale=w_blend[:, 0, m:m + 1]).then_inc(weighed, 1)

            def temporal_hi(i, m):
                after(act, wt_mm, i * NC)
                act.wait_ge(blended, i * NC + (m + 1))
                nc.scalar.activation(t_h[:, m, :], tr0[:, m % 2, :], ACT.Identity).then_inc(temp_hi, 1)

            def trace_part(i, first=False):
                z_tanh(i, 0)
                if first:
                    prepare(4, W4_AFTER[0])
                for m in range(NC - 1):
                    z_tanh(i, m + 1)
                    if first:
                        prepare(4, W4_AFTER[m + 1])
                    weigh(i, m)
                    temporal_hi(i, m)

            def trace_end(i):
                copy_x(i + 1, 0)
                weigh(i, 3)
                copy_x(i + 1, 1)
                temporal_hi(i, 3)
                copy_x(i + 1, 2)
                copy_x(i + 1, 3)

            def step(i, first=False):
                gates(i - 1)
                hidden(i)
                soma_gelu(i, 0)
                context_hi(i, 0)
                soma_gelu(i, 1)
                context_hi(i, 1)
                context_hi(i, 2)
                soma_gelu(i, 2)
                context_hi(i, 3)
                soma_gelu(i, 3)
                if first:
                    prepare(5, range(NC))
                mod_tanh(i)
                trace_part(i)
                trace_end(i)

            for k in range(TILES):
                copy_x(0, k)
            prepare(0, [0])
            prepare(1, range(NC))
            act.wait_ge(consts_v, 1)
            nc.scalar.activation(alpha[:, :], taus[:, :], ACT.Tanh, scale=-0.5).then_inc(consts_a, 1)
            nc.scalar.activation(w_blend[:, :, :], dblend[:, :, :], ACT.Tanh, scale=0.5).then_inc(consts_a, 1)
            hidden(0)
            soma_gelu(0, 0)
            prepare(2, [0, 1])
            context_hi(0, 0)
            context_hi(0, 1)
            soma_gelu(0, 1)
            prepare(2, [2, 3])
            context_hi(0, 2)
            context_hi(0, 3)
            soma_gelu(0, 2)
            prepare(3, [0, 1])
            soma_gelu(0, 3)
            prepare(3, [2, 3])
            mod_tanh(0)
            trace_part(0, first=True)
            trace_end(0)
            step(1, first=True)
            with act.Fori(2, NBLK) as i:
                step(i)

            def linear_hi(b):
                act.wait_ge(l1_eye, (b + 1) * NC)
                for k in range(NC):
                    nc.scalar.activation(l1_w(b)[0][:, k, :], l1_chunk(b, k), ACT.Identity).then_inc(l1_hi, 1)

            def adapter_hi(b):
                act.wait_ge(l2_in[b], 32)
                nc.scalar.activation(w1_w(b)[0], l2_raw[b][:, 0, :].rearrange("p (k a) -> p k a", k=NC),
                                     ACT.Identity).then_inc(l2_hi, 1)
                nc.scalar.activation(w2_w(b)[0], l2_raw[b][:, 1, :], ACT.Identity).then_inc(l2_hi, 1)

            def subject_hi(b, k, bank):
                if k == 0:
                    act.wait_ge(wt_mm if b == 0 else wo_mm, NBLK * NC)
                act.wait_ge(l3_turned, b * NC + k + 1)
                nc.scalar.activation(l3_w(b)[0][:, k, :], bank[:, :], ACT.Identity).then_inc(l3_hi, 1)

            def copy_y(i, k):
                tok = slice(k * P, (k + 1) * P)
                act.wait_ge(ty_done, i * TILES + (k - 3))
                if k == 0:
                    after(act, l1_mm, i * NC)
                nc.scalar.activation(x_h[:, :, tok], pt[k % 2][:, :].rearrange("p (c q) -> p c q", c=NC),
                                     ACT.Identity).then_inc(y_hi, 1)

            def x2_parts(i, b, m):
                act.wait_ge(l1_mm, i * NC + (m + 1))
                after(act, w1_mm, i)
                nc.scalar.activation(c_h[:, m, :], pc[m % 2][:, :], ACT.Identity, bias=seq["b1"][:, b, m:m + 1])
                after(act, xx_mm, i * TILES)
                after(act, x2_all, i * NC + (m - 3))
                nc.scalar.activation(x_t[:, m, :], pc[m % 2][:, :], ACT.Identity,
                                     bias=seq["b1b2"][:, b, m:m + 1]).then_inc(x2_hi, 1)

            def x2_beta(i, b, m):
                after(act, x3_sum, i * NC + (m - 3))
                act.wait_ge(x2_hi, i * NC + (m + 1))
                nc.scalar.activation(soma[:, m, :], x_t[:, m, :], ACT.Identity,
                                     bias=seq["beta_b2"][:, b, m:m + 1]).then_inc(x2_all, 1)

            def x3_hi_part(j, m):
                after(act, l3_mm, j * TILES)
                act.wait_ge(x3_sum, j * NC + (m + 1))
                nc.scalar.activation(t_h[:, m, :], gate[:, m % 2, :], ACT.Identity).then_inc(x3_hi, 1)

            def relu_part(i, b):
                act.wait_ge(w1_mm, i + 1)
                after(act, hid_lo, i)
                nc.scalar.activation(h1[:, :], pc[0][:, :], ACT.Relu, bias=seq["lb1"][:, b, 0:1]).then_inc(relu_done, 1)
                act.wait_ge(relu_done, i + 1)
                after(act, xx_mm, i * TILES)
                nc.scalar.activation(h_h[:, :], h1[:, :], ACT.Identity).then_inc(hid_hi, 1)

            def normalise(i, k):
                act.wait_ge(ln2_rstd, i + 1)
                after(act, tn_done, i * NC)
                nc.scalar.activation(stage_a[:, k, :], pm[k][:, :], ACT.Identity, bias=nbias[:, k:k + 1],
                                     scale=rstd[:, k:k + 1]).then_inc(n2_act, 1)

            def step2(i, b, nxt, weights=False, adapter=False):
                x2_parts(i, b, 0)
                x3_hi_part(i - 1, 0)
                x3_hi_part(i - 1, 1)
                x2_parts(i, b, 1)
                x3_hi_part(i - 1, 2)
                x3_hi_part(i - 1, 3)
                x2_parts(i, b, 2)
                x2_beta(i, b, 0)
                x2_parts(i, b, 3)
                if adapter:
                    adapter_hi(1)
                if nxt:
                    copy_y(i + 1, 0)
                    copy_y(i + 1, 1)
                x2_beta(i, b, 1)
                relu_part(i, b)
                if nxt:
                    copy_y(i + 1, 2)
                x2_beta(i, b, 2)
                if nxt:
                    copy_y(i + 1, 3)
                x2_beta(i, b, 3)
                if weights:
                    subject_hi(1, 0, pt[1])
                    subject_hi(1, 1, pc[1])
                normalise(i, 0)
                normalise(i, 1)
                if weights:
                    subject_hi(1, 2, pt[1])
                    subject_hi(1, 3, pc[1])

            linear_hi(0)
            gates(NBLK - 1)
            act.wait_ge(bias_done, 1)
            x2_parts(0, 0, 0)
            x2_parts(0, 0, 1)
            adapter_hi(0)
            x2_parts(0, 0, 2)
            x2_parts(0, 0, 3)
            subject_hi(0, 0, pt[0])
            subject_hi(0, 1, pt[1])
            relu_part(0, 0)
            subject_hi(0, 2, pt[0])
            subject_hi(0, 3, pt[1])
            for k in range(TILES):
                copy_y(1, k)
            linear_hi(1)
            act.wait_ge(l2_lo, 2)
            for m in range(NC):
                x2_beta(0, 0, m)
            act.wait_ge(x1_out[0], 16 * 2 * NBLK)
            act.wait_ge(x1_out[1], 16 * 2 * NBLK)
            normalise(0, 0)
            normalise(0, 1)
            step2(1, 0, True, weights=True)
            act.wait_ge(bias_done, 2)
            with act.Fori(2, PER_SEQ) as i:
                step2(i, 0, True)
            step2(PER_SEQ, 1, True, adapter=True)
            with act.Fori(PER_SEQ + 1, NBLK - 1) as i:
                step2(i, 1, True)
            step2(NBLK - 1, 1, False)
            for m in range(NC):
                x3_hi_part(NBLK - 1, m)

        @block.vector
        def _(dve):
            def f32(ap):
                return ap.bitcast(F32)

            def prepare(n, chunks):
                for k in chunks:
                    c = W_BEFORE[n] + k
                    hi, lo = w_dest(n, k)
                    dve.wait_ge(w_hi, c + 1)
                    nc.vector.scalar_tensor_tensor(lo, pm[c % 4][:, :], W_SCALE[n], f32(hi), ALU.mult,
                                                   ALU.subtract).then_inc(w_lo, 1)

            def x_lo_part(i, k):
                tok = slice(k * P, (k + 1) * P)
                dve.wait_ge(xcopy, i * TILES + k + 1)
                after(dve, z_mm, i * NC)
                nc.vector.tensor_tensor(x_l[:, :, tok], x_t[:, :, tok], f32(x_h[:, :, tok]),
                                        ALU.subtract).then_inc(xlo, 1)

            def scan_context(i, c):
                after(dve, ctx_hi, i * NC + (c - 1))
                after(dve, ctx_lo, i * NC + (c - 1))
                after(dve, ctx_carry, i * NC + (c - 3))
                nc.vector.tensor_tensor_scan(ctx_t[:, c % 2, :], alpha[:, 0:1].to_broadcast([P, BLK]), x_t[:, c, :],
                                             carry[:, 0, c:c + 1], ALU.mult, ALU.add).then_inc(ctx_scan, 1)

            def carry_context(i, c):
                dve.wait_ge(ctx_scan, i * NC + (c + 1))
                nc.vector.tensor_scalar(carry[:, 0, c:c + 1], ctx_t[:, c % 2, BLK - 1:BLK],
                                        keep[:, bass.ds(i + 1, 1)], None, ALU.mult).then_inc(ctx_carry, 1)

            def split_context(i, c):
                dve.wait_ge(ctx_hi, i * NC + (c + 1))
                nc.vector.tensor_tensor(c_l[:, c, :], ctx_t[:, c % 2, :], f32(c_h[:, c, :]),
                                        ALU.subtract).then_inc(ctx_lo, 1)

            def context(i, hidden=True):
                dve.wait_ge(xcopy, i * TILES + TILES)
                after(dve, z_mm, i * NC)
                scan_context(i, 0)
                scan_context(i, 1)
                carry_context(i, 0)
                split_context(i, 0)
                scan_context(i, 2)
                carry_context(i, 1)
                split_context(i, 1)
                if hidden:
                    hidden_lo(i)
                scan_context(i, 3)
                carry_context(i, 2)
                split_context(i, 2)
                carry_context(i, 3)
                split_context(i, 3)

            def hidden_lo(i):
                dve.wait_ge(h1_hi, i + 1)
                after(dve, mod_mm, i * D)
                nc.vector.tensor_tensor(h_l[:, :], h1[:, :], f32(h_h[:, :]), ALU.subtract).then_inc(h1_lo, 1)

            def gate_soma(j, m):
                dve.wait_ge(gate_t, j * NC + (m + 1))
                dve.wait_ge(soma_g, j * NC + (m + 1))
                nc.vector.scalar_tensor_tensor(gate[:, m % 2, :], gate[:, m % 2, :], 1.0, soma[:, m, :],
                                               ALU.add, ALU.mult).then_inc(s_prod, 1)

            def gated_soma_lo(j, m):
                after(dve, wo_mm, j * TILES)
                dve.wait_ge(s_hi, j * NC + (m + 1))
                nc.vector.tensor_tensor(s_l[:, m, :], gate[:, m % 2, :], f32(s_h[:, m, :]),
                                        ALU.subtract).then_inc(s_lo, 1)

            def gates(j):
                gate_soma(j, 0)
                gate_soma(j, 1)
                gated_soma_lo(j, 0)
                gate_soma(j, 2)
                gated_soma_lo(j, 1)
                gate_soma(j, 3)
                gated_soma_lo(j, 2)
                gated_soma_lo(j, 3)

            def gate_x(i, m):
                dve.wait_ge(z_t, i * NC + (m + 1))
                nc.vector.scalar_tensor_tensor(tr1[:, m % 2, :], tr1[:, m % 2, :], 1.0, x_t[:, m, :],
                                               ALU.add, ALU.mult).then_inc(gated, 1)

            def modulate(i, m):
                dve.wait_ge(gated, i * NC + (m + 1))
                dve.wait_ge(mod_t, i * D + D)
                nc.vector.scalar_tensor_tensor(tr0[:, m % 2, :], mod[:, 0, :], 2.0, tr1[:, m % 2, :],
                                               ALU.add, ALU.mult).then_inc(prods, 1)
                nc.vector.scalar_tensor_tensor(tr1[:, m % 2, :], mod[:, 1, :], 2.0, tr1[:, m % 2, :],
                                               ALU.add, ALU.mult).then_inc(prods, 1)

            def scan_traces(i, m):
                after(dve, tr_carry, (i * NC + (m - 3)) * D)
                for d, tr in enumerate((tr0, tr1)):
                    dve.wait_ge(prods, i * (D * NC) + (m * D + d + 1))
                    nc.vector.tensor_tensor_scan(tr[:, m % 2, :], alpha[:, 1 + d:2 + d].to_broadcast([P, BLK]),
                                                 tr[:, m % 2, :], carry[:, 1 + d, m:m + 1], ALU.mult,
                                                 ALU.add).then_inc(traces, 1)
                for d, tr in enumerate((tr0, tr1)):
                    dve.wait_ge(traces, i * (D * NC) + (m * D + d + 1))
                    nc.vector.tensor_scalar(carry[:, 1 + d, m:m + 1], tr[:, m % 2, BLK - 1:BLK],
                                            keep[:, bass.ds(i + 1, 1)], None, ALU.mult).then_inc(tr_carry, 1)

            def blend_traces(i, m):
                dve.wait_ge(weighed, i * NC + (m + 1))
                nc.vector.scalar_tensor_tensor(tr0[:, m % 2, :], tr1[:, m % 2, :], w_blend[:, 1, m:m + 1],
                                               tr0[:, m % 2, :], ALU.mult, ALU.add).then_inc(blended, 1)

            def temporal_lo(i, m):
                after(dve, wt_mm, i * NC)
                dve.wait_ge(temp_hi, i * NC + (m + 1))
                nc.vector.tensor_tensor(t_l[:, m, :], tr0[:, m % 2, :], f32(t_h[:, m, :]),
                                        ALU.subtract).then_inc(temp_lo, 1)

            def trace_part(i, first=False):
                gate_x(i, 0)
                modulate(i, 0)
                scan_traces(i, 0)
                if first:
                    prepare(4, W4_AFTER[0])
                gate_x(i, 1)
                blend_traces(i, 0)
                modulate(i, 1)
                temporal_lo(i, 0)
                scan_traces(i, 1)
                if first:
                    prepare(4, W4_AFTER[1])
                gate_x(i, 2)
                blend_traces(i, 1)
                modulate(i, 2)
                temporal_lo(i, 1)
                scan_traces(i, 2)
                gate_x(i, 3)
                if first:
                    prepare(4, W4_AFTER[2])
                blend_traces(i, 2)
                modulate(i, 3)
                temporal_lo(i, 2)
                scan_traces(i, 3)

            def norm_stats(j, k):
                dve.wait_ge(wo_mm, j * TILES + (k + 1))
                after(dve, ln_mv, j * TILES + (k - 3))
                nc.vector.bn_stats(stats[:, k, :], pm[k][:, :]).then_inc(ln_stats, 1)
                dve.wait_ge(ln_stats, j * TILES + (k + 1))
                dve.sem_inc(stats_seen, 1)
                nc.vector.bn_aggr(mv[:, k, :], stats[:, k, :]).then_inc(ln_mv, 1)
                dve.wait_ge(ln_mv, j * TILES + (k + 1))
                after(dve, x1_ready, j * TILES + (k - 1))
                nc.vector.scalar_tensor_tensor(normed[:, k % 2, :], pm[k][:, :], mv[:, k, 0:1], gamma_row[:, :],
                                               ALU.subtract, ALU.mult).then_inc(ln_centred, 1)

            def norm_sum(j, k):
                dve.wait_ge(ln_centred, j * TILES + (k + 1))
                dve.wait_ge(ln_rstd, j * TILES + (k + 1))
                dve.wait_ge(again_in[k % 2], (j * 2 + (k // 2 + 1)) * 16)
                nc.vector.scalar_tensor_tensor(x_again[:, k % 2, :], normed[:, k % 2, :], rstd[:, k:k + 1],
                                               x_again[:, k % 2, :], ALU.mult, ALU.add).then_inc(x1_ready, 1)

            def tail(i):
                j = i - 1
                norm_stats(j, 0)
                blend_traces(i, 3)
                norm_stats(j, 1)
                temporal_lo(i, 3)
                norm_sum(j, 0)
                norm_stats(j, 2)
                norm_sum(j, 1)
                norm_stats(j, 3)
                norm_sum(j, 2)
                norm_sum(j, 3)

            def step(i, first=False):
                gates(i - 1)
                context(i)
                if first:
                    prepare(5, range(NC))
                trace_part(i)
                tail(i)

            nc.vector.memset(keep[:, :], 1.0).then_inc(setup_v, 1)
            nc.vector.memset(carry[:, :, :], 0.0).then_inc(setup_v, 1)
            dve.wait_ge(setup_v, 2)
            for b in range(B + 1):
                nc.vector.memset(keep[:, b * PER_SEQ:b * PER_SEQ + 1], 0.0).then_inc(setup_v, 1)
            for k in range(TILES):
                x_lo_part(0, k)
            prepare(0, [0])
            prepare(1, range(NC))
            dve.wait_ge(small_in, 16 * 7)
            dve.wait_ge(wide_in, 16 * 5)
            for d in range(D):
                nc.vector.tensor_tensor(dblend[:, d, :], blend[:, d, :], blend[:, 1 - d, :],
                                        ALU.subtract).then_inc(setup_v, 1)
            nc.vector.tensor_scalar(cols["bg"][:, :], cols["bg"][:, :], 0.5, None, ALU.mult).then_inc(setup_v, 1)
            nc.vector.tensor_scalar(cols["btemp"][:, :], cols["btemp"][:, :], 0.5, None, ALU.mult).then_inc(setup_v, 1)
            nc.vector.tensor_scalar(col_bn2[:, :], col_bn2[:, :], 0.5, None, ALU.mult).then_inc(consts_v, 1)
            dve.wait_ge(consts_a, 2)
            nc.vector.tensor_scalar(alpha[:, :], alpha[:, :], 0.5, 0.5, ALU.mult, ALU.add).then_inc(setup_v, 1)
            nc.vector.tensor_scalar(w_blend[:, :, :], w_blend[:, :, :], 0.125, 0.125, ALU.mult,
                                    ALU.add).then_inc(setup_v, 1)
            dve.wait_ge(setup_v, 7 + B + D)
            dve.wait_ge(setup_done, 1)
            for d in range(D):
                nc.vector.tensor_scalar(wn2_h[:, d, :], ident[:, :], 0.0, col_wn2[:, d:d + 1], ALU.mult,
                                        ALU.add).then_inc(setup_v, 1)
            dve.wait_ge(setup_v, 7 + B + 2 * D)
            for d in range(D):
                nc.vector.tensor_scalar(wn2_l[:, d, :], f32(wn2_h[:, d, :]), -1.0, col_wn2[:, d:d + 1], ALU.mult,
                                        ALU.add).then_inc(consts_v, 1)
            hidden_lo(0)
            prepare(2, [0, 1])
            context(0, hidden=False)
            prepare(2, [2, 3])
            prepare(3, range(NC))
            trace_part(0, first=True)
            blend_traces(0, 3)
            temporal_lo(0, 3)
            step(1, first=True)
            with dve.Fori(2, NBLK) as i:
                step(i)

            def biases(b):
                dve.wait_ge(bias_mm, b + 1)
                dve.wait_ge(lw_in[b], 16 * 5)
                share = pc[1][:, 0:2 * NC].rearrange("p (c q) -> p c q", q=2)[:, :, 0]
                nc.vector.tensor_tensor(seq["b1"][:, b, :], share, seq["b1"][:, b, :], ALU.add).then_inc(setup_v, 1)
                dve.wait_ge(setup_v, 7 + B + 2 * D + b + 1)
                nc.vector.tensor_tensor(seq["b1b2"][:, b, :], seq["b1"][:, b, :], seq["b2"][:, b, :], ALU.add)
                nc.vector.tensor_tensor(seq["beta_b2"][:, b, :], seq["beta2"][:, b, :], seq["b2"][:, b, :],
                                        ALU.subtract).then_inc(bias_done, 1)

            def subject_lo(b, k, bank):
                dve.wait_ge(l3_hi, b * NC + k + 1)
                wh, wl = l3_w(b)
                nc.vector.tensor_tensor(wl[:, k, :], bank[:, :], f32(wh[:, k, :]),
                                        ALU.subtract).then_inc(l3_lo, 1)

            def y_lo_part(i, k):
                tok = slice(k * P, (k + 1) * P)
                dve.wait_ge(y_hi, i * TILES + (k - 3))
                nc.vector.tensor_tensor(x_l[:, :, tok], pt[k % 2][:, :].rearrange("p (c q) -> p c q", c=NC),
                                        f32(x_h[:, :, tok]), ALU.subtract).then_inc(y_lo, 1)

            def x2_lo_part(i, b, m):
                after(dve, w1_mm, i)
                dve.wait_ge(x2_hi, i * NC + (m + 1))
                nc.vector.scalar_tensor_tensor(c_l[:, m, :], pc[m % 2][:, :], seq["b1"][:, b, m:m + 1],
                                               f32(c_h[:, m, :]), ALU.add, ALU.subtract).then_inc(x2_lo, 1)

            def x3_sum_part(j, b, m):
                dve.wait_ge(tn_done, j * NC + (m + 1))
                dve.wait_ge(x2_all, j * NC + (m + 1))
                if m >= 2:
                    dve.wait_ge(x3_hi, j * NC + (m - 1))
                    dve.wait_ge(x3_lo, j * NC + (m - 1))
                nc.vector.scalar_tensor_tensor(gate[:, m % 2, :], pt[m % 2][:, :], seq["gamma2"][:, b, m:m + 1],
                                               soma[:, m, :], ALU.mult, ALU.add).then_inc(x3_sum, 1)

            def x3_lo_part(j, m):
                after(dve, l3_mm, j * TILES)
                dve.wait_ge(x3_hi, j * NC + (m + 1))
                nc.vector.tensor_tensor(t_l[:, m, :], gate[:, m % 2, :], f32(t_h[:, m, :]),
                                        ALU.subtract).then_inc(x3_lo, 1)

            def hid_lo_part(i):
                dve.wait_ge(hid_hi, i + 1)
                nc.vector.tensor_tensor(h_l[:, :], h1[:, :], f32(h_h[:, :]), ALU.subtract).then_inc(hid_lo, 1)

            def output(j, b, k):
                dve.wait_ge(l3_mm, j * TILES + (k + 1))
                after(dve, out_done[k % 2], (j * 2 + k // 2) * 16)
                bank = pm[k] if k < 3 else pt[0]
                nc.vector.tensor_tensor(ctx_t[:, k % 2, :], bank[:, :], mod[:, b, :], ALU.add).then_inc(out_ready, 1)

            def norm2_stats(i, k):
                dve.wait_ge(xx_mm, i * TILES + (k + 1))
                nc.vector.bn_stats(stats[:, k, :], pm[k][:, :]).then_inc(ln2_stats, 1)
                dve.wait_ge(ln2_stats, i * TILES + (k + 1))
                dve.sem_inc(stats_seen, 1)
                nc.vector.bn_aggr(mv[:, k, :], stats[:, k, :]).then_inc(ln2_mv, 1)

            def normalise(i, k):
                dve.wait_ge(ln2_rstd, i + 1)
                after(dve, tn_done, i * NC)
                nc.vector.tensor_scalar(stage_a[:, k, :], pm[k][:, :], rstd[:, k:k + 1], nbias[:, k:k + 1],
                                        ALU.mult, ALU.add).then_inc(n2_dve, 1)

            def step2(i, b, bp, nxt, weights=False):
                x2_lo_part(i, b, 0)
                x3_sum_part(i - 1, bp, 0)
                x3_sum_part(i - 1, bp, 1)
                x3_lo_part(i - 1, 0)
                x3_lo_part(i - 1, 1)
                x2_lo_part(i, b, 1)
                x3_sum_part(i - 1, bp, 2)
                x3_sum_part(i - 1, bp, 3)
                x3_lo_part(i - 1, 2)
                x3_lo_part(i - 1, 3)
                x2_lo_part(i, b, 2)
                x2_lo_part(i, b, 3)
                if nxt:
                    y_lo_part(i + 1, 0)
                    y_lo_part(i + 1, 1)
                output(i - 1, bp, 0)
                hid_lo_part(i)
                if nxt:
                    y_lo_part(i + 1, 2)
                output(i - 1, bp, 1)
                if nxt:
                    y_lo_part(i + 1, 3)
                output(i - 1, bp, 2)
                for k in range(TILES):
                    norm2_stats(i, k)
                if weights:
                    subject_lo(1, 0, pt[1])
                    subject_lo(1, 1, pc[1])
                output(i - 1, bp, 3)
                normalise(i, 2)
                normalise(i, 3)
                if weights:
                    subject_lo(1, 2, pt[1])
                    subject_lo(1, 3, pc[1])

            x_lo_part(NBLK, 2)
            x_lo_part(NBLK, 3)
            biases(0)
            gates(NBLK - 1)
            x2_lo_part(0, 0, 0)
            x2_lo_part(0, 0, 1)
            for k in range(TILES):
                norm_stats(NBLK - 1, k)
                if k:
                    norm_sum(NBLK - 1, k - 1)
            norm_sum(NBLK - 1, TILES - 1)
            x2_lo_part(0, 0, 2)
            x2_lo_part(0, 0, 3)
            subject_lo(0, 0, pt[0])
            subject_lo(0, 1, pt[1])
            hid_lo_part(0)
            subject_lo(0, 2, pt[0])
            subject_lo(0, 3, pt[1])
            for k in range(TILES):
                y_lo_part(1, k)
            for k in range(TILES):
                norm2_stats(0, k)
            biases(1)
            for s in range(2):
                dve.wait_ge(x1_out[s], 16 * 2 * NBLK)
            normalise(0, 2)
            normalise(0, 3)
            dve.wait_ge(lw_in[0], 16 * 6)
            dve.wait_ge(lw_in[1], 16 * 6)
            step2(1, 0, 0, True, weights=True)
            with dve.Fori(2, PER_SEQ) as i:
                step2(i, 0, 0, True)
            step2(PER_SEQ, 1, 0, True)
            with dve.Fori(PER_SEQ + 1, NBLK - 1) as i:
                step2(i, 1, 1, True)
            step2(NBLK - 1, 1, 1, False)
            x3_sum_part(NBLK - 1, 1, 0)
            x3_sum_part(NBLK - 1, 1, 1)
            x3_lo_part(NBLK - 1, 0)
            x3_sum_part(NBLK - 1, 1, 2)
            x3_lo_part(NBLK - 1, 1)
            x3_sum_part(NBLK - 1, 1, 3)
            x3_lo_part(NBLK - 1, 2)
            x3_lo_part(NBLK - 1, 3)
            for k in range(TILES):
                output(NBLK - 1, 1, k)


_INS = ['x', 'condB_tauraws', 'cond_256', 'condB_bn2', 'cond_1024', 'itok_B_0_30', 'itok_B_0_8', 'itok_B_0_7',
        'L0_cond_tau_ctx', 'L0_cond_Wg', 'L0_cond_bg', 'L0_cond_Wn1', 'L0_cond_bn1', 'L0_cond_Wsoma',
        'L0_cond_bsoma', 'L0_cond_Wtemp', 'L0_cond_btemp', 'L0_cond_Wout', 'L0_cond_gamma', 'L0_cond_beta',
        'L1_cond_W', 'L1_cond_b', 'L2_cond_W1', 'L2_cond_b1', 'L2_cond_W2', 'L2_cond_b2', 'L2_cond_gamma',
        'L2_cond_beta', 'L3_cond_weight', 'L3_cond_bias']


def kernel(**inputs):
    import numpy as _np
    import concourse.bacc as _bacc
    from concourse import mybir as _mybir
    from concourse.bass_utils import run_bass_kernel_spmd as _run

    nc = _bacc.Bacc("TRN2", target_bir_lowering=False, num_devices=1)
    arrays, args = {}, {}
    for name in _INS:
        a = _np.ascontiguousarray(inputs[name])
        if a.ndim == 0:
            a = a.reshape(1)
        arrays[f"in_{name}_dram"] = a
        args[name] = nc.dram_tensor(f"in_{name}_dram", a.shape, _mybir.dt.from_np(a.dtype), kind="ExternalInput").ap()
    x = arrays["in_x_dram"]
    out = nc.dram_tensor("out_0_dram", x.shape, _mybir.dt.from_np(x.dtype), kind="ExternalOutput").ap()
    residual_chain_kernel(nc, args, out)
    r = _run(nc, [arrays], core_ids=[0])
    return r.results[0]["out_0_dram"]
```

```python
from contextlib import ExitStack

import concourse.bass as bass
from concourse import mybir

P = 128
BLK = 512
ALU = mybir.AluOpType
ACT = mybir.ActivationFunctionType
F32 = mybir.dt.float32
F32R = mybir.dt.float32r
I32 = mybir.dt.int32
EPS = 1e-5


def after(engine, semaphore, count):
    if not isinstance(count, int) or count > 0:
        engine.wait_ge(semaphore, count)


def residual_chain_kernel(nc: bass.Bass, t: dict, out: bass.AP):
    B, SEQ, E = t["x"].shape
    NC = E // P
    NBLK = B * SEQ // BLK
    PER_SEQ = SEQ // BLK
    TILES = BLK // P
    D = t["condB_tauraws"].shape[0]
    H = t["L0_cond_Wn1"].shape[0]
    A = t["L2_cond_W1"].shape[2]
    assert NC == 4 and TILES == 4 and D == 2 and B == 2 and H == P and A == P and NBLK == 8

    x_tiles = t["x"].rearrange("b (n p) e -> (b n) p e", p=P)
    out_tiles = out.rearrange("b (n p) e -> (b n) p e", p=P)
    x1_tiles = nc.dram_tensor("x1_scratch", (NBLK * TILES, P, E), F32, kind="Internal").ap()
    mod_rows = nc.dram_tensor("mod_scratch", (D, BLK), F32, kind="Internal").ap()

    with ExitStack() as ctx:
        def sb(name, shape, dt=F32):
            return ctx.enter_context(nc.sbuf_tensor(name, shape, dt))

        def sem(name):
            return ctx.enter_context(nc.semaphore(name))

        wg_h, wg_l = sb("wg_h", [P, 2 * NC, E], F32R), sb("wg_l", [P, 2 * NC, E], F32R)
        ws_h, ws_l = sb("ws_h", [P, NC, E], F32R), sb("ws_l", [P, NC, E], F32R)
        wt_h, wt_l = sb("wt_h", [P, NC, E], F32R), sb("wt_l", [P, NC, E], F32R)
        wo_h, wo_l = sb("wo_h", [P, NC, E], F32R), sb("wo_l", [P, NC, E], F32R)
        wn1_h, wn1_l = sb("wn1_h", [P, NC, H], F32R), sb("wn1_l", [P, NC, H], F32R)
        wn2_h, wn2_l = sb("wn2_h", [P, D], F32R), sb("wn2_l", [P, D], F32R)
        x_tok = sb("x_tok", [P, 2, E])
        x_h, x_l = sb("x_h", [P, NC, BLK], F32R), sb("x_l", [P, NC, BLK], F32R)
        x_t = sb("x_t", [P, NC, BLK])
        ctx_t = sb("ctx_t", [P, 2, BLK])
        c_h, c_l = sb("c_h", [P, NC, BLK], F32R), sb("c_l", [P, NC, BLK], F32R)
        h1 = sb("h1", [P, BLK])
        h_h, h_l = sb("h_h", [P, BLK], F32R), sb("h_l", [P, BLK], F32R)
        mod = sb("mod", [P, D, BLK])
        soma = sb("soma", [P, NC, BLK])
        gate = sb("gate", [P, 2, BLK])
        t_h, t_l = sb("t_h", [P, NC, BLK], F32R), sb("t_l", [P, NC, BLK], F32R)
        s_h, s_l = sb("s_h", [P, NC, BLK], F32R), sb("s_l", [P, NC, BLK], F32R)
        stage_a = sb("stage_a", [P, 4, E])
        stage_b = sb("stage_b", [P, 4, E])
        x_again, normed = stage_a[:, 0:2, :], stage_a[:, 2:4, :]
        tr1, tr0 = stage_b[:, 0:2, :], stage_b[:, 2:4, :]
        gamma_row, beta_row = sb("gamma_row", [P, E]), sb("beta_row", [P, E])
        ident = sb("ident", [P, P])
        names = ["bg", "bsoma", "btemp"]
        cols = {n: sb("col_" + n, [P, NC]) for n in names}
        col_bn1 = sb("col_bn1", [P, 1])
        col_bn2 = sb("col_bn2", [P, 1])
        col_wn2 = sb("col_wn2", [P, D])
        blend = sb("blend", [P, D, NC])
        dblend = sb("dblend", [P, D, NC])
        w_blend = sb("w_blend", [P, D, NC])
        taus = sb("taus", [P, 1 + D])
        alpha = sb("alpha", [P, 1 + D])
        carry = sb("carry", [P, 1 + D, NC])
        keep = sb("keep", [P, NBLK + 1])
        stats = sb("stats", [P, TILES, 6])
        mv = sb("mv", [P, TILES, 2])
        rstd = sb("rstd", [P, TILES])
        nbias = sb("nbias", [P, TILES])
        newton = sb("newton", [P, 3, TILES])
        const = sb("const", [P, 4, TILES])
        l2names = ["b1", "lb1", "b2", "gamma2", "beta2", "b1b2", "beta_b2"]
        seq = {n: sb("seq_" + n, [P, B, NC]) for n in l2names}
        idx = sb("idx", [1, 8], I32)

        pt = [ctx.enter_context(nc.psum_tensor(f"pt{i}", [P, 512], F32)) for i in range(2)]
        pc = [ctx.enter_context(nc.psum_tensor(f"pc{i}", [P, 512], F32)) for i in range(2)]
        pm = [ctx.enter_context(nc.psum_tensor(f"pm{i}", [P, 512], F32)) for i in range(4)]

        x_in = [sem(f"x_in{s}") for s in range(2)]
        first_in = [sem(f"first_in{s}") for s in range(2)]
        mod_out, mod_in = sem("mod_out"), sem("mod_in")
        again_in = [sem(f"again_in{s}") for s in range(2)]
        x1_out = [sem(f"x1_out{s}") for s in range(2)]
        small_in, wide_in = sem("small_in"), sem("wide_in")
        weight_in = [sem(f"weight_in{n}") for n in range(6)]
        idx_in = sem("idx_in")
        l1_in, l2_in, l3_in = ([sem(f"{n}{b}") for b in range(B)] for n in ("l1_in", "l2_in", "l3_in"))
        lw_in, b3_in = sem("lw_in"), sem("b3_in")
        setup_done = sem("setup_done")
        consts_v = sem("consts_v")
        consts_a = sem("consts_a")
        w_turned = sem("w_turned")
        w_hi = sem("w_hi")
        w_lo = sem("w_lo")
        tx_done, h1_mm, soma_mm, mod_mm, z_mm, wt_mm, wo_mm = (
            sem(n) for n in ("tx_done", "h1_mm", "soma_mm", "mod_mm", "z_mm", "wt_mm", "wo_mm"))
        xcopy, ctx_hi, h1_gelu, h1_hi, soma_g, mod_t, z_t, weighed, temp_hi, gate_t, s_hi = (
            sem(n) for n in ("xcopy", "ctx_hi", "h1_gelu", "h1_hi", "soma_g", "mod_t", "z_t",
                             "weighed", "temp_hi", "gate_t", "s_hi"))
        xlo, ctx_scan, ctx_carry, ctx_lo, h1_lo, s_prod, s_lo, gated, prods, traces, tr_carry = (
            sem(n) for n in ("xlo", "ctx_scan", "ctx_carry", "ctx_lo", "h1_lo", "s_prod", "s_lo",
                             "gated", "prods", "traces", "tr_carry"))
        blended, temp_lo, ln_stats, ln_mv, ln_centred, x1_ready = (
            sem(n) for n in ("blended", "temp_lo", "ln_stats", "ln_mv", "ln_centred", "x1_ready"))
        pool_step, ln_rstd = sem("pool_step"), sem("ln_rstd")
        y_in = [sem(f"y_in{s}") for s in range(2)]
        out_done = [sem(f"out_done{s}") for s in range(2)]
        (ty_done, l1_mm, tn_done, w1_mm, xx_mm, l3_mm) = (
            sem(n) for n in ("ty_done", "l1_mm", "tn_done", "w1_mm", "xx_mm", "l3_mm"))
        (y_hi, x2_hi, x2_all, relu_done, hid_hi, n2_act, n2_dve, x3_hi) = (
            sem(n) for n in ("y_hi", "x2_hi", "x2_all", "relu_done", "hid_hi", "n2_act", "n2_dve", "x3_hi"))
        (y_lo, x2_lo, hid_lo, ln2_stats, ln2_mv, x3_sum, x3_lo, out_ready) = (
            sem(n) for n in ("y_lo", "x2_lo", "hid_lo", "ln2_stats", "ln2_mv", "x3_sum", "x3_lo",
                             "out_ready"))
        ln2_rstd = sem("ln2_rstd")
        setup_v, stats_seen = sem("setup_v"), sem("stats_seen")
        l1_hi, l1_lo, l2_hi, l2_lo, l3_hi, l3_lo = (
            sem(n) for n in ("l1_hi", "l1_lo", "l2_hi", "l2_lo", "l3_hi", "l3_lo"))
        l1_eye, l3_eye, l3_turned = (sem(n) for n in ("l1_eye", "l3_eye", "l3_turned"))
        bias_done, beta_in = sem("bias_done"), sem("beta_in")

        def l1_w(b):
            return wg_h[:, b * NC:(b + 1) * NC, :], wg_l[:, b * NC:(b + 1) * NC, :]

        def w1_w(b):
            if b == 0:
                return wn1_h[:, :, :], wn1_l[:, :, :]
            return tuple(w[:, 1, :].rearrange("p (k a) -> p k a", k=NC) for w in (ws_h, ws_l))

        def w2_w(b):
            return ws_h[:, 2 * b, :], ws_l[:, 2 * b, :]

        def l3_w(b):
            return (wt_h[:, :, :], wt_l[:, :, :]) if b == 0 else (wo_h[:, :, :], wo_l[:, :, :])

        l1_raw = [[ctx_t[:, :, :], mod[:, :, :]], [stage_b[:, 0:2, :], stage_b[:, 2:4, :]]]
        l2_raw = [soma[:, 0:2, :], stage_b[:, 0:2, :]]
        l3_raw = stage_b[:, :, :]

        def adapter_parts(b):
            return [(l2_raw[b][:, 0, :].rearrange("p (k a) -> p k a", k=NC),) + w1_w(b),
                    (l2_raw[b][:, 1, :],) + w2_w(b)]

        def l1_chunk(b, k):
            return l1_raw[b][k // 2][:, k % 2, :]

        block = ctx.enter_context(nc.Block())

        def tile_of(tiles, i, j):
            return tiles[bass.ds(i * TILES + j, 1)].rearrange("a p e -> (a p) e")

        L0W = [(src.rearrange("(n p) c -> p n c", p=P), raw) for src, raw in (
            (t["L0_cond_Wn1"], gate[:, 0:1, :]),
            (t["L0_cond_Wsoma"], stage_a[:, :, :]),
            (t["L0_cond_Wg"][:, 0:E], stage_b[:, :, :]),
            (t["L0_cond_Wg"][:, E:2 * E], stage_a[:, :, :]),
            (t["L0_cond_Wtemp"], stage_a[:, :, :]),
            (t["L0_cond_Wout"], stage_a[:, :, :]))]
        W_COUNT = [1, 4, 4, 4, 4, 4]
        W_SCALE = [1.0, 1.0, 1.0, 1.0, 1.0, 0.5]
        W_BEFORE = [sum(W_COUNT[:n]) for n in range(6)]

        W4_AFTER = [[0, 1], [2], [3], []]

        def w_dest(n, k):
            if n == 0:
                return (w[:, :, :].rearrange("p a b -> p (a b)") for w in (wn1_h, wn1_l))
            h, lo, at = [None, (ws_h, ws_l, 0), (wg_h, wg_l, 0), (wg_h, wg_l, NC), (wt_h, wt_l, 0),
                         (wo_h, wo_l, 0)][n]
            return h[:, at + k, :], lo[:, at + k, :]

        def last_block(j):
            return isinstance(j, int) and j == NBLK - 1

        def out_tile(j, k):
            return stage_b[:, k, :] if last_block(j) else ctx_t[:, k % 2, :]

        def n2_bank(j, c):
            return [pc[0], pc[1], pt[1], pt[0]][c] if last_block(j) else pt[c % 2]

        def l3_bank(j, k):
            if isinstance(j, int) and j == NBLK - 2:
                return [pm[0], pm[1], pt[1], pt[0]][k]
            return [pm[0], pm[1], pm[2], pm[3] if last_block(j) else pt[0]][k]

        def x_first(j):
            return x_tok[:, j, :] if j < 2 else soma[:, j - 2, :]

        @block.sync
        def _(sp):
            def load_weight(n):
                src, raw = L0W[n]
                if n == 3:
                    sp.wait_ge(w_turned, W_BEFORE[2])
                if n in (4, 5):
                    sp.wait_ge(w_turned, W_BEFORE[n])
                sp.dma_start(raw, src).then_inc(weight_in[n], 16)

            def load_x(i, j):
                if isinstance(i, int) and i == 0:
                    loaded = x_in[j] if j < 2 else first_in[j - 2]
                    sp.dma_start(x_first(j), tile_of(x_tiles, 0, j)).then_inc(loaded, 16)
                    return
                after(sp, tx_done, i * TILES + (j - 1))
                if isinstance(i, int) and i == NBLK:
                    sp.wait_ge(x1_out[j % 2], (j // 2 + 1) * 16)
                    src = tile_of(x1_tiles, 0, j)
                else:
                    src = tile_of(x_tiles, i, j)
                sp.dma_start(x_tok[:, j % 2, :], src).then_inc(x_in[j % 2], 16)

            def load_again(j, k):
                after(sp, x1_out[k % 2], (j * 2 + k // 2) * 16)
                sp.dma_start(x_again[:, k % 2, :], tile_of(x_tiles, j, k)).then_inc(again_in[k % 2], 16)

            def spread_mod(i):
                sp.wait_ge(mod_t, i + 1)
                sp.dma_start(mod_rows, h1[0:D, :]).then_inc(mod_out, 16)
                sp.wait_ge(mod_out, i * 16 + 16)
                sp.dma_start(mod[:, :, :], mod_rows.partition_broadcast(P)).then_inc(mod_in, 16)

            def store_x1(j, k):
                sp.wait_ge(x1_ready, j * TILES + k + 1)
                sp.dma_start(tile_of(x1_tiles, j, k), x_again[:, k % 2, :]).then_inc(x1_out[k % 2], 16)

            for j in range(TILES):
                load_x(0, j)
            load_weight(0)
            load_weight(1)
            with nc.allow_non_contiguous_dma(reason="bias columns, a few hundred words"):
                sp.dma_start(col_bn1[:, :], t["L0_cond_bn1"].rearrange("(p k) -> p k", k=1)).then_inc(small_in, 16)
                for n, src in (("bsoma", "L0_cond_bsoma"), ("bg", "L0_cond_bg"),
                               ("btemp", "L0_cond_btemp")):
                    sp.dma_start(cols[n][:, :], t[src].rearrange("(k p) -> p k", p=P)).then_inc(small_in, 16)
                for d in range(D):
                    sp.dma_start(blend[:, d, :],
                                 t["cond_1024"][d, :].rearrange("(k p) -> p k", p=P)).then_inc(small_in, 16)
            load_weight(2)
            load_weight(3)

            def step(i, first=False, weights=None):
                j = i - 1
                if not first:
                    store_x1(j - 1, 2)
                    store_x1(j - 1, 3)
                load_x(i + 1, 0)
                load_x(i + 1, 1)
                load_again(j, 0)
                load_again(j, 1)
                spread_mod(i)
                if weights:
                    weights()
                load_x(i + 1, 2)
                load_x(i + 1, 3)
                store_x1(j, 0)
                store_x1(j, 1)
                load_again(j, 2)
                load_again(j, 3)

            load_x(1, 0)
            load_x(1, 1)
            load_weight(4)
            spread_mod(0)
            load_x(1, 2)
            load_x(1, 3)
            load_weight(5)
            sp.wait_ge(w_turned, W_BEFORE[5] + W_COUNT[5])
            step(1, first=True)
            with sp.Fori(2, NBLK - 1) as i:
                step(i)

            sp.wait_ge(idx_in, 48)
            which = [sp.value_load(idx[0:1, n:n + 1], min_val=0, max_val=m)
                     for n, m in enumerate([31, 31, 9, 9, 7, 7])]

            def cat(b):
                return which[b]

            def lang(b):
                return which[2 + b]

            def subj(b):
                return which[4 + b]

            def cols_of(src, n):
                return src[bass.ds(n, 1), :].rearrange("a (k p) -> p (a k)", p=P)

            with nc.allow_non_contiguous_dma(reason="bias columns, a few hundred words"):
                for b in range(B):
                    sp.dma_start(seq["b1"][:, b, :], cols_of(t["L1_cond_b"], cat(b))).then_inc(lw_in, 16)
                    sp.dma_start(seq["lb1"][:, b, 0:1], cols_of(t["L2_cond_b1"], lang(b))).then_inc(lw_in, 16)
                    for n, src in (("b2", "L2_cond_b2"), ("gamma2", "L2_cond_gamma"), ("beta2", "L2_cond_beta")):
                        sp.dma_start(seq[n][:, b, :], cols_of(t[src], lang(b))).then_inc(lw_in, 16)

            def load_l1(b, half):
                src = t["L1_cond_W"][bass.ds(cat(b), 1)].rearrange("a (k p) o -> p (a k) o", p=P)
                sp.dma_start(l1_raw[b][half], src[:, 2 * half:2 * half + 2, :]).then_inc(l1_in[b], 16)

            def load_l2(b):
                sp.dma_start(l2_raw[b][:, 0, :].rearrange("p (k a) -> p k a", k=NC),
                             t["L2_cond_W1"][bass.ds(lang(b), 1)].rearrange(
                                 "a (k p) h -> p (a k) h", p=P)).then_inc(l2_in[b], 16)
                sp.dma_start(l2_raw[b][:, 1, :], t["L2_cond_W2"][bass.ds(lang(b), 1)].rearrange(
                    "a p o -> (a p) o")).then_inc(l2_in[b], 16)

            def load_l3(b):
                sp.dma_start(l3_raw, t["L3_cond_weight"][bass.ds(subj(b), 1)].rearrange(
                    "a (k p) c -> p (a k) c", p=P)).then_inc(l3_in[b], 16)

            def load_b3(b):
                sp.wait_ge(prods, NBLK * NC * D)
                sp.dma_start(mod[:, b, :], t["L3_cond_bias"][bass.ds(subj(b), 1), :].rearrange(
                    "a c -> (a c)").partition_broadcast(P)).then_inc(b3_in, 16)

            def load_y(i, j):
                if isinstance(i, int) and i == 1 and j < 2:
                    sp.wait_ge(tx_done, NBLK * TILES + TILES)
                else:
                    sp.wait_ge(ty_done, i * TILES + (j - 5))
                sp.dma_start(x_tok[:, j % 2, :], tile_of(x1_tiles, i, j)).then_inc(y_in[j % 2], 16)

            def store_out(j, k):
                sp.wait_ge(out_ready, j * TILES + k + 1)
                sp.dma_start(tile_of(out_tiles, j, k), out_tile(j, k)).then_inc(out_done[k % 2], 16)

            def first_weights():
                for done in (ctx_hi, ctx_lo, ctx_carry):
                    sp.wait_ge(done, NBLK * NC)
                load_l1(0, 0)
                sp.wait_ge(prods, NBLK * NC * D)
                load_l1(0, 1)

            step(NBLK - 1, weights=first_weights)
            sp.wait_ge(temp_lo, NBLK * NC)
            sp.wait_ge(temp_hi, NBLK * NC)
            load_l3(0)
            sp.wait_ge(s_prod, NBLK * NC)
            load_l2(0)
            for s in range(2):
                sp.wait_ge(x1_out[s], 16 * 2 * 2)
            load_y(1, 0)
            load_y(1, 1)
            store_x1(NBLK - 2, 2)
            store_x1(NBLK - 2, 3)
            load_again(NBLK - 1, 0)
            load_again(NBLK - 1, 1)
            sp.wait_ge(l3_turned, NC)
            load_l1(1, 0)
            load_l1(1, 1)
            store_x1(NBLK - 1, 0)
            store_x1(NBLK - 1, 1)
            load_again(NBLK - 1, 2)
            load_again(NBLK - 1, 3)
            load_y(1, 2)
            load_y(1, 3)
            store_x1(NBLK - 1, 2)
            store_x1(NBLK - 1, 3)
            for s in range(2):
                sp.wait_ge(x1_out[s], 16 * 2 * NBLK)
            for done, count in ((l1_hi, NC), (l1_lo, NC)):
                sp.wait_ge(done, count)
            load_b3(0)
            load_b3(1)

            def second_l3():
                for done, count in ((l1_hi, 2 * NC), (l1_lo, 2 * NC)):
                    sp.wait_ge(done, count)
                load_l3(1)

            def second_l2():
                sp.wait_ge(l3_turned, 2 * NC)
                load_l2(1)

            def step2(i):
                load_y(i + 1, 0)
                load_y(i + 1, 1)
                load_y(i + 1, 2)
                store_out(i - 1, 0)
                load_y(i + 1, 3)
                for k in (1, 2, 3):
                    store_out(i - 1, k)

            second_l3()
            step2(1)
            second_l2()
            with sp.Fori(2, NBLK - 1) as i:
                step2(i)
            for j in (NBLK - 2, NBLK - 1):
                for k in range(TILES):
                    store_out(j, k)
            for s in range(2):
                sp.wait_ge(out_done[s], 16 * 2 * NBLK)

        @block.gpsimd
        def _(pool):
            nc.gpsimd.memset(ident[:, :], 0.0).then_inc(pool_step, 1)
            pool.wait_ge(pool_step, 1)
            nc.gpsimd.affine_select(out=ident[:, :], in_=ident[:, :], compare_op=ALU.not_equal, fill=1.0,
                                    base=0, pattern=[[-1, P]], channel_multiplier=1).then_inc(setup_done, 1)
            with nc.allow_non_contiguous_dma(reason="bias columns, a few hundred words"):
                pool.dma_start(col_wn2[:, :], t["cond_256"].rearrange("d p -> p d")).then_inc(wide_in, 16)
                pool.dma_start(col_bn2[0:D, :], t["condB_bn2"].rearrange("(d k) -> d k", k=1)).then_inc(wide_in, 16)
                pool.dma_start(taus[:, 0:1], t["L0_cond_tau_ctx"].partition_broadcast(P)).then_inc(wide_in, 16)
                pool.dma_start(taus[:, 1:1 + D], t["condB_tauraws"].partition_broadcast(P)).then_inc(wide_in, 16)
                pool.dma_start(gamma_row[:, :], t["L0_cond_gamma"].partition_broadcast(P)).then_inc(wide_in, 16)
                pool.dma_start(beta_row[:, :], t["L0_cond_beta"].partition_broadcast(P)).then_inc(wide_in, 16)
            for n, src in enumerate(("itok_B_0_30", "itok_B_0_8", "itok_B_0_7")):
                pool.dma_start(idx[0:1, 2 * n:2 * n + 2], t[src].rearrange("(a k) -> a k", a=1)).then_inc(idx_in, 16)
            eps, minus_half, minus_three, half = (const[:, q, :] for q in range(4))
            for c, value in ((eps, EPS), (minus_half, -0.5), (minus_three, -3.0), (half, 0.5)):
                nc.gpsimd.memset(c, value).then_inc(pool_step, 1)
            pool.wait_ge(pool_step, 5)

            def inv_sqrt(tiles, at):
                n = tiles.stop - tiles.start
                v, y, q = newton[:, 0, 0:n], newton[:, 1, 0:n], newton[:, 2, 0:n]
                nc.gpsimd.tensor_tensor(v, mv[:, tiles, 1], eps[:, 0:n], ALU.add).then_inc(pool_step, 1)
                pool.wait_ge(pool_step, at + 1)
                nc.gpsimd.tensor_tensor(y, v, minus_half[:, 0:n], ALU.pow).then_inc(pool_step, 1)
                pool.wait_ge(pool_step, at + 2)
                nc.gpsimd.tensor_tensor(q, y, y, ALU.mult).then_inc(pool_step, 1)
                pool.wait_ge(pool_step, at + 3)
                nc.gpsimd.tensor_tensor(q, q, v, ALU.mult).then_inc(pool_step, 1)
                pool.wait_ge(pool_step, at + 4)
                nc.gpsimd.tensor_tensor(q, q, minus_three[:, 0:n], ALU.add).then_inc(pool_step, 1)
                pool.wait_ge(pool_step, at + 5)
                nc.gpsimd.tensor_tensor(q, q, y, ALU.mult).then_inc(pool_step, 1)
                pool.wait_ge(pool_step, at + 6)
                return q

            def x_lo_part(i, k):
                tok = slice(k * P, (k + 1) * P)
                pool.wait_ge(xcopy, i * TILES + (k + 1))
                if k == 0:
                    pool.wait_ge(z_mm, i * NC)
                nc.gpsimd.tensor_tensor(x_l[:, :, tok], x_t[:, :, tok], x_h[:, :, tok].bitcast(F32),
                                        ALU.subtract).then_inc(xlo, 1)

            def norm_scale(j, k):
                pool.wait_ge(ln_mv, j * TILES + (k + 1))
                corr = inv_sqrt(slice(k, k + 1), j * (TILES * 6) + (5 + k * 6))
                nc.gpsimd.tensor_tensor(rstd[:, k:k + 1], corr, minus_half[:, 0:1], ALU.mult).then_inc(ln_rstd, 1)
                pool.wait_ge(ln_rstd, j * TILES + (k + 1))

            def add_beta(j, k):
                pool.wait_ge(again_in[k % 2], (j * 2 + (k // 2 + 1)) * 16)
                nc.gpsimd.tensor_tensor(x_again[:, k % 2, :], x_again[:, k % 2, :], beta_row[:, :],
                                        ALU.add).then_inc(beta_in, 1)

            for k in range(TILES):
                x_lo_part(1, k)
            pool.wait_ge(wide_in, 16 * 6)
            with pool.Fori(1, NBLK - 1) as i:
                add_beta(i - 1, 0)
                add_beta(i - 1, 1)
                norm_scale(i - 1, 0)
                x_lo_part(i + 1, 0)
                norm_scale(i - 1, 1)
                x_lo_part(i + 1, 1)
                norm_scale(i - 1, 2)
                norm_scale(i - 1, 3)
                x_lo_part(i + 1, 2)
                x_lo_part(i + 1, 3)
                add_beta(i - 1, 2)
                add_beta(i - 1, 3)

            def add_eye(chunks, eye):
                for q, chunk in enumerate(chunks):
                    o = slice(q * P, (q + 1) * P)
                    nc.gpsimd.tensor_tensor(chunk[:, o], chunk[:, o], ident[:, :], ALU.add).then_inc(eye, 1)

            def l1_residual(b):
                pool.wait_ge(l1_in[b], 32)
                add_eye([l1_chunk(b, q) for q in range(NC)], l1_eye)

            def l3_residual(b):
                pool.wait_ge(l3_in[b], 16)
                add_eye([l3_raw[:, q, :] for q in range(NC)], l3_eye)

            def linear_lo(b):
                wh, wl = l1_w(b)
                pool.wait_ge(l1_eye, (b + 1) * NC)
                for k in range(NC):
                    pool.wait_ge(l1_hi, b * NC + k + 1)
                    nc.gpsimd.tensor_tensor(wl[:, k, :], l1_chunk(b, k), wh[:, k, :].bitcast(F32),
                                            ALU.subtract).then_inc(l1_lo, 1)

            def adapter_lo(b):
                for n, (raw, wh, wl) in enumerate(adapter_parts(b)):
                    pool.wait_ge(l2_hi, b * 2 + n + 1)
                    nc.gpsimd.tensor_tensor(wl, raw, wh.bitcast(F32), ALU.subtract).then_inc(l2_lo, 1)

            second = 5 + NBLK * TILES * 6

            def norm2_scale(j):
                at = j * 8 + second
                pool.wait_ge(ln2_mv, j * TILES + TILES)
                nc.gpsimd.tensor_tensor(nbias[:, :], mv[:, :, 0], half, ALU.mult).then_inc(pool_step, 1)
                corr = inv_sqrt(slice(0, TILES), at + 1)
                nc.gpsimd.tensor_tensor(rstd[:, :], corr, minus_half, ALU.mult).then_inc(pool_step, 1)
                nc.gpsimd.tensor_tensor(nbias[:, :], corr, nbias[:, :], ALU.mult).then_inc(ln2_rstd, 1)
                pool.wait_ge(pool_step, at + 8)
                pool.wait_ge(ln2_rstd, j + 1)

            add_beta(NBLK - 2, 0)
            add_beta(NBLK - 2, 1)
            l1_residual(0)
            norm_scale(NBLK - 2, 0)
            norm_scale(NBLK - 2, 1)
            linear_lo(0)
            norm_scale(NBLK - 2, 2)
            norm_scale(NBLK - 2, 3)
            add_beta(NBLK - 2, 2)
            add_beta(NBLK - 2, 3)
            l3_residual(0)
            add_beta(NBLK - 1, 0)
            add_beta(NBLK - 1, 1)
            norm_scale(NBLK - 1, 0)
            norm_scale(NBLK - 1, 1)
            add_beta(NBLK - 1, 2)
            norm_scale(NBLK - 1, 2)
            add_beta(NBLK - 1, 3)
            norm_scale(NBLK - 1, 3)
            l1_residual(1)
            norm2_scale(0)
            linear_lo(1)
            l3_residual(1)
            with pool.Fori(1, PER_SEQ) as j:
                norm2_scale(j)
            adapter_lo(1)
            with pool.Fori(PER_SEQ, NBLK) as j:
                norm2_scale(j)

        @block.tensor
        def _(pe):
            def product(acc, pairs, start=True, stop=True):
                n = len(pairs)
                for q, (ah, al, bh, bl) in enumerate(pairs):
                    nc.tensor.matmul(acc, ah, bh, start=start and q == 0, stop=False)
                    nc.tensor.matmul(acc, ah, bl, start=False, stop=False)
                    last = nc.tensor.matmul(acc, al, bh, start=False, stop=stop and q == n - 1)
                return last

            def turn(acc, sources, stop=True):
                for q, src in enumerate(sources):
                    last = nc.tensor.matmul(acc[:, q * P:(q + 1) * P], src, ident[:, :], is_transpose=True,
                                            start=(q == 0), stop=stop and (q == 3), skip_group_check=True)
                return last

            def out_cols(m):
                return slice(m * P, (m + 1) * P)

            def prepare(n, chunks):
                pe.wait_ge(weight_in[n], 16)
                raw = L0W[n][1]
                for k in chunks:
                    c = W_BEFORE[n] + k
                    if c >= 4:
                        pe.wait_ge(w_hi, c - 3)
                        pe.wait_ge(w_lo, c - 3)
                    pieces = ([raw[:, 0, out_cols(q)] for q in range(4)] if n == 0 else
                              [raw[:, q, out_cols(k)] for q in range(4)])
                    turn(pm[c % 4], pieces).then_inc(w_turned, 1)

            def ready(n):
                pe.wait_ge(w_hi, W_BEFORE[n] + W_COUNT[n])
                pe.wait_ge(w_lo, W_BEFORE[n] + W_COUNT[n])

            def turn_x(i, k):
                if isinstance(i, int) and i == 0:
                    pe.wait_ge(x_in[k] if k < 2 else first_in[k - 2], 16)
                else:
                    pe.wait_ge(x_in[k % 2], (i * 2 + k // 2) * 16)
                if k == 0:
                    after(pe, mod_t, i)
                if k >= 2:
                    pe.wait_ge(xcopy, i * TILES + (k - 1))
                src = x_first(k) if isinstance(i, int) and i == 0 else x_tok[:, k % 2, :]
                turn(pt[k % 2], [src[:, out_cols(c)] for c in range(NC)]).then_inc(tx_done, 1)

            def h1_product(i):
                pe.wait_ge(xcopy, i * TILES + TILES)
                pe.wait_ge(xlo, i * TILES + TILES)
                product(pt[0][:, :], [(wn1_h[:, c, :], wn1_l[:, c, :], x_h[:, c, :], x_l[:, c, :])
                                      for c in range(NC)]).then_inc(h1_mm, 1)

            def soma_product(i, after_chunk=None):
                for m in range(NC):
                    if m >= 2:
                        pe.wait_ge(soma_g, i * NC + (m - 1))
                    else:
                        after(pe, z_t, i * NC + (m - 1))
                    o = out_cols(m)
                    product(pc[m % 2][:, :], [(ws_h[:, c, o], ws_l[:, c, o], x_h[:, c, :], x_l[:, c, :])
                                              for c in range(NC)]).then_inc(soma_mm, 1)
                    if after_chunk:
                        after_chunk(m)

            def mod_product(i):
                pe.wait_ge(h1_hi, i + 1)
                pe.wait_ge(h1_lo, i + 1)
                product(pt[0][0:D, :], [(wn2_h[:, :], wn2_l[:, :], h_h[:, :], h_l[:, :])]).then_inc(mod_mm, 1)

            def z_product(i, first=False):
                for m in range(NC):
                    if m < 2:
                        pe.wait_ge(soma_g, i * NC + (3 + m))
                    else:
                        pe.wait_ge(z_t, i * NC + (m - 1))
                    o = out_cols(m)
                    product(pc[m % 2][:, :],
                            [(wg_h[:, c, o], wg_l[:, c, o], x_h[:, c, :], x_l[:, c, :]) for c in range(NC)],
                            stop=False)
                    if first and m == 0:
                        ready(3)
                    if m == 0:
                        pe.wait_ge(ctx_hi, i * NC + NC)
                        pe.wait_ge(ctx_lo, i * NC + NC)
                    product(pc[m % 2][:, :],
                            [(wg_h[:, NC + c, o], wg_l[:, NC + c, o], c_h[:, c, :], c_l[:, c, :])
                             for c in range(NC)], start=False).then_inc(z_mm, 1)
                    if first:
                        prepare(4, W4_AFTER[m])

            def temp_product(j, halves=(0, 1)):
                def part(c, m):
                    if c == 0:
                        after(pe, ln_centred, j * TILES + (m - 3))
                    o = out_cols(m)
                    nc.tensor.matmul(pm[m][:, :], wt_h[:, c, o], t_h[:, c, :], start=(c == 0), stop=False)
                    nc.tensor.matmul(pm[m][:, :], wt_h[:, c, o], t_l[:, c, :], start=False, stop=False)
                    last = nc.tensor.matmul(pm[m][:, :], wt_l[:, c, o], t_h[:, c, :], start=False,
                                            stop=(c == NC - 1))
                    if c == NC - 1:
                        last.then_inc(wt_mm, 1)

                for c in (0, 1) if 0 in halves else ():
                    pe.wait_ge(temp_hi, j * NC + (c + 1))
                    pe.wait_ge(temp_lo, j * NC + (c + 1))
                    for m in range(NC - 1):
                        part(c, m)
                for c in (0, 1) if 0 in halves else ():
                    part(c, NC - 1)
                for c in (2, 3) if 1 in halves else ():
                    pe.wait_ge(temp_hi, j * NC + (c + 1))
                    pe.wait_ge(temp_lo, j * NC + (c + 1))
                    for m in range(NC):
                        part(c, m)

            def out_product(j, k):
                if k == 0:
                    pe.wait_ge(gate_t, j * NC + NC)
                    pe.wait_ge(s_hi, j * NC + NC)
                    pe.wait_ge(s_lo, j * NC + NC)
                tok = out_cols(k)
                product(pm[k][:, :], [(s_h[:, c, tok], s_l[:, c, tok], wo_h[:, c, :], wo_l[:, c, :])
                                      for c in range(NC)]).then_inc(wo_mm, 1)

            def step(i):
                temp_product(i - 1)
                h1_product(i)
                soma_product(i, lambda m: mod_product(i) if m == 2 else None)
                z_product(i)
                for k in range(TILES):
                    out_product(i - 1, k)
                    turn_x(i + 1, k)

            pe.wait_ge(setup_done, 1)
            for k in range(TILES):
                turn_x(0, k)
            prepare(0, [0])
            prepare(1, range(NC))
            ready(0)
            h1_product(0)
            ready(1)
            soma_product(0, lambda m: prepare(2 + m // 2, [m % 2 * 2, m % 2 * 2 + 1]))
            pe.wait_ge(consts_v, 2)
            mod_product(0)
            ready(2)
            z_product(0, first=True)
            turn_x(1, 0)
            turn_x(1, 1)
            ready(4)
            temp_product(0, [0])
            turn_x(1, 2)
            turn_x(1, 3)
            temp_product(0, [1])
            h1_product(1)
            soma_product(1, lambda m: mod_product(1) if m == 2 else None)
            pe.wait_ge(gate_t, NC)
            prepare(5, range(NC))
            z_product(1)
            ready(5)
            for k in range(TILES):
                out_product(0, k)
                turn_x(2, k)
            with pe.Fori(2, NBLK) as i:
                step(i)

            def turn_l3(b, k, bank):
                pe.wait_ge(l3_eye, (b + 1) * NC)
                if k >= 2:
                    pe.wait_ge(l3_hi, b * NC + k - 1)
                    pe.wait_ge(l3_lo, b * NC + k - 1)
                turn(bank, [l3_raw[:, q, out_cols(k)] for q in range(4)]).then_inc(l3_turned, 1)

            def turn_y(i, k, shared=False):
                if k < 2 and shared:
                    pe.wait_ge(x3_sum, i * NC + (k - 5))
                pe.wait_ge(y_in[k % 2], (i * 2 + (k // 2 - 1)) * 16)
                if k >= 2:
                    pe.wait_ge(y_hi, i * TILES + (k - 5))
                    pe.wait_ge(y_lo, i * TILES + (k - 5))
                turn(pt[k % 2], [x_tok[:, k % 2, out_cols(c)] for c in range(NC)]).then_inc(ty_done, 1)

            def l1_product(i, b, m, between=None):
                if m == 0 and isinstance(i, int) and i == 0:
                    pe.wait_ge(xcopy, (NBLK + 1) * TILES)
                    pe.wait_ge(xlo, (NBLK + 1) * TILES)
                elif m == 0:
                    pe.wait_ge(y_hi, i * TILES)
                    pe.wait_ge(y_lo, i * TILES)
                    after(pe, relu_done, i)
                if m >= 2:
                    pe.wait_ge(x2_hi, i * NC + (m - 1))
                    pe.wait_ge(x2_lo, i * NC + (m - 1))
                o = out_cols(m)
                wh, wl = l1_w(b)
                pairs = [(wh[:, c, o], wl[:, c, o], x_h[:, c, :], x_l[:, c, :]) for c in range(NC)]
                product(pc[m % 2][:, :], pairs[:2], stop=False)
                if between:
                    between()
                product(pc[m % 2][:, :], pairs[2:], start=False).then_inc(l1_mm, 1)

            def w1_product(i, b):
                if isinstance(i, int):
                    pe.wait_ge(l2_hi, b * 2 + 2)
                    pe.wait_ge(l2_lo, b * 2 + 2)
                pe.wait_ge(x2_hi, i * NC + NC - 1)
                pe.wait_ge(x2_lo, i * NC + NC - 1)
                wh, wl = w1_w(b)
                pairs = [(wh[:, c, :], wl[:, c, :], c_h[:, c, :], c_l[:, c, :]) for c in range(NC)]
                product(pc[0][:, :], pairs[:3], stop=False)
                pe.wait_ge(x2_hi, i * NC + NC)
                pe.wait_ge(x2_lo, i * NC + NC)
                product(pc[0][:, :], pairs[3:], start=False).then_inc(w1_mm, 1)

            def xx_product(i, b, k):
                if k == 0:
                    pe.wait_ge(hid_hi, i + 1)
                    pe.wait_ge(hid_lo, i + 1)
                if k < (2 if last_block(i) else 3):
                    after(pe, out_ready, i * TILES + (k - 3))
                tok = out_cols(k)
                turn(pm[k], [x_t[:, c, tok] for c in range(NC)], stop=False)
                wh, wl = w2_w(b)
                nc.tensor.matmul(pm[k][:, :], h_h[:, tok], wh, start=False, stop=False, skip_group_check=True)
                nc.tensor.matmul(pm[k][:, :], h_l[:, tok], wh, start=False, stop=False, skip_group_check=True)
                nc.tensor.matmul(pm[k][:, :], h_h[:, tok], wl, start=False, stop=True,
                                 skip_group_check=True).then_inc(xx_mm, 1)

            def turn_n2(j, chunks):
                for c in chunks:
                    if c == 0:
                        pe.wait_ge(n2_act, j * 2 + 2)
                        pe.wait_ge(n2_dve, j * 2 + 2)
                        if not last_block(j):
                            after(pe, out_ready, j * TILES)
                    if c >= 2 and last_block(j):
                        pe.wait_ge(out_ready, j * TILES - c % 2)
                    elif c >= 2:
                        pe.wait_ge(x3_sum, j * NC + (c - 1))
                    turn(n2_bank(j, c), [stage_a[:, k, out_cols(c)] for k in range(TILES)]).then_inc(tn_done, 1)

            def l3_product(j, b, k):
                if k == 0:
                    pe.wait_ge(x3_hi, j * NC + NC)
                    pe.wait_ge(x3_lo, j * NC + NC)
                if k == 3:
                    pe.wait_ge(y_hi, j * TILES + 7)
                    pe.wait_ge(y_lo, j * TILES + 7)
                l3_tile(l3_bank(j, k), b, k)

            def l3_tile(bank, b, k):
                tok = out_cols(k)
                wh, wl = l3_w(b)
                product(bank[:, :], [(t_h[:, c, tok], t_l[:, c, tok], wh[:, c, :], wl[:, c, :])
                                     for c in range(NC)]).then_inc(l3_mm, 1)

            def step2(i, b, bp, weights=False):
                l1_product(i, b, 0)
                l1_product(i, b, 1, lambda: turn_n2(i - 1, (0, 1)))
                l1_product(i, b, 2, lambda: turn_n2(i - 1, (2, 3)))
                l1_product(i, b, 3)
                turn_y(i + 1, 0, True)
                turn_y(i + 1, 1, True)
                l3_product(i - 1, bp, 0)
                w1_product(i, b)
                turn_y(i + 1, 2)
                l3_product(i - 1, bp, 1)
                turn_y(i + 1, 3)
                l3_product(i - 1, bp, 2)
                if weights:
                    pe.wait_ge(y_hi, i * TILES + TILES)
                    pe.wait_ge(y_lo, i * TILES + TILES)
                    turn_l3(1, 0, pt[1])
                    turn_l3(1, 1, pc[1])
                for k in range(TILES):
                    xx_product(i, b, k)
                if weights:
                    turn_l3(1, 2, pt[1])
                    turn_l3(1, 3, pc[1])
                l3_product(i - 1, bp, 3)

            def last_step2(i, b):
                l1_product(i, b, 0)
                l1_product(i, b, 1, lambda: turn_n2(i - 1, (0, 1)))
                l1_product(i, b, 2, lambda: turn_n2(i - 1, (2, 3)))
                l1_product(i, b, 3)
                l3_product(i - 1, b, 0)
                w1_product(i, b)
                l3_product(i - 1, b, 1)
                for k in range(TILES):
                    xx_product(i, b, k)
                pe.wait_ge(x3_sum, i * NC)
                l3_tile(l3_bank(i - 1, 2), b, 2)
                l3_tile(l3_bank(i - 1, 3), b, 3)
                turn_n2(i, range(NC))
                wh, wl = l3_w(b)
                for c in range(NC):
                    pe.wait_ge(x3_hi, i * NC + c + 1)
                    pe.wait_ge(x3_lo, i * NC + c + 1)
                    for k in range(TILES):
                        tok, bank = out_cols(k), l3_bank(i, k)
                        nc.tensor.matmul(bank[:, :], t_h[:, c, tok], wh[:, c, :], start=(c == 0), stop=False)
                        nc.tensor.matmul(bank[:, :], t_h[:, c, tok], wl[:, c, :], start=False, stop=False)
                        last = nc.tensor.matmul(bank[:, :], t_l[:, c, tok], wh[:, c, :], start=False,
                                                stop=(c == NC - 1))
                        if c == NC - 1:
                            last.then_inc(l3_mm, 1)

            temp_product(NBLK - 1)
            pe.wait_ge(l1_hi, NC)
            pe.wait_ge(l1_lo, NC)
            l1_product(0, 0, 0)
            l1_product(0, 0, 1)
            turn_l3(0, 0, pt[0])
            turn_l3(0, 1, pt[1])
            out_product(NBLK - 1, 0)
            out_product(NBLK - 1, 1)
            turn_l3(0, 2, pt[0])
            turn_l3(0, 3, pt[1])
            out_product(NBLK - 1, 2)
            out_product(NBLK - 1, 3)
            l1_product(0, 0, 2)
            l1_product(0, 0, 3)
            pe.wait_ge(l3_hi, NC)
            pe.wait_ge(l3_lo, NC)
            turn_y(1, 0)
            turn_y(1, 1)
            w1_product(0, 0)
            turn_y(1, 2)
            turn_y(1, 3)
            pe.wait_ge(ln_centred, NBLK * TILES)
            for k in range(TILES):
                xx_product(0, 0, k)
            step2(1, 0, 0, weights=True)
            pe.wait_ge(l3_hi, 2 * NC)
            pe.wait_ge(l3_lo, 2 * NC)
            with pe.Fori(2, PER_SEQ) as i:
                step2(i, 0, 0)
            pe.wait_ge(l1_hi, 2 * NC)
            pe.wait_ge(l1_lo, 2 * NC)
            step2(PER_SEQ, 1, 0)
            with pe.Fori(PER_SEQ + 1, NBLK - 1) as i:
                step2(i, 1, 1)
            last_step2(NBLK - 1, 1)

        @block.scalar
        def _(act):
            def prepare(n, chunks):
                for k in chunks:
                    c = W_BEFORE[n] + k
                    hi, _ = w_dest(n, k)
                    act.wait_ge(w_turned, c + 1)
                    nc.scalar.activation(hi, pm[c % 4][:, :], ACT.Identity, scale=W_SCALE[n]).then_inc(w_hi, 1)

            def copy_x(i, k):
                tok = slice(k * P, (k + 1) * P)
                act.wait_ge(tx_done, i * TILES + (k + 1))
                if k == 0:
                    after(act, z_mm, i * NC)
                    after(act, gated, i * NC)
                src = pt[k % 2][:, :].rearrange("p (c q) -> p c q", c=NC)
                nc.scalar.activation(x_h[:, :, tok], src, ACT.Identity)
                nc.scalar.activation(x_t[:, :, tok], src, ACT.Identity).then_inc(xcopy, 1)

            def context_hi(i, c):
                if c == 0:
                    after(act, z_mm, i * NC)
                act.wait_ge(ctx_scan, i * NC + (c + 1))
                nc.scalar.activation(c_h[:, c, :], ctx_t[:, c % 2, :], ACT.Identity).then_inc(ctx_hi, 1)

            def hidden(i):
                act.wait_ge(h1_mm, i + 1)
                after(act, h1_lo, i)
                after(act, mod_out, i * 16)
                nc.scalar.activation(h1[:, :], pt[0][:, :], ACT.Gelu, bias=col_bn1[:, 0:1]).then_inc(h1_gelu, 1)
                act.wait_ge(h1_gelu, i + 1)
                after(act, mod_mm, i)
                nc.scalar.activation(h_h[:, :], h1[:, :], ACT.Identity).then_inc(h1_hi, 1)

            def gate_tanh(j, m):
                act.wait_ge(wt_mm, j * NC + (m + 1))
                after(act, s_lo, j * NC + (m - 1))
                nc.scalar.activation(gate[:, m % 2, :], pm[m][:, :], ACT.Tanh, bias=cols["btemp"][:, m:m + 1],
                                     scale=0.5).then_inc(gate_t, 1)

            def gated_soma_hi(j, m):
                after(act, wo_mm, j * TILES)
                act.wait_ge(s_prod, j * NC + (m + 1))
                nc.scalar.activation(s_h[:, m, :], gate[:, m % 2, :], ACT.Identity).then_inc(s_hi, 1)

            def gates(j):
                gate_tanh(j, 0)
                gate_tanh(j, 1)
                gated_soma_hi(j, 0)
                gate_tanh(j, 2)
                gated_soma_hi(j, 1)
                gate_tanh(j, 3)
                gated_soma_hi(j, 2)
                gated_soma_hi(j, 3)

            def soma_gelu(i, m):
                act.wait_ge(soma_mm, i * NC + (m + 1))
                after(act, s_prod, i * NC + (m - 3))
                nc.scalar.activation(soma[:, m, :], pc[m % 2][:, :], ACT.Gelu,
                                     bias=cols["bsoma"][:, m:m + 1]).then_inc(soma_g, 1)

            def mod_tanh(i):
                act.wait_ge(mod_mm, i + 1)
                nc.scalar.activation(h1[0:D, :], pt[0][0:D, :], ACT.Tanh, bias=col_bn2[0:D, 0:1],
                                     scale=0.5).then_inc(mod_t, 1)

            def z_tanh(i, m):
                act.wait_ge(z_mm, i * NC + (m + 1))
                after(act, temp_lo, i * NC + (m - 1))
                nc.scalar.activation(tr1[:, m % 2, :], pc[m % 2][:, :], ACT.Tanh, bias=cols["bg"][:, m:m + 1],
                                     scale=0.5).then_inc(z_t, 1)

            def weigh(i, m):
                act.wait_ge(traces, (i * NC + (m + 1)) * D)
                act.wait_ge(tr_carry, (i * NC + (m + 1)) * D)
                nc.scalar.activation(tr0[:, m % 2, :], tr0[:, m % 2, :], ACT.Identity,
                                     scale=w_blend[:, 0, m:m + 1]).then_inc(weighed, 1)

            def temporal_hi(i, m):
                after(act, wt_mm, i * NC)
                act.wait_ge(blended, i * NC + (m + 1))
                nc.scalar.activation(t_h[:, m, :], tr0[:, m % 2, :], ACT.Identity).then_inc(temp_hi, 1)

            def trace_part(i, first=False):
                z_tanh(i, 0)
                if first:
                    prepare(4, W4_AFTER[0])
                for m in range(NC - 1):
                    z_tanh(i, m + 1)
                    if first:
                        prepare(4, W4_AFTER[m + 1])
                    weigh(i, m)
                    temporal_hi(i, m)

            def trace_end(i):
                copy_x(i + 1, 0)
                weigh(i, 3)
                copy_x(i + 1, 1)
                temporal_hi(i, 3)
                copy_x(i + 1, 2)
                copy_x(i + 1, 3)

            def step(i, first=False):
                gates(i - 1)
                hidden(i)
                soma_gelu(i, 0)
                context_hi(i, 0)
                soma_gelu(i, 1)
                context_hi(i, 1)
                context_hi(i, 2)
                soma_gelu(i, 2)
                mod_tanh(i)
                context_hi(i, 3)
                soma_gelu(i, 3)
                if first:
                    prepare(5, range(NC))
                trace_part(i)
                trace_end(i)

            for k in range(TILES):
                copy_x(0, k)
            prepare(0, [0])
            prepare(1, range(NC))
            act.wait_ge(consts_v, 1)
            nc.scalar.activation(alpha[:, :], taus[:, :], ACT.Tanh, scale=-0.5).then_inc(consts_a, 1)
            nc.scalar.activation(w_blend[:, :, :], dblend[:, :, :], ACT.Tanh, scale=0.5).then_inc(consts_a, 1)
            hidden(0)
            soma_gelu(0, 0)
            prepare(2, [0, 1])
            context_hi(0, 0)
            context_hi(0, 1)
            soma_gelu(0, 1)
            prepare(2, [2, 3])
            context_hi(0, 2)
            context_hi(0, 3)
            soma_gelu(0, 2)
            prepare(3, [0, 1])
            soma_gelu(0, 3)
            prepare(3, [2, 3])
            mod_tanh(0)
            trace_part(0, first=True)
            trace_end(0)
            step(1, first=True)
            with act.Fori(2, NBLK) as i:
                step(i)

            def linear_hi(b):
                act.wait_ge(l1_eye, (b + 1) * NC)
                for k in range(NC):
                    nc.scalar.activation(l1_w(b)[0][:, k, :], l1_chunk(b, k), ACT.Identity).then_inc(l1_hi, 1)

            def adapter_hi(b):
                act.wait_ge(l2_in[b], 32)
                for raw, wh, _ in adapter_parts(b):
                    nc.scalar.activation(wh, raw, ACT.Identity).then_inc(l2_hi, 1)

            def subject_hi(b, k, bank):
                if k == 0:
                    act.wait_ge(wt_mm if b == 0 else wo_mm, NBLK * NC)
                act.wait_ge(l3_turned, b * NC + k + 1)
                nc.scalar.activation(l3_w(b)[0][:, k, :], bank[:, :], ACT.Identity).then_inc(l3_hi, 1)

            def copy_y(i, k):
                tok = slice(k * P, (k + 1) * P)
                act.wait_ge(ty_done, i * TILES + (k - 3))
                if k == 0:
                    after(act, l1_mm, i * NC)
                nc.scalar.activation(x_h[:, :, tok], pt[k % 2][:, :].rearrange("p (c q) -> p c q", c=NC),
                                     ACT.Identity).then_inc(y_hi, 1)

            def x2_parts(i, b, m):
                act.wait_ge(l1_mm, i * NC + (m + 1))
                after(act, w1_mm, i)
                nc.scalar.activation(c_h[:, m, :], pc[m % 2][:, :], ACT.Identity, bias=seq["b1"][:, b, m:m + 1])
                after(act, xx_mm, i * TILES)
                after(act, x2_all, i * NC + (m - 3))
                nc.scalar.activation(x_t[:, m, :], pc[m % 2][:, :], ACT.Identity,
                                     bias=seq["b1b2"][:, b, m:m + 1]).then_inc(x2_hi, 1)

            def x2_beta(i, b, m):
                after(act, x3_sum, i * NC + (m - 3))
                act.wait_ge(x2_hi, i * NC + (m + 1))
                nc.scalar.activation(soma[:, m, :], x_t[:, m, :], ACT.Identity,
                                     bias=seq["beta_b2"][:, b, m:m + 1]).then_inc(x2_all, 1)

            def x3_hi_part(j, m):
                after(act, l3_mm, j * TILES)
                act.wait_ge(x3_sum, j * NC + (m + 1))
                nc.scalar.activation(t_h[:, m, :], gate[:, m % 2, :], ACT.Identity).then_inc(x3_hi, 1)

            def relu_part(i, b):
                act.wait_ge(w1_mm, i + 1)
                after(act, hid_lo, i)
                nc.scalar.activation(h1[:, :], pc[0][:, :], ACT.Relu, bias=seq["lb1"][:, b, 0:1]).then_inc(relu_done, 1)
                act.wait_ge(relu_done, i + 1)
                after(act, xx_mm, i * TILES)
                nc.scalar.activation(h_h[:, :], h1[:, :], ACT.Identity).then_inc(hid_hi, 1)

            def normalise(i, k):
                act.wait_ge(ln2_rstd, i + 1)
                after(act, tn_done, i * NC)
                nc.scalar.activation(stage_a[:, k, :], pm[k][:, :], ACT.Identity, bias=nbias[:, k:k + 1],
                                     scale=rstd[:, k:k + 1]).then_inc(n2_act, 1)

            def step2(i, b, nxt, weights=False, adapter=False):
                x2_parts(i, b, 0)
                if adapter:
                    adapter_hi(1)
                x3_hi_part(i - 1, 0)
                x3_hi_part(i - 1, 1)
                x2_parts(i, b, 1)
                x3_hi_part(i - 1, 2)
                x3_hi_part(i - 1, 3)
                x2_parts(i, b, 2)
                x2_beta(i, b, 0)
                x2_parts(i, b, 3)
                if nxt:
                    copy_y(i + 1, 0)
                    copy_y(i + 1, 1)
                x2_beta(i, b, 1)
                relu_part(i, b)
                if nxt:
                    copy_y(i + 1, 2)
                x2_beta(i, b, 2)
                if nxt:
                    copy_y(i + 1, 3)
                x2_beta(i, b, 3)
                if weights:
                    for k in range(NC):
                        subject_hi(1, k, (pt if k % 2 == 0 else pc)[1])
                normalise(i, 0)
                normalise(i, 1)

            linear_hi(0)
            gates(NBLK - 1)
            act.wait_ge(bias_done, 1)
            x2_parts(0, 0, 0)
            x2_parts(0, 0, 1)
            subject_hi(0, 0, pt[0])
            subject_hi(0, 1, pt[1])
            adapter_hi(0)
            subject_hi(0, 2, pt[0])
            subject_hi(0, 3, pt[1])
            x2_parts(0, 0, 2)
            x2_parts(0, 0, 3)
            copy_y(1, 0)
            copy_y(1, 1)
            relu_part(0, 0)
            copy_y(1, 2)
            copy_y(1, 3)
            linear_hi(1)
            act.wait_ge(l2_lo, 2)
            for m in range(NC):
                x2_beta(0, 0, m)
            act.wait_ge(x1_out[0], 16 * 2 * NBLK)
            act.wait_ge(x1_out[1], 16 * 2 * NBLK)
            normalise(0, 0)
            normalise(0, 1)
            step2(1, 0, True, weights=True)
            with act.Fori(2, PER_SEQ) as i:
                step2(i, 0, True)
            step2(PER_SEQ, 1, True, adapter=True)
            with act.Fori(PER_SEQ + 1, NBLK - 1) as i:
                step2(i, 1, True)
            step2(NBLK - 1, 1, False)
            for m in range(NC):
                x3_hi_part(NBLK - 1, m)

        @block.vector
        def _(dve):
            def f32(ap):
                return ap.bitcast(F32)

            def prepare(n, chunks):
                for k in chunks:
                    c = W_BEFORE[n] + k
                    hi, lo = w_dest(n, k)
                    dve.wait_ge(w_hi, c + 1)
                    nc.vector.scalar_tensor_tensor(lo, pm[c % 4][:, :], W_SCALE[n], f32(hi), ALU.mult,
                                                   ALU.subtract).then_inc(w_lo, 1)

            def x_lo_part(i, k):
                tok = slice(k * P, (k + 1) * P)
                dve.wait_ge(xcopy, i * TILES + k + 1)
                after(dve, z_mm, i * NC)
                nc.vector.tensor_tensor(x_l[:, :, tok], x_t[:, :, tok], f32(x_h[:, :, tok]),
                                        ALU.subtract).then_inc(xlo, 1)

            def scan_context(i, c):
                after(dve, ctx_hi, i * NC + (c - 1))
                after(dve, ctx_lo, i * NC + (c - 1))
                after(dve, ctx_carry, i * NC + (c - 3))
                nc.vector.tensor_tensor_scan(ctx_t[:, c % 2, :], alpha[:, 0:1].to_broadcast([P, BLK]), x_t[:, c, :],
                                             carry[:, 0, c:c + 1], ALU.mult, ALU.add).then_inc(ctx_scan, 1)

            def carry_context(i, c):
                dve.wait_ge(ctx_scan, i * NC + (c + 1))
                nc.vector.tensor_scalar(carry[:, 0, c:c + 1], ctx_t[:, c % 2, BLK - 1:BLK],
                                        keep[:, bass.ds(i + 1, 1)], None, ALU.mult).then_inc(ctx_carry, 1)

            def split_context(i, c):
                dve.wait_ge(ctx_hi, i * NC + (c + 1))
                nc.vector.tensor_tensor(c_l[:, c, :], ctx_t[:, c % 2, :], f32(c_h[:, c, :]),
                                        ALU.subtract).then_inc(ctx_lo, 1)

            def context(i, hidden=True):
                dve.wait_ge(xcopy, i * TILES + TILES)
                after(dve, z_mm, i * NC)
                scan_context(i, 0)
                scan_context(i, 1)
                if hidden:
                    hidden_lo(i)
                carry_context(i, 0)
                split_context(i, 0)
                scan_context(i, 2)
                carry_context(i, 1)
                split_context(i, 1)
                scan_context(i, 3)
                carry_context(i, 2)
                split_context(i, 2)
                carry_context(i, 3)
                split_context(i, 3)

            def hidden_lo(i):
                dve.wait_ge(h1_hi, i + 1)
                after(dve, mod_mm, i)
                nc.vector.tensor_tensor(h_l[:, :], h1[:, :], f32(h_h[:, :]), ALU.subtract).then_inc(h1_lo, 1)

            def gate_soma(j, m):
                dve.wait_ge(gate_t, j * NC + (m + 1))
                dve.wait_ge(soma_g, j * NC + (m + 1))
                nc.vector.scalar_tensor_tensor(gate[:, m % 2, :], gate[:, m % 2, :], 1.0, soma[:, m, :],
                                               ALU.add, ALU.mult).then_inc(s_prod, 1)

            def gated_soma_lo(j, m):
                after(dve, wo_mm, j * TILES)
                dve.wait_ge(s_hi, j * NC + (m + 1))
                nc.vector.tensor_tensor(s_l[:, m, :], gate[:, m % 2, :], f32(s_h[:, m, :]),
                                        ALU.subtract).then_inc(s_lo, 1)

            def gates(j):
                gate_soma(j, 0)
                gate_soma(j, 1)
                gated_soma_lo(j, 0)
                gate_soma(j, 2)
                gated_soma_lo(j, 1)
                gate_soma(j, 3)
                gated_soma_lo(j, 2)
                gated_soma_lo(j, 3)

            def gate_x(i, m):
                dve.wait_ge(z_t, i * NC + (m + 1))
                nc.vector.scalar_tensor_tensor(tr1[:, m % 2, :], tr1[:, m % 2, :], 1.0, x_t[:, m, :],
                                               ALU.add, ALU.mult).then_inc(gated, 1)

            def modulate(i, m):
                dve.wait_ge(gated, i * NC + (m + 1))
                dve.wait_ge(mod_in, i * 16 + 16)
                nc.vector.scalar_tensor_tensor(tr0[:, m % 2, :], mod[:, 0, :], 2.0, tr1[:, m % 2, :],
                                               ALU.add, ALU.mult).then_inc(prods, 1)
                nc.vector.scalar_tensor_tensor(tr1[:, m % 2, :], mod[:, 1, :], 2.0, tr1[:, m % 2, :],
                                               ALU.add, ALU.mult).then_inc(prods, 1)

            def scan_traces(i, m):
                after(dve, tr_carry, (i * NC + (m - 3)) * D)
                for d, tr in enumerate((tr0, tr1)):
                    dve.wait_ge(prods, i * (D * NC) + (m * D + d + 1))
                    nc.vector.tensor_tensor_scan(tr[:, m % 2, :], alpha[:, 1 + d:2 + d].to_broadcast([P, BLK]),
                                                 tr[:, m % 2, :], carry[:, 1 + d, m:m + 1], ALU.mult,
                                                 ALU.add).then_inc(traces, 1)
                for d, tr in enumerate((tr0, tr1)):
                    dve.wait_ge(traces, i * (D * NC) + (m * D + d + 1))
                    nc.vector.tensor_scalar(carry[:, 1 + d, m:m + 1], tr[:, m % 2, BLK - 1:BLK],
                                            keep[:, bass.ds(i + 1, 1)], None, ALU.mult).then_inc(tr_carry, 1)

            def blend_traces(i, m):
                dve.wait_ge(weighed, i * NC + (m + 1))
                nc.vector.scalar_tensor_tensor(tr0[:, m % 2, :], tr1[:, m % 2, :], w_blend[:, 1, m:m + 1],
                                               tr0[:, m % 2, :], ALU.mult, ALU.add).then_inc(blended, 1)

            def temporal_lo(i, m):
                after(dve, wt_mm, i * NC)
                dve.wait_ge(temp_hi, i * NC + (m + 1))
                nc.vector.tensor_tensor(t_l[:, m, :], tr0[:, m % 2, :], f32(t_h[:, m, :]),
                                        ALU.subtract).then_inc(temp_lo, 1)

            def trace_part(i, first=False):
                gate_x(i, 0)
                modulate(i, 0)
                scan_traces(i, 0)
                if first:
                    prepare(4, W4_AFTER[0])
                gate_x(i, 1)
                blend_traces(i, 0)
                modulate(i, 1)
                temporal_lo(i, 0)
                scan_traces(i, 1)
                if first:
                    prepare(4, W4_AFTER[1])
                gate_x(i, 2)
                blend_traces(i, 1)
                modulate(i, 2)
                temporal_lo(i, 1)
                scan_traces(i, 2)
                gate_x(i, 3)
                if first:
                    prepare(4, W4_AFTER[2])
                blend_traces(i, 2)
                modulate(i, 3)
                temporal_lo(i, 2)
                scan_traces(i, 3)

            def norm_stats(j, k):
                dve.wait_ge(wo_mm, j * TILES + (k + 1))
                after(dve, ln_mv, j * TILES + (k - 3))
                nc.vector.bn_stats(stats[:, k, :], pm[k][:, :]).then_inc(ln_stats, 1)
                dve.wait_ge(ln_stats, j * TILES + (k + 1))
                dve.sem_inc(stats_seen, 1)
                nc.vector.bn_aggr(mv[:, k, :], stats[:, k, :]).then_inc(ln_mv, 1)
                dve.wait_ge(ln_mv, j * TILES + (k + 1))
                after(dve, x1_ready, j * TILES + (k - 1))
                nc.vector.scalar_tensor_tensor(normed[:, k % 2, :], pm[k][:, :], mv[:, k, 0:1], gamma_row[:, :],
                                               ALU.subtract, ALU.mult).then_inc(ln_centred, 1)

            def norm_sum(j, k):
                dve.wait_ge(ln_centred, j * TILES + (k + 1))
                dve.wait_ge(ln_rstd, j * TILES + (k + 1))
                dve.wait_ge(beta_in, j * TILES + (k + 1))
                nc.vector.scalar_tensor_tensor(x_again[:, k % 2, :], normed[:, k % 2, :], rstd[:, k:k + 1],
                                               x_again[:, k % 2, :], ALU.mult, ALU.add).then_inc(x1_ready, 1)

            def tail(i):
                j = i - 1
                norm_stats(j, 0)
                blend_traces(i, 3)
                norm_stats(j, 1)
                temporal_lo(i, 3)
                norm_sum(j, 0)
                norm_stats(j, 2)
                norm_sum(j, 1)
                norm_stats(j, 3)

            def norm_end(j):
                norm_sum(j, 2)
                norm_sum(j, 3)

            def step(i, first=False):
                gates(i - 1)
                if not first:
                    norm_end(i - 2)
                context(i)
                if first:
                    prepare(5, range(NC))
                trace_part(i)
                tail(i)

            nc.vector.memset(keep[:, :], 1.0).then_inc(setup_v, 1)
            nc.vector.memset(carry[:, :, :], 0.0).then_inc(setup_v, 1)
            dve.wait_ge(setup_v, 2)
            for b in range(B + 1):
                nc.vector.memset(keep[:, b * PER_SEQ:b * PER_SEQ + 1], 0.0).then_inc(setup_v, 1)
            for k in range(TILES):
                x_lo_part(0, k)
            prepare(0, [0])
            prepare(1, range(NC))
            dve.wait_ge(small_in, 16 * 6)
            dve.wait_ge(wide_in, 16 * 6)
            for d in range(D):
                nc.vector.tensor_tensor(dblend[:, d, :], blend[:, d, :], blend[:, 1 - d, :],
                                        ALU.subtract).then_inc(setup_v, 1)
            nc.vector.tensor_scalar(cols["bg"][:, :], cols["bg"][:, :], 0.5, None, ALU.mult).then_inc(setup_v, 1)
            nc.vector.tensor_scalar(cols["btemp"][:, :], cols["btemp"][:, :], 0.5, None, ALU.mult).then_inc(setup_v, 1)
            nc.vector.tensor_scalar(col_bn2[0:D, :], col_bn2[0:D, :], 0.5, None, ALU.mult).then_inc(consts_v, 1)
            dve.wait_ge(consts_a, 2)
            nc.vector.tensor_scalar(alpha[:, :], alpha[:, :], 0.5, 0.5, ALU.mult, ALU.add).then_inc(setup_v, 1)
            nc.vector.tensor_scalar(w_blend[:, :, :], w_blend[:, :, :], 0.125, 0.125, ALU.mult,
                                    ALU.add).then_inc(setup_v, 1)
            dve.wait_ge(setup_v, 7 + B + D)
            nc.vector.tensor_scalar(wn2_h[:, :], col_wn2[:, :], 1.0, None, ALU.mult).then_inc(setup_v, 1)
            dve.wait_ge(setup_v, 8 + B + D)
            nc.vector.tensor_tensor(wn2_l[:, :], col_wn2[:, :], f32(wn2_h[:, :]), ALU.subtract).then_inc(consts_v, 1)
            hidden_lo(0)
            prepare(2, [0, 1])
            context(0, hidden=False)
            prepare(2, [2, 3])
            prepare(3, range(NC))
            trace_part(0, first=True)
            blend_traces(0, 3)
            temporal_lo(0, 3)
            step(1, first=True)
            with dve.Fori(2, NBLK) as i:
                step(i)

            def biases():
                dve.wait_ge(lw_in, 16 * 5 * B)
                nc.vector.tensor_tensor(seq["b1b2"][:, :, :], seq["b1"][:, :, :], seq["b2"][:, :, :], ALU.add)
                nc.vector.tensor_tensor(seq["beta_b2"][:, :, :], seq["beta2"][:, :, :], seq["b2"][:, :, :],
                                        ALU.subtract).then_inc(bias_done, 1)

            def subject_lo(b, k, bank):
                dve.wait_ge(l3_hi, b * NC + k + 1)
                wh, wl = l3_w(b)
                nc.vector.tensor_tensor(wl[:, k, :], bank[:, :], f32(wh[:, k, :]),
                                        ALU.subtract).then_inc(l3_lo, 1)

            def y_lo_part(i, k):
                tok = slice(k * P, (k + 1) * P)
                dve.wait_ge(y_hi, i * TILES + (k - 3))
                nc.vector.tensor_tensor(x_l[:, :, tok], pt[k % 2][:, :].rearrange("p (c q) -> p c q", c=NC),
                                        f32(x_h[:, :, tok]), ALU.subtract).then_inc(y_lo, 1)

            def x2_lo_part(i, b, m):
                after(dve, w1_mm, i)
                dve.wait_ge(x2_hi, i * NC + (m + 1))
                nc.vector.scalar_tensor_tensor(c_l[:, m, :], pc[m % 2][:, :], seq["b1"][:, b, m:m + 1],
                                               f32(c_h[:, m, :]), ALU.add, ALU.subtract).then_inc(x2_lo, 1)

            def x3_sum_part(j, b, m):
                dve.wait_ge(tn_done, j * NC + (m + 1))
                dve.wait_ge(x2_all, j * NC + (m + 1))
                if m >= 2:
                    dve.wait_ge(x3_hi, j * NC + (m - 1))
                    dve.wait_ge(x3_lo, j * NC + (m - 1))
                nc.vector.scalar_tensor_tensor(gate[:, m % 2, :], n2_bank(j, m)[:, :], seq["gamma2"][:, b, m:m + 1],
                                               soma[:, m, :], ALU.mult, ALU.add).then_inc(x3_sum, 1)

            def x3_lo_part(j, m):
                after(dve, l3_mm, j * TILES)
                dve.wait_ge(x3_hi, j * NC + (m + 1))
                nc.vector.tensor_tensor(t_l[:, m, :], gate[:, m % 2, :], f32(t_h[:, m, :]),
                                        ALU.subtract).then_inc(x3_lo, 1)

            def hid_lo_part(i):
                dve.wait_ge(hid_hi, i + 1)
                nc.vector.tensor_tensor(h_l[:, :], h1[:, :], f32(h_h[:, :]), ALU.subtract).then_inc(hid_lo, 1)

            def output(j, b, k):
                dve.wait_ge(l3_mm, j * TILES + (k + 1))
                if not last_block(j):
                    after(dve, out_done[k % 2], (j * 2 + k // 2) * 16)
                bank = l3_bank(j, k)
                nc.vector.tensor_tensor(out_tile(j, k), bank[:, :], mod[:, b, :], ALU.add).then_inc(out_ready, 1)

            def norm2_stats(i, k):
                dve.wait_ge(xx_mm, i * TILES + (k + 1))
                nc.vector.bn_stats(stats[:, k, :], pm[k][:, :]).then_inc(ln2_stats, 1)
                dve.wait_ge(ln2_stats, i * TILES + (k + 1))
                dve.sem_inc(stats_seen, 1)
                nc.vector.bn_aggr(mv[:, k, :], stats[:, k, :]).then_inc(ln2_mv, 1)

            def normalise(i, k):
                dve.wait_ge(ln2_rstd, i + 1)
                after(dve, tn_done, i * NC)
                nc.vector.tensor_scalar(stage_a[:, k, :], pm[k][:, :], rstd[:, k:k + 1], nbias[:, k:k + 1],
                                        ALU.mult, ALU.add).then_inc(n2_dve, 1)

            def step2(i, b, bp, weights=False):
                last = last_block(i)
                x2_lo_part(i, b, 0)
                x3_sum_part(i - 1, bp, 0)
                x3_sum_part(i - 1, bp, 1)
                x3_lo_part(i - 1, 0)
                x3_lo_part(i - 1, 1)
                x2_lo_part(i, b, 1)
                x3_sum_part(i - 1, bp, 2)
                x3_sum_part(i - 1, bp, 3)
                x3_lo_part(i - 1, 2)
                x3_lo_part(i - 1, 3)
                x2_lo_part(i, b, 2)
                x2_lo_part(i, b, 3)
                if not last:
                    y_lo_part(i + 1, 0)
                    y_lo_part(i + 1, 1)
                output(i - 1, bp, 0)
                hid_lo_part(i)
                if not last:
                    y_lo_part(i + 1, 2)
                output(i - 1, bp, 1)
                if not last:
                    y_lo_part(i + 1, 3)
                    output(i - 1, bp, 2)
                if weights:
                    subject_lo(1, 0, pt[1])
                    subject_lo(1, 1, pc[1])
                for k in range(TILES):
                    norm2_stats(i, k)
                if weights:
                    subject_lo(1, 2, pt[1])
                    subject_lo(1, 3, pc[1])
                if last:
                    output(i - 1, bp, 2)
                else:
                    output(i - 1, bp, 3)
                normalise(i, 2)
                normalise(i, 3)
                if last:
                    output(i - 1, bp, 3)

            for k in range(TILES):
                x_lo_part(NBLK, k)
            biases()
            gates(NBLK - 1)
            norm_end(NBLK - 2)
            x2_lo_part(0, 0, 0)
            x2_lo_part(0, 0, 1)
            subject_lo(0, 0, pt[0])
            subject_lo(0, 1, pt[1])
            for n, (raw, wh, wl) in enumerate(adapter_parts(0)):
                dve.wait_ge(l2_hi, n + 1)
                nc.vector.tensor_tensor(wl, raw, f32(wh), ALU.subtract).then_inc(l2_lo, 1)
            norm_stats(NBLK - 1, 0)
            norm_stats(NBLK - 1, 1)
            norm_sum(NBLK - 1, 0)
            subject_lo(0, 2, pt[0])
            subject_lo(0, 3, pt[1])
            norm_stats(NBLK - 1, 2)
            norm_sum(NBLK - 1, 1)
            norm_stats(NBLK - 1, 3)
            x2_lo_part(0, 0, 2)
            x2_lo_part(0, 0, 3)
            y_lo_part(1, 0)
            y_lo_part(1, 1)
            hid_lo_part(0)
            norm_sum(NBLK - 1, 2)
            y_lo_part(1, 2)
            y_lo_part(1, 3)
            norm_sum(NBLK - 1, 3)
            for k in range(TILES):
                norm2_stats(0, k)
            for s in range(2):
                dve.wait_ge(x1_out[s], 16 * 2 * NBLK)
            normalise(0, 2)
            normalise(0, 3)
            dve.wait_ge(b3_in, 16 * B)
            step2(1, 0, 0, weights=True)
            with dve.Fori(2, PER_SEQ) as i:
                step2(i, 0, 0)
            step2(PER_SEQ, 1, 0)
            with dve.Fori(PER_SEQ + 1, NBLK - 1) as i:
                step2(i, 1, 1)
            step2(NBLK - 1, 1, 1)
            x3_sum_part(NBLK - 1, 1, 0)
            x3_sum_part(NBLK - 1, 1, 1)
            x3_lo_part(NBLK - 1, 0)
            x3_sum_part(NBLK - 1, 1, 2)
            x3_lo_part(NBLK - 1, 1)
            x3_sum_part(NBLK - 1, 1, 3)
            x3_lo_part(NBLK - 1, 2)
            x3_lo_part(NBLK - 1, 3)
            for k in range(TILES):
                output(NBLK - 1, 1, k)


_INS = ['x', 'condB_tauraws', 'cond_256', 'condB_bn2', 'cond_1024', 'itok_B_0_30', 'itok_B_0_8', 'itok_B_0_7',
        'L0_cond_tau_ctx', 'L0_cond_Wg', 'L0_cond_bg', 'L0_cond_Wn1', 'L0_cond_bn1', 'L0_cond_Wsoma',
        'L0_cond_bsoma', 'L0_cond_Wtemp', 'L0_cond_btemp', 'L0_cond_Wout', 'L0_cond_gamma', 'L0_cond_beta',
        'L1_cond_W', 'L1_cond_b', 'L2_cond_W1', 'L2_cond_b1', 'L2_cond_W2', 'L2_cond_b2', 'L2_cond_gamma',
        'L2_cond_beta', 'L3_cond_weight', 'L3_cond_bias']


def kernel(**inputs):
    import numpy as _np
    import concourse.bacc as _bacc
    from concourse import mybir as _mybir
    from concourse.bass_utils import run_bass_kernel_spmd as _run

    nc = _bacc.Bacc("TRN2", target_bir_lowering=False, num_devices=1)
    arrays, args = {}, {}
    for name in _INS:
        a = _np.ascontiguousarray(inputs[name])
        if a.ndim == 0:
            a = a.reshape(1)
        arrays[f"in_{name}_dram"] = a
        args[name] = nc.dram_tensor(f"in_{name}_dram", a.shape, _mybir.dt.from_np(a.dtype), kind="ExternalInput").ap()
    x = arrays["in_x_dram"]
    out = nc.dram_tensor("out_0_dram", x.shape, _mybir.dt.from_np(x.dtype), kind="ExternalOutput").ap()
    residual_chain_kernel(nc, args, out)
    r = _run(nc, [arrays], core_ids=[0])
    return r.results[0]["out_0_dram"]
```
